# Optimizing a Trainium2 kernel written in Bass

```python
import numpy as np
import jax
import jax.numpy as jnp

def _softmax(x, axis=-1):
    return jax.nn.softmax(x, axis=axis)

def _gelu(x):
    return jax.nn.gelu(x, approximate=True)

def _silu(x):
    return jax.nn.silu(x)

def _sigmoid(x):
    return jax.nn.sigmoid(x)

def _layernorm(x, axis=-1, eps=1e-05):
    m = jnp.mean(x, axis=axis, keepdims=True)
    v = jnp.var(x, axis=axis, keepdims=True)
    return (x - m) / jnp.sqrt(v + eps)

def _scatter_add(tgt, idx, src, axis=0):
    return tgt.at[idx].add(src)

def _segment_sum(src, seg, n):
    return jax.ops.segment_sum(src, seg, n)
kernel_name = 'mk_gnn_preln_d2_gnn_r32_abafca'

def setup_inputs(seed: int=0):
    np.random.seed(seed)
    _w = jnp.asarray

    def _rec_inputs():
        import jax
        import jax.numpy as jnp
        _gk = jax.random.key(seed)
        x = -0.0005121 + 1.001 * jax.random.normal(jax.random.fold_in(_gk, 1), (50000, 64), jnp.float32)
        src = jax.random.randint(jax.random.fold_in(_gk, 2), (50000,), 0, 50000, jnp.int32)
        dst = jnp.minimum((50000 * jax.random.uniform(jax.random.fold_in(_gk, 3), (50000,)) ** 2.0).astype(jnp.int32), 49999)
        _o = jnp.argsort(dst, stable=True)
        src = src[_o]
        dst = dst[_o]
        edge_attr_64 = 5.93493e-05 + 1.00006 * jax.random.normal(jax.random.fold_in(_gk, 11), (50000, 64), jnp.float32)
        edge_weight = 6.14103e-05 + 0.0999867 * jax.random.normal(jax.random.fold_in(_gk, 13), (50000,), jnp.float32)
        return (x, src, dst, edge_attr_64, edge_weight)
    x, src, dst, edge_attr_64, edge_weight = _rec_inputs()

    def _L0_gnn_setup():
        import jax, jax.numpy as jnp
        import numpy as np
        N_NODES = 50000
        N_EDGES = 25000
        IN_F = 64
        OUT_F = 64
        K = 6

        def _spmv(edge_index, lap_vals, h):
            src, dst = (edge_index[0], edge_index[1])
            msgs = lap_vals[:, None] * h[src]
            return jax.ops.segment_sum(msgs, dst, num_segments=N_NODES)
        key = jax.random.key(seed)
        k1, k2, k3, k4, k5 = jax.random.split(key, 5)
        x = jax.random.normal(k1, (N_NODES, IN_F), dtype=jnp.float32)
        edge_index = jax.random.randint(k2, (2, N_EDGES), 0, N_NODES, dtype=jnp.int64)
        laplacian = jax.random.normal(k3, (N_EDGES,), dtype=jnp.float32) * 0.1
        W = jax.random.normal(k4, (K, IN_F, OUT_F), dtype=jnp.float32) / np.sqrt(IN_F)
        bias = jax.random.normal(k5, (OUT_F,), dtype=jnp.float32) * 0.01
        return {'x': x, 'edge_index': edge_index, 'laplacian': laplacian, 'W': W, 'bias': bias}
    _L0_gnn_all = _L0_gnn_setup()
    _L0_gnn_in = {k: v for k, v in _L0_gnn_all.items() if k in ('W', 'bias')}
    del _L0_gnn_all

    def _L1_gnn_setup():
        import jax, jax.numpy as jnp
        import numpy as np
        N = 3125
        E = 37500
        D = 64

        def leaky_relu(x, slope=0.2):
            return jnp.where(x >= 0, x, slope * x)
        key = jax.random.key(seed)
        ks = jax.random.split(key, 10)
        indices = jax.random.randint(ks[0], (2, E), 0, N, dtype=jnp.int64)
        features = jax.random.normal(ks[1], (N, D), dtype=jnp.float32)
        e_r = jax.random.normal(ks[2], (E, D), dtype=jnp.float32)
        s = 1.0 / np.sqrt(D)
        W1_w = jax.random.normal(ks[3], (D, D), dtype=jnp.float32) * s
        W1_b = jax.random.normal(ks[4], (D,), dtype=jnp.float32) * s
        W2_w = jax.random.normal(ks[5], (D, D), dtype=jnp.float32) * s
        W2_b = jax.random.normal(ks[6], (D,), dtype=jnp.float32) * s
        Watt_w = jax.random.normal(ks[7], (D, D), dtype=jnp.float32) * s
        Watt_b = jax.random.normal(ks[8], (D,), dtype=jnp.float32) * s
        return {'indices': indices, 'features': features, 'e_r': e_r, 'num_nodes': N, 'W1_w': W1_w, 'W1_b': W1_b, 'W2_w': W2_w, 'W2_b': W2_b, 'Watt_w': Watt_w, 'Watt_b': Watt_b}
    _L1_gnn_all = _L1_gnn_setup()
    _L1_gnn_in = {k: v for k, v in _L1_gnn_all.items() if k in ('W1_w', 'W1_b', 'W2_w', 'W2_b', 'Watt_w', 'Watt_b')}
    del _L1_gnn_all
    return {'x': x, 'src': src, 'dst': dst, 'edge_attr_64': edge_attr_64, 'edge_weight': edge_weight, 'L0_gnn_W': _L0_gnn_in['W'], 'L0_gnn_bias': _L0_gnn_in['bias'], 'L1_gnn_W1_w': _L1_gnn_in['W1_w'], 'L1_gnn_W1_b': _L1_gnn_in['W1_b'], 'L1_gnn_W2_w': _L1_gnn_in['W2_w'], 'L1_gnn_W2_b': _L1_gnn_in['W2_b'], 'L1_gnn_Watt_w': _L1_gnn_in['Watt_w'], 'L1_gnn_Watt_b': _L1_gnn_in['Watt_b']}

def reference(x, src, dst, edge_attr_64, edge_weight, L0_gnn_W, L0_gnn_bias, L1_gnn_W1_w, L1_gnn_W1_b, L1_gnn_W2_w, L1_gnn_W2_b, L1_gnn_Watt_w, L1_gnn_Watt_b):
    import jax
    import jax.numpy as jnp

    def _L0_gnn_ref(x, edge_index, laplacian, W, bias):
        import jax, jax.numpy as jnp
        import numpy as np
        N_NODES = 50000
        N_EDGES = 25000
        IN_F = 64
        OUT_F = 64
        K = 6

        def _spmv(edge_index, lap_vals, h):
            src, dst = (edge_index[0], edge_index[1])
            msgs = lap_vals[:, None] * h[src]
            return jax.ops.segment_sum(msgs, dst, num_segments=N_NODES)
        Tx0 = x
        out = Tx0 @ W[0]
        Tx1 = _spmv(edge_index, laplacian, Tx0)
        out = out + Tx1 @ W[1]
        for k in range(2, K):
            Tx2 = 2.0 * _spmv(edge_index, laplacian, Tx1) - Tx0
            out = out + Tx2 @ W[k]
            Tx0, Tx1 = (Tx1, Tx2)
        return jax.nn.relu(out + bias)

    def _L1_gnn_ref(indices, features, e_r, num_nodes, W1_w, W1_b, W2_w, W2_b, Watt_w, Watt_b):
        import jax, jax.numpy as jnp
        import numpy as np
        N = 3125
        E = 37500
        D = 64

        def leaky_relu(x, slope=0.2):
            return jnp.where(x >= 0, x, slope * x)
        src, dst = (indices[0], indices[1])
        out_dim = Watt_w.shape[0]
        h_trans = features @ Watt_w.T + Watt_b
        h_src = h_trans[src]
        h_dst = h_trans[dst]
        e_raw = jnp.sum(h_dst * jnp.tanh(h_src + e_r), axis=-1, keepdims=True)
        scaling = 1.0 / out_dim ** 0.5
        e_ij = leaky_relu(e_raw * scaling).astype(jnp.float32)
        max_score = jax.ops.segment_max(jax.lax.stop_gradient(e_ij), dst, num_segments=num_nodes)
        exp_e = jnp.exp(e_ij - max_score[dst])
        denom = jax.ops.segment_sum(exp_e, dst, num_segments=num_nodes)
        alpha = exp_e / (denom[dst] + 1e-09)
        weighted_msg = features[src] * alpha.astype(features.dtype)
        h_neigh = jax.ops.segment_sum(weighted_msg, dst, num_segments=num_nodes)
        sum_h = features + h_neigh
        prod_h = features * h_neigh
        h_out = leaky_relu(sum_h @ W1_w.T + W1_b + (prod_h @ W2_w.T + W2_b))
        return h_out
    edge_index = jnp.stack([src, dst])
    h = jnp.maximum(_layernorm(x, axis=-1), 0.0)
    x = x + _L0_gnn_ref(h, edge_index, edge_weight, L0_gnn_W, L0_gnn_bias)
    h = jnp.maximum(_layernorm(x, axis=-1), 0.0)
    x = x + _L1_gnn_ref(edge_index, h, edge_attr_64, 50000, L1_gnn_W1_w, L1_gnn_W1_b, L1_gnn_W2_w, L1_gnn_W2_b, L1_gnn_Watt_w, L1_gnn_Watt_b)
    return x

_drawn_inputs = setup_inputs


def setup_inputs(seed=0):
    import zlib

    import numpy as np

    out = dict(_drawn_inputs(seed))
    spreads = {}
    factors = {'L0_gnn_bias': 8.0, 'L1_gnn_Watt_b': 8.0}
    for name, (base, spread) in spreads.items():
        noise = np.random.default_rng([zlib.crc32(name.encode()), seed]).standard_normal(out[name].shape)
        drawn = base * np.exp(spread * noise) if base else spread * noise
        out[name] = jnp.asarray(drawn.astype(out[name].dtype))
    for name, factor in factors.items():
        out[name] = (out[name] * factor).astype(out[name].dtype)
    return out
```

```python
from contextlib import ExitStack

import concourse.bass as bass
from concourse import mybir
from concourse.alu_op_type import AluOpType as ALU

ACT = mybir.ActivationFunctionType
AX = mybir.AxisListType
F32 = mybir.dt.float32
F16 = mybir.dt.float16
I32 = mybir.dt.int32

P = 128
D = 64
N_NODES = 50000
NT = 392
ROWS = P * NT
T = 14
NC = NT // T
PAIR = 2 * D
PAIRS = T // 2
CW = T * D
FIX = ROWS
EMPTY = ROWS + P
TROWS = ROWS + 2 * P
ROW = 3 * D + 1
RX, RZ, RH, RREP = 0, D, 2 * D, 3 * D
EPS = 1e-5
ROUND = 1.5 * 2.0 ** 23
BIG = 1e30
ORDER = 5
HR = 4
KB = 512
STOP = None
F_DIAG, F_MAX, F_WTS, N_FIN = 1, 13, 14, 20
N_IOTA, N_CUM, N_REP, N_DIAG1, N_DIAG2, N_PREP = 1, 8, 29, 38, 39, 64
CHAIN = 2 * T - 1


def steps(eng, lo, hi, step):
    with eng.Fori(0, (hi - lo) // 2) as i:
        for j in range(2):
            step(2 * i + (lo + j), (lo + j) % 2, i + (lo + j) // 2)


def one(c, step):
    step(c, c % 2, c // 2)


def build(nc, x, src, dst, dst_next, edge_w, edge_attr, W, b0, W1, b1, W2, b2, Wa, ba, out, stop=None):
    with ExitStack() as ctx:
        def sb(name, shape, dt=F32):
            return ctx.enter_context(nc.sbuf_tensor(name, shape, dt))

        def ps(name, shape, dt=F32):
            return ctx.enter_context(nc.psum_tensor(name, shape, dt))

        def sem(name):
            return ctx.enter_context(nc.semaphore(name))

        def dram(name, shape, dt=F32):
            return nc.dram_tensor(name, shape, dt, kind="Internal").ap()

        node_rows = dram("node_rows", (ROWS, ROW))
        tables = [dram(f"segsum{k}", (TROWS, D)) for k in range(1, ORDER)]
        yn_table = dram("yn_table", (TROWS, 2 * D))
        y_table = dram("y_table", (TROWS, D))
        src_xz = dram("src_xz", (ROWS, 2 * D))
        htd_table = dram("htd_table", (ROWS, D))

        def by_part(t):
            return t[0:ROWS, :].rearrange("(p t) d -> p t d", t=NT)

        x_pt, er_pt, out_pt = by_part(x), by_part(edge_attr), by_part(out)
        node_pt, xz_pt, htd_pt, yn_pt = by_part(node_rows), by_part(src_xz), by_part(htd_table), by_part(yn_table)
        y_pt = by_part(y_table)
        tab_pt = [by_part(t) for t in tables]

        src_i = sb("src_i", [P, NT], I32)
        dst_i = sb("dst_i", [P, NT], I32)
        dstf = sb("dstf", [P, NT])
        w1 = sb("w1", [P, NT])
        w2 = sb("w2", [P, NT])
        same = sb("same", [P, NT])
        first = sb("first", [P, NT])
        last = sb("last", [P, NT])
        notlast = sb("notlast", [P, NT])
        last_first = sb("last_first", [P, NT])
        tmp = sb("tmp", [P, NT])
        hi = sb("hi", [P, NT])
        lo = sb("lo", [P, NT])
        incl = sb("incl", [P, NT])
        rep_i = sb("rep_i", [P, NT], I32)
        reps_i = sb("reps_i", [P, NT], I32)
        ident = sb("ident", [P, P])
        ones = sb("ones", [P, P])
        below = sb("below", [P, P])
        above = sb("above", [P, P])
        center = sb("center", [P, P])
        pidx_i = sb("pidx_i", [P, 1], I32)
        pidx = sb("pidx", [P, 1])
        zrow = sb("zrow", [P, PAIR])
        wmix = sb("wmix", [P, 6, PAIR])
        watt = sb("watt", [P, PAIR])
        w12 = sb("w12", [P, D])
        brow = sb("brow", [1, 4, D])
        bias = sb("bias", [1, 3, 8, D])
        eps_c = sb("eps_c", [P, 1])
        diag = sb("diag", [P, P])
        carry_in = sb("carry_in", [P, P])
        carry_to = sb("carry_to", [P, P])
        v_from = sb("v_from", [P, P])
        ends_in = sb("ends_in", [P, 1])
        small = sb("small", [P, 8])
        idx = sb("idx", [P, 2, T], I32)
        gat = sb("gat", [P, 2, T, ROW])
        xbuf = sb("xbuf", [P, 2, CW])
        hbuf = sb("hbuf", [P, 2, CW])
        xT = sb("xT", [P, CW])
        hT = sb("hT", [P, CW])
        sq = sb("sq", [P, 2, CW])
        run = sb("run", [P, 2, CW])
        sout = sb("sout", [P, 2, CW])
        stat = sb("stat", [P, 2, 4, T])
        fseg = sb("fseg", [P, D])
        fixp = sb("fixp", [P, ORDER + 1, PAIR])
        fixT = sb("fixT", [P, P])
        yfix = sb("yfix", [P, PAIR])
        yall = sb("yall", [P, NT * D])

        early = [NT * D]

        def early_room(n):
            early[0] -= n
            return yall[:, early[0]:early[0] + n]

        iota_i = early_room(NT).bitcast(I32)
        iota_h = early_room(NT // 2).bitcast(F16)
        zeros_h = early_room(P // 2).bitcast(F16)
        onehot = early_room(HR * (P + NT) // 2).bitcast(F16).rearrange("p (r c) -> p r c", r=HR)
        wraw = early_room(6 * PAIR).rearrange("p (k d) -> p k d", k=6)
        wa_raw = early_room(PAIR)
        w12_raw = early_room(2 * D)[0:D, :]
        vinit = sb("vinit", [P, D])
        cfill = sb("cfill", [P, D])
        spare = [0]

        def room(n):
            spare[0] += n
            return yall[:, spare[0] - n:spare[0]]

        xzb = room(2 * T * PAIR).rearrange("p (b t d) -> p b t d", b=2, t=T)
        erb = room(2 * CW).rearrange("p (b c) -> p b c", b=2)
        htb = room(2 * CW).rearrange("p (b c) -> p b c", b=2)
        ub = room(2 * CW).rearrange("p (b c) -> p b c", b=2)
        thb = room(2 * CW).rearrange("p (b c) -> p b c", b=2)
        ob = room(2 * CW).rearrange("p (b c) -> p b c", b=2)
        spb = room(2 * T * PAIR).rearrange("p (b t d) -> p b t d", b=2, t=T)
        m_all = room(NT + 1)
        den_all = room(NT + 1)
        restart = room(NT)
        ab = room(2 * 2 * T).rearrange("p (b k t) -> p b k t", b=2, k=2)
        sc = room(2 * 4 * T).rearrange("p (b k t) -> p b k t", b=2, k=4)
        masked = room(P)
        wts = room(P)
        wtsT = room(P)
        nd = room(D + 1)
        fz = room(16)

        psA = ps("psA", [P, 2 * KB])
        psB = ps("psB", [P, 2 * KB])
        psC = ps("psC", [P, 2 * KB])
        psD = ps("psD", [P, 2 * KB])

        def rows3(ap):
            return ap.rearrange("p (t d) -> p t d", d=D)

        def over_d(ap):
            return ap.unsqueeze(2).to_broadcast([P, T, D])

        def cols(c):
            return bass.ds(c * T, T)

        s_turn = sem("sp_turns")
        s_const = sem("constants_set")
        s_load = sem("inputs_loaded")
        s_wload = sem("weights_loaded")
        s_prep = sem("prep_steps")
        s_pe0 = sem("prep_products")
        s_hot = sem("onehot_made")
        s_hot_free = sem("onehot_slot_free")
        s_count = sem("counts_made")
        s_xin = [sem(f"x_loaded{b}") for b in range(2)]
        s_xc = sem("x_centered")
        s_sq = sem("squares_made")
        s_mean = sem("means_made")
        s_var = sem("variances_made")
        s_rs = sem("inverse_deviations_made")
        s_sd = sem("deviations_made")
        s_h = sem("h_made")
        s_rowx = sem("row_x_rep_set")
        s_row = sem("row_chunk_stored")
        s_rowfree = sem("row_slot_free")
        s_node = sem("node_rows_ready")
        s_btr = sem("h_transposed")
        s_bcp = sem("h_transpose_copied")
        s_lin = sem("linear_made")
        s_linu = sem("linear_used")
        s_started = sem("gathers_started")
        s_got = [sem(f"gathered{b}") for b in range(2)]
        s_gread = sem("gather_read")
        s_scan = sem("scan_steps")
        s_rlast = sem("scan_done")
        s_sub = sem("older_product_subtracted")
        s_prev = [sem(f"older_product_loaded{b}") for b in range(2)]
        s_str = sem("product_transposed")
        s_scp = sem("product_transpose_copied")
        s_ymm = sem("y_part_made")
        s_yadd = sem("y_part_added")
        s_tst = sem("table_chunk_stored")
        s_tfree = sem("table_slot_free")
        s_xz = sem("xz_chunk_stored")
        s_xzfree = sem("xz_slot_free")
        s_fixm = sem("fix_products")
        s_fixv = sem("fix_steps")
        s_fixa = sem("fix_transpose_copied")
        s_fixst = sem("fix_rows_stored")
        s_pass = sem("table_ready")
        s_zero = sem("zero_rows_stored")
        s_yst = sem("y_chunk_stored")
        s_out = sem("out_stored")
        s_repi = sem("source_reps_ready")
        s_idx = sem("indices_staged")
        s_fseg = sem("first_sum_steps")
        s_vin = sem("fill_start_made")
        s_vins = sem("fill_start_steps")
        s_ysel = sem("segment_ends_selected")
        s_fill = sem("fill_steps")
        s_u = sem("l0_sum_made")
        s_x1 = sem("x1_made")
        s_ftr = sem("x1_transposed")
        s_fcp = sem("x1_transpose_copied")
        s_cen = sem("x1_centered")
        s_ht = sem("target_rows_stored")
        s_htfree = sem("target_slot_free")
        s_ld = [sem(f"edge_rows_loaded{b}") for b in range(2)]
        s_lh = [sem(f"target_rows_loaded{b}") for b in range(2)]
        s_th = sem("tanh_made")
        s_q = sem("score_terms_made")
        s_d = sem("score_steps")
        s_exp = sem("exponentials_made")
        s_hw = sem("weighted_h_made")
        s_nb = sem("neighbour_sum_made")
        s_nbst = sem("neighbour_sum_stored")
        s_nbfree = sem("neighbour_slot_free")
        s_fin = sem("attention_fix_steps")
        s_finm = sem("attention_fix_products")
        s_fina = sem("attention_fix_exponentials")
        s_yn = sem("update_table_ready")
        s_nl = [sem(f"node_xz_loaded{b}") for b in range(2)]
        s_sp = sem("sum_and_product_made")
        s_utr = sem("update_transposed")
        s_ucp = sem("update_transpose_copied")
        s_slope = sem("leaky_slope_made")
        s_o = sem("output_made")
        s_ofree = sem("output_slot_free")

        N_CONST, N_LOAD = 12, 4
        N_WLOAD = 2 * 6 + 2 + 2 + 4
        inv = 1.0 / NT
        block = ctx.enter_context(nc.Block())

        @block.sync
        def _(sp):
            sp.dma_start(src_i[:], src.rearrange("(p t) -> p t", t=NT)).then_inc(s_load, 16)
            sp.dma_start(dst_i[:], dst.rearrange("(p t) -> p t", t=NT)).then_inc(s_load, 16)
            sp.dma_start(rep_i[:], dst_next.rearrange("(p t) -> p t", t=NT)).then_inc(s_load, 16)
            sp.dma_start(w1[:], edge_w.rearrange("(p t) -> p t", t=NT)).then_inc(s_load, 16)
            sp.wait_ge(s_const, N_CONST)
            for k in range(6):
                for h in range(2):
                    sp.dma_start(wraw[h * D:(h + 1) * D, k, h * D:(h + 1) * D], W[k]).then_inc(s_wload, 16)
            for h in range(2):
                sp.dma_start(wa_raw[h * D:(h + 1) * D, h * D:(h + 1) * D], Wa).then_inc(s_wload, 16)
            sp.dma_start(w12_raw[:, 0:D], W1).then_inc(s_wload, 16)
            sp.dma_start(w12_raw[:, D:2 * D], W2).then_inc(s_wload, 16)
            for j, b in enumerate((b0, ba, b1, b2)):
                sp.dma_start(brow[:, j, :], b.rearrange("(a d) -> a d", a=1)).then_inc(s_wload, 16)
            for t in tables:
                sp.dma_start(t[EMPTY:EMPTY + P, :], zrow[:, 0:D]).then_inc(s_zero, 16)
            sp.dma_start(y_table[EMPTY:EMPTY + P, :], zrow[:, 0:D]).then_inc(s_zero, 16)
            sp.dma_start(yn_table[EMPTY:EMPTY + P, :], zrow[:]).then_inc(s_zero, 16)

            def load_x(c, b, n):
                if not isinstance(c, int):
                    sp.wait_ge(s_xc, c - 1)
                    sp.sem_inc(s_turn)
                    sp.wait_ge(s_rowx, 3 * (c - 1))
                sp.dma_start(rows3(xbuf[:, b, :]), x_pt[:, cols(c), :]).then_inc(s_xin[b], 16)

            def store_row(c, b, n):
                sp.wait_ge(s_rowx, 3 * (c + 1))
                sp.sem_inc(s_turn)
                sp.wait_ge(s_linu, c + 2)
                sp.dma_start(node_pt[:, cols(c), :], gat[:, b]).then_inc(s_row, 16)
                sp.wait_ge(s_row, (c + 1) * 16)
                sp.sem_inc(s_rowfree)

            sp.sem_inc(s_rowfree, 2)
            one(0, load_x)
            one(1, load_x)

            def row_step(c, b, n):
                store_row(c, b, n)
                load_x(c + 2, b, n + 1)

            steps(sp, 0, NC - 2, row_step)
            one(NC - 2, store_row)
            one(NC - 1, store_row)
            sp.sem_inc(s_node)

            for k in range(1, ORDER + 1):
                g0 = (k - 1) * NC

                def load(c, b, n):
                    if k >= 3:
                        if not isinstance(c, int):
                            sp.wait_ge(s_sub, (k - 3) * NC + c - 1)
                        elif k > 3:
                            sp.wait_ge(s_sub, (k - 3) * NC - 1 + c)
                            sp.sem_inc(s_turn)
                        sp.dma_start(rows3(xbuf[:, b, :]), tab_pt[k - 3][:, cols(c), :]).then_inc(s_prev[b], 16)

                def store(c, b, n):
                    if k < 3:
                        sp.wait_ge(s_rlast, g0 + c + 1)
                        sp.sem_inc(s_turn)
                        rows = run
                    elif k < ORDER:
                        sp.wait_ge(s_sub, (k - 3) * NC + c + 1)
                        sp.sem_inc(s_turn)
                        rows = sout
                    if k < ORDER:
                        sp.dma_start(tab_pt[k - 1][:, cols(c), :], rows3(rows[:, b, :])).then_inc(s_tst, 16)
                    if k == 1:
                        sp.dma_start(xz_pt[:, cols(c), :], gat[:, b, :, 0:2 * D]).then_inc(s_xz, 16)
                        sp.wait_ge(s_xz, (c + 1) * 16)
                        sp.sem_inc(s_xzfree)
                    if k < ORDER:
                        sp.wait_ge(s_tst, (g0 + c + 1) * 16)
                        sp.sem_inc(s_tfree)
                    else:
                        sp.wait_ge(s_yadd, g0 + c + 3)
                        sp.dma_start(yn_pt[:, cols(c), 0:D], rows3(yall[:, bass.ds(c * CW, CW)])).then_inc(s_yst, 16)
                        sp.dma_start(y_pt[:, cols(c), :], rows3(yall[:, bass.ds(c * CW, CW)])).then_inc(s_yst, 16)

                def step(c, b, n):
                    store(c, b, n)
                    load(c + 2, b, n + 1)

                one(0, load)
                one(1, load)
                steps(sp, 0, NC - 2, step)
                one(NC - 2, store)
                one(NC - 1, store)
                if k < ORDER:
                    sp.wait_ge(s_fixv, 3 * k - 1)
                    sp.dma_start(tables[k - 1][FIX:FIX + P, :], fixp[:, k, 0:D]).then_inc(s_fixst, 16)
                    sp.wait_ge(s_fixst, k * 16)
                    sp.wait_ge(s_zero, 16 * (ORDER + 1))
                    sp.sem_inc(s_pass)
            sp.wait_ge(s_fixv, 3 * ORDER)
            sp.dma_start(yn_table[FIX:FIX + P, 0:D], yfix[:, 0:D]).then_inc(s_fixst, 16)
            sp.dma_start(y_table[FIX:FIX + P, :], yfix[:, 0:D]).then_inc(s_fixst, 16)
            sp.wait_ge(s_fixst, (ORDER + 1) * 16)
            sp.wait_ge(s_yst, NC * 32)
            sp.wait_ge(s_zero, 16 * (ORDER + 1))
            sp.sem_inc(s_pass)
            if stop == "y":
                for p in range(1):
                    sp.dma_start(out.rearrange("(p t) d -> p (t d)", t=NT), yall[:]).then_inc(s_out, 16)
                    sp.wait_ge(s_out, 16)
                return

            sp.sem_inc(s_htfree, 2)

            def store_target(c, b, n):
                sp.wait_ge(s_linu, NC + c + 2)
                sp.sem_inc(s_turn)
                sp.dma_start(htd_pt[:, cols((NC - 1) - c), :], rows3(run[:, b, :])).then_inc(s_ht, 16)
                sp.wait_ge(s_ht, (c + 1) * 16)
                sp.sem_inc(s_htfree)

            steps(sp, 0, NC, store_target)

            def load_xz(c, b, n):
                if not isinstance(c, int):
                    sp.wait_ge(s_x1, NC + c - 1)
                    sp.sem_inc(s_turn)
                sp.dma_start(xzb[:, b], xz_pt[:, cols(c), :]).then_inc(s_nl[b], 16)

            def load_edges(c, b, n):
                if not isinstance(c, int):
                    sp.wait_ge(s_linu, 2 * NC + c)
                    sp.sem_inc(s_turn)
                sp.dma_start(rows3(erb[:, b, :]), er_pt[:, cols(c), :]).then_inc(s_ld[b], 16)
                if not isinstance(c, int):
                    sp.wait_ge(s_q, c - 1)
                    sp.sem_inc(s_turn)
                sp.dma_start(rows3(htb[:, b, :]), htd_pt[:, cols(c), :]).then_inc(s_lh[b], 16)

            def store_neighbours(c, b, n):
                sp.wait_ge(s_nb, c + 1)
                sp.sem_inc(s_turn)
                sp.dma_start(yn_pt[:, cols(c), D:PAIR], rows3(sout[:, b, :])).then_inc(s_nbst, 16)
                sp.wait_ge(s_nbst, (c + 1) * 16)
                sp.sem_inc(s_nbfree)

            def source_step(c, b, n):
                load_xz(c + 2, b, n + 1)
                load_edges(c + 2, b, n + 1)
                store_neighbours(c, b, n)

            sp.sem_inc(s_nbfree, 2)
            sp.wait_ge(s_vins, NC + 2)
            one(0, load_xz)
            one(1, load_xz)
            one(0, load_edges)
            one(1, load_edges)
            steps(sp, 0, NC - 2, source_step)
            one(NC - 2, store_neighbours)
            one(NC - 1, store_neighbours)
            sp.wait_ge(s_fin, N_FIN)
            sp.dma_start(yn_table[FIX:FIX + P, D:PAIR], yfix[:, D:PAIR]).then_inc(s_fixst, 16)

            def load_nodes(c, b, n):
                if not isinstance(c, int):
                    sp.wait_ge(s_x1, 2 * NC + c - 1)
                    sp.sem_inc(s_turn)
                sp.dma_start(xzb[:, b], node_pt[:, cols(c), 0:2 * D]).then_inc(s_nl[b], 16)

            def store_out(c, b, n):
                sp.wait_ge(s_o, c + 1)
                sp.sem_inc(s_turn)
                sp.dma_start(out_pt[:, cols(c), :], rows3(sout[:, b, :])).then_inc(s_out, 16)
                sp.wait_ge(s_out, (c + 1) * 16)
                sp.sem_inc(s_ofree)

            def update_io(c, b, n):
                store_out(c, b, n)
                load_nodes(c + 2, b, n + 1)

            one(0, load_nodes)
            one(1, load_nodes)
            sp.wait_ge(s_fixst, (ORDER + 2) * 16)
            sp.sem_inc(s_yn)
            sp.sem_inc(s_ofree, 2)
            steps(sp, 0, NC - 2, update_io)
            one(NC - 2, store_out)
            one(NC - 1, store_out)

        @block.gpsimd
        def _(pool):
            g = nc.gpsimd
            g.memset(ident[:], 0.0).then_inc(s_const, 1)
            g.memset(ones[:], 1.0).then_inc(s_const, 1)
            g.memset(wraw, 0.0).then_inc(s_const, 1)
            g.memset(wa_raw, 0.0).then_inc(s_const, 1)
            g.memset(zrow[:], 0.0).then_inc(s_const, 1)
            g.memset(zeros_h, 0.0).then_inc(s_const, 1)
            g.memset(eps_c[:], EPS).then_inc(s_const, 1)
            g.iota(iota_i, [[1, NT]], base=0, channel_multiplier=0).then_inc(s_const, 1)
            g.iota(pidx_i[:], [[0, 1]], base=0, channel_multiplier=1).then_inc(s_const, 1)
            pool.wait_ge(s_const, 9)
            g.affine_select(out=ident[:], in_=ident[:], compare_op=ALU.not_equal, fill=1.0, base=0,
                            pattern=[[-1, P]], channel_multiplier=1).then_inc(s_const, 1)
            g.affine_select(out=below[:], in_=ones[:], compare_op=ALU.is_gt, fill=0.0, base=0,
                            pattern=[[1, P]], channel_multiplier=-1).then_inc(s_const, 1)
            g.affine_select(out=above[:], in_=ones[:], compare_op=ALU.is_gt, fill=0.0, base=0,
                            pattern=[[-1, P]], channel_multiplier=1).then_inc(s_const, 1)

            pool.wait_ge(s_prep, N_REP)

            def row_parts(c, b, n):
                pool.wait_ge(s_rowfree, c + 1)
                pool.wait_ge(s_xin[b], 16 * (n + 1))
                pool.sem_inc(s_started)
                g.tensor_copy(gat[:, b, :, RREP], lo[:, cols(c)]).then_inc(s_rowx, 1)
                g.tensor_copy(gat[:, b, :, RX:RX + D], rows3(xbuf[:, b, :])).then_inc(s_rowx, 1)
                pool.wait_ge(s_h, c + 1)
                pool.sem_inc(s_started)
                g.tensor_copy(gat[:, b, :, RH:RH + D], rows3(hbuf[:, b, :])).then_inc(s_rowx, 1)

            steps(pool, 0, NC, row_parts)
            pool.wait_ge(s_node, 1)

            def gathers(g0, width, table, indices, freed, at=lambda c: c):
                def chunk(c, b, n):
                    freed(c)
                    pool.sem_inc(s_started)
                    g.tensor_copy(idx[:, b, :], indices[:, cols(at(c))]).then_inc(s_idx, 1)
                    pool.wait_ge(s_idx, g0 + c + 1)
                    pool.sem_inc(s_started)
                    for t in range(T):
                        g.indirect_dma_start(gat[:, b, t, 0:width], None, table,
                                             bass.IndirectOffsetOnAxis(ap=idx[:, b, t:t + 1], axis=0)
                                             ).then_inc(s_got[b], 16)
                one(0, chunk)
                one(1, chunk)
                steps(pool, 2, NC, chunk)

            def freed1(c):
                if not isinstance(c, int):
                    pool.wait_ge(s_gread, c - 1)
                    pool.wait_ge(s_xzfree, c - 1)

            gathers(0, ROW, node_rows, src_i, freed1)
            pool.wait_ge(s_xzfree, NC)
            for k in range(2, ORDER + 1):
                pool.wait_ge(s_pass, k - 1)
                if k == 2:
                    pool.wait_ge(s_repi, 1)

                def freed(c):
                    pool.wait_ge(s_gread, (k - 1) * NC + c - 1)

                gathers((k - 1) * NC, D, tables[k - 2], reps_i, freed)
            if stop == "y":
                return

            def freed_targets(c):
                if isinstance(c, int):
                    pool.wait_ge(s_gread, ORDER * NC + c - 1)
                else:
                    pool.wait_ge(s_x1, c - 1)

            gathers(ORDER * NC, ROW, node_rows, dst_i, freed_targets, at=lambda c: (NC - 1) - c)

            def freed_sources(c):
                pool.wait_ge(s_x1, NC + c - 1)

            pool.wait_ge(s_pass, ORDER)
            gathers((ORDER + 1) * NC, D, y_table, reps_i, freed_sources)

            def freed_nodes(c):
                if isinstance(c, int):
                    pool.wait_ge(s_x1, 2 * NC + c - 1)
                else:
                    pool.wait_ge(s_sp, 2 * (c - 1))

            pool.wait_ge(s_yn, 1)
            gathers((ORDER + 2) * NC, PAIR, yn_table, rep_i, freed_nodes)

        @block.scalar
        def _(act):
            a = nc.scalar

            def square(c, b, n):
                act.wait_ge(s_xc, c + 1)
                a.activation(sq[:, b, :], hbuf[:, b, :], ACT.Square).then_inc(s_sq, 1)

            def node_tail(c, b, n):
                act.wait_ge(s_var, c + 1)
                a.activation(stat[:, b, 3, :], stat[:, b, 2, :], ACT.Sqrt, bias=eps_c[:], scale=1.0 / D
                             ).then_inc(s_sd, 1)
                act.wait_ge(s_btr, c + 1)
                a.copy(hT[:], psC[:, 0:CW]).then_inc(s_bcp, 1)
                act.wait_ge(s_lin, c + 1)
                act.wait_ge(s_rowfree, c + 1)
                a.copy(gat[:, b, :, RZ:RZ + D], rows3(psD[:, 0:CW])).then_inc(s_linu, 1)

            def node_step(c, b, n):
                square(c + 1, 1 - b, n + b)
                node_tail(c, b, n)

            act.wait_ge(s_const, N_CONST)
            act.sem_inc(s_linu)
            one(0, square)
            one(0, node_step)
            steps(act, 1, NC - 1, node_step)
            one(NC - 1, node_tail)

            for k in range(1, ORDER + 1):
                g0 = (k - 1) * NC

                def copy(c, b, n):
                    act.wait_ge(s_str, g0 + c + 1)
                    a.copy(xT[:], psA[:, 0:CW]).then_inc(s_scp, 1)

                steps(act, 0, NC, copy)
                act.wait_ge(s_fixm, 3 * k - 1)
                a.copy(fixT[:], psC[:, P:2 * P]).then_inc(s_fixa, 1)
            if stop == "y":
                return

            def copy_x1(seq, b):
                act.wait_ge(s_ftr, seq + 1)
                a.copy(xT[:], psA[:, 0:CW]).then_inc(s_fcp, 1)

            def squares(seq, b):
                act.wait_ge(s_cen, seq + 1)
                a.activation(sq[:, b, :], psB[:, 0:CW], ACT.Square).then_inc(s_sq, 1)

            def deviations(seq, b):
                act.wait_ge(s_var, NC + seq + 1)
                a.activation(stat[:, b, 3, :], stat[:, b, 2, :], ACT.Sqrt, bias=eps_c[:], scale=1.0 / D
                             ).then_inc(s_sd, 1)

            def copy_h(seq, b):
                act.wait_ge(s_btr, NC + seq + 1)
                a.copy(hT[:], psC[:, 0:CW]).then_inc(s_bcp, 1)

            def target_tail(c, b, n):
                deviations(c, b)

            def target_out(c, b, n):
                copy_h(c, b)
                act.wait_ge(s_lin, NC + c + 1)
                act.wait_ge(s_htfree, c + 1)
                a.copy(run[:, b, :], psD[:, 0:CW]).then_inc(s_linu, 1)

            def target_step(c, b, n):
                copy_x1(c + 1, 1 - b)
                deviations(c, b)
                squares(c + 1, 1 - b)
                target_out(c, b, n)

            copy_x1(0, 0)
            squares(0, 0)
            one(0, target_step)
            steps(act, 1, NC - 1, target_step)
            deviations(NC - 1, 1)
            target_out(NC - 1, 1, 0)

            def source_front(c, b):
                copy_x1(NC + c, b)
                squares(NC + c, b)
                deviations(NC + c, b)
                copy_h(NC + c, b)

            def tanh(c, b):
                act.wait_ge(s_linu, 2 * NC + c + 2)
                a.activation(thb[:, b, :], ub[:, b, :], ACT.Tanh).then_inc(s_th, 1)

            def exponentials(c, b):
                act.wait_ge(s_d, 12 * c + 7)
                a.activation(ab[:, b], ab[:, b], ACT.Exp).then_inc(s_exp, 1)

            def source_step(c, b, n):
                if not (isinstance(c, int) and c == 0):
                    exponentials(c - 1, 1 - b)
                source_front(c + 1, 1 - b)
                tanh(c, b)

            source_front(0, 0)
            one(0, source_step)
            steps(act, 1, NC - 1, source_step)
            exponentials(NC - 2, 0)
            tanh(NC - 1, 1)
            exponentials(NC - 1, 1)
            act.wait_ge(s_fin, F_MAX)
            a.activation(wts, masked, ACT.Exp, bias=fz[:, 3:4]).then_inc(s_fina, 1)
            a.activation(fz[:, 4:5], fz[:, 0:1], ACT.Exp, bias=fz[:, 3:4]).then_inc(s_fina, 1)

            def update_out(c, b, n):
                for q in range(2):
                    act.wait_ge(s_utr, 2 * c + q + 1)
                    a.copy(hT[:], psC[:, 0:CW]).then_inc(s_ucp, 1)
                act.wait_ge(s_lin, 3 * NC + c + 1)
                a.mul(ob[:, b, :], psD[:, 0:CW], 0.2).then_inc(s_slope, 1)

            def update_step(c, b, n):
                copy_x1(2 * NC + c + 1, 1 - b)
                deviations(2 * NC + c, b)
                squares(2 * NC + c + 1, 1 - b)
                update_out(c, b, n)

            copy_x1(2 * NC, 0)
            squares(2 * NC, 0)
            one(0, update_step)
            steps(act, 1, NC - 1, update_step)
            deviations(3 * NC - 1, 1)
            update_out(NC - 1, 1, 0)

        @block.tensor
        def _(pe):
            m = nc.tensor
            pe.wait_ge(s_const, N_CONST)
            pe.wait_ge(s_prep, N_IOTA)
            m.matmul(psA[:, 0:NT], zeros_h, iota_h, start=True, stop=False)
            with pe.Fori(0, NT // HR) as i:
                for j in range(HR):
                    pe.wait_ge(s_hot, 2 * HR * i + 2 * (j + 1))
                    m.matmul(psA[:, 0:NT], onehot[:, j, 0:P], onehot[:, j, P:], start=False, stop=False
                             ).then_inc(s_hot_free, 1)
            m.matmul(psA[:, 0:NT], zeros_h, iota_h, start=False, stop=True).then_inc(s_count, 1)
            pe.wait_ge(s_prep, N_CUM)
            m.matmul(psB[:, 0:1], below[:], incl[:, NT - 1:NT], start=True, stop=True).then_inc(s_pe0, 1)
            pe.wait_ge(s_prep, N_DIAG1)
            m.matmul(psD[:, 0:P], ones[:], diag[:], start=True, stop=True).then_inc(s_pe0, 1)
            pe.wait_ge(s_prep, N_DIAG2)
            m.matmul(psD[:, KB:KB + P], ones[:], diag[:], start=True, stop=True).then_inc(s_pe0, 1)
            pe.wait_ge(s_wload, 16 * N_WLOAD)
            m.transpose(psC[:, 0:P], wa_raw, ident[:]).then_inc(s_pe0, 1)
            m.transpose(psC[:, P:P + D], w12_raw, ident[0:D, 0:D]).then_inc(s_pe0, 1)
            pe.wait_ge(s_prep, N_PREP)

            def bias_rows(ps_, j, stop=False):
                for q in range(2):
                    n = min(KB, CW - q * KB)
                    m.matmul(ps_[:, q * KB:q * KB + n], ones[0:1, :],
                             bias[:, j].rearrange("a t d -> a (t d)")[:, 0:n], start=True, stop=False)

            def linear_h(c, b, n):
                pe.wait_ge(s_h, c + 1)
                for j in range(PAIRS):
                    i_ = m.transpose(psC[:, j * P:(j + 1) * P], hbuf[:, b, j * P:(j + 1) * P], ident[:])
                i_.then_inc(s_btr, 1)
                pe.wait_ge(s_linu, c + 1)
                bias_rows(psD, 0)
                pe.wait_ge(s_bcp, c + 1)
                for j in range(PAIRS):
                    i_ = m.matmul(psD[:, j * P:(j + 1) * P], hT[:, j * P:(j + 1) * P], wmix[:, 0, :],
                                  start=False, stop=(j % 4 == 3 or j == PAIRS - 1))
                i_.then_inc(s_lin, 1)

            steps(pe, 0, NC, linear_h)

            for k in range(1, ORDER + 1):
                g0 = (k - 1) * NC

                def y_part(c, b, n):
                    if k < 3:
                        pe.wait_ge(s_rlast, g0 + c + 1)
                        made = run
                    else:
                        pe.wait_ge(s_sub, (k - 3) * NC + c + 1)
                        made = sout
                    for j in range(PAIRS):
                        i_ = m.transpose(psA[:, j * P:(j + 1) * P], made[:, b, j * P:(j + 1) * P], ident[:])
                    i_.then_inc(s_str, 1)
                    pe.wait_ge(s_yadd, g0 + c + 1)
                    pe.wait_ge(s_scp, g0 + c + 1)
                    part = (psB, psD)[b]
                    for j in range(PAIRS):
                        i_ = m.matmul(part[:, j * P:(j + 1) * P], xT[:, j * P:(j + 1) * P], wmix[:, k, :],
                                      start=True, stop=True)
                    i_.then_inc(s_ymm, 1)

                steps(pe, 0, NC, y_part)
                pe.wait_ge(s_rlast, k * NC)
                m.matmul(psC[:, 0:D], carry_in[:], run[:, 1, CW - D:CW], start=True, stop=True
                         ).then_inc(s_fixm, 1)
                pe.wait_ge(s_fixv, 3 * k - 1)
                m.transpose(psC[:, P:2 * P], fixp[:, k, :], ident[:]).then_inc(s_fixm, 1)
                pe.wait_ge(s_fixa, k)
                m.matmul(psC[:, 2 * P:3 * P], fixT[:], wmix[:, k, :], start=True, stop=True
                         ).then_inc(s_fixm, 1)
            if stop == "y":
                return
            pe.wait_ge(s_fixv, 3 * ORDER)
            m.matmul(psC[:, 0:D], v_from[:], yfix[:, 0:D], start=True, stop=True).then_inc(s_vin, 1)

            def front_transpose(seq, b):
                pe.wait_ge(s_x1, seq + 1)
                for j in range(PAIRS):
                    i_ = m.transpose(psA[:, j * P:(j + 1) * P], xbuf[:, b, j * P:(j + 1) * P], ident[:])
                i_.then_inc(s_ftr, 1)

            def front_center(seq, b):
                pe.wait_ge(s_fcp, seq + 1)
                pe.wait_ge(s_h, NC + seq)
                for j in range(PAIRS):
                    i_ = m.matmul(psB[:, j * P:(j + 1) * P], xT[:, j * P:(j + 1) * P], center[:],
                                  start=True, stop=True)
                i_.then_inc(s_cen, 1)

            def attention_map(seq, b):
                pe.wait_ge(s_h, NC + seq + 1)
                for j in range(PAIRS):
                    i_ = m.transpose(psC[:, j * P:(j + 1) * P], hbuf[:, b, j * P:(j + 1) * P], ident[:])
                i_.then_inc(s_btr, 1)
                pe.wait_ge(s_linu, NC + seq + 1)
                bias_rows(psD, 1)
                pe.wait_ge(s_bcp, NC + seq + 1)
                for j in range(PAIRS):
                    i_ = m.matmul(psD[:, j * P:(j + 1) * P], hT[:, j * P:(j + 1) * P], watt[:],
                                  start=False, stop=(j % 4 == 3 or j == PAIRS - 1))
                i_.then_inc(s_lin, 1)

            def target_step(c, b, n):
                front_transpose(c + 1, 1 - b)
                front_center(c + 1, 1 - b)
                attention_map(c, b)

            pe.wait_ge(s_vins, NC + 1)
            front_transpose(0, 0)
            front_center(0, 0)
            one(0, target_step)
            steps(pe, 1, NC - 1, target_step)
            attention_map(NC - 1, 1)

            def source_step(c, b, n):
                front_transpose(NC + c, b)
                front_center(NC + c, b)
                attention_map(NC + c, b)

            steps(pe, 0, NC, source_step)
            pe.wait_ge(s_fin, F_DIAG)
            m.matmul(psC[:, 0:P], ones[:], diag[:], start=True, stop=True).then_inc(s_finm, 1)
            pe.wait_ge(s_fina, 2)
            m.transpose(psC[:, P:2 * P], wts, ident[:]).then_inc(s_finm, 1)
            pe.wait_ge(s_fin, F_WTS)
            m.matmul(psC[:, 2 * P:2 * P + D + 1], wtsT, nd, start=True, stop=True).then_inc(s_finm, 1)
            pe.wait_ge(s_fin, N_FIN)

            def update_map(c, b):
                pe.wait_ge(s_sp, 2 * (c + 1))
                pe.wait_ge(s_linu, 3 * NC + c + 1)
                bias_rows(psD, 2)
                for q in range(2):
                    for j in range(PAIRS):
                        i_ = m.transpose(psC[:, j * P:(j + 1) * P], spb[:, b, q * PAIRS + j, :], ident[:])
                    i_.then_inc(s_utr, 1)
                    pe.wait_ge(s_ucp, 2 * c + q + 1)
                    for j in range(PAIRS):
                        t = q * PAIRS + j
                        i_ = m.matmul(psD[:, t * D:(t + 1) * D], hT[:, j * P:(j + 1) * P], w12[:],
                                      start=False, stop=(t % 8 == 7 or t == T - 1))
                i_.then_inc(s_lin, 1)

            def update_step(c, b, n):
                front_transpose(2 * NC + c + 1, 1 - b)
                front_center(2 * NC + c + 1, 1 - b)
                update_map(c, b)

            front_transpose(2 * NC, 0)
            front_center(2 * NC, 0)
            one(0, update_step)
            steps(pe, 1, NC - 1, update_step)
            update_map(NC - 1, 1)

        @block.vector
        def _(dve):
            v = nc.vector
            done = [0]
            marks = {}

            def prep(i_, wait=True):
                i_.then_inc(s_prep, 1)
                done[0] += 1
                if wait:
                    dve.wait_ge(s_prep, done[0])

            def floor_nt(out_, in_):
                prep(v.tensor_scalar(out_, in_, inv, -0.5 + 0.5 * inv, ALU.mult, ALU.add))
                prep(v.tensor_scalar(out_, out_, ROUND, -ROUND, ALU.add, ALU.add))

            dve.wait_ge(s_const, N_CONST)
            prep(v.tensor_copy(iota_h, iota_i))
            assert done[0] == N_IOTA
            dve.wait_ge(s_load, 16 * N_LOAD)
            prep(v.tensor_copy(dstf[:], dst_i[:]))
            floor_nt(hi[:], dstf[:])
            prep(v.scalar_tensor_tensor(out=lo[:], in0=hi[:], scalar=-float(NT), in1=dstf[:],
                                        op0=ALU.mult, op1=ALU.add))
            dve.sem_inc(s_hot_free, HR)
            with dve.Fori(0, NT // HR) as i:
                for j in range(HR):
                    dve.wait_ge(s_hot_free, HR * i + j + 1)
                    v.tensor_scalar(onehot[:, j, 0:P], iota_h[:, 0:P], hi[:, bass.ds(HR * i + j, 1)], None,
                                    ALU.is_equal).then_inc(s_hot, 1)
                    v.tensor_scalar(onehot[:, j, P:], iota_h, lo[:, bass.ds(HR * i + j, 1)], None,
                                    ALU.is_equal).then_inc(s_hot, 1)
            dve.wait_ge(s_count, 1)
            prep(v.tensor_copy(hi[:], psA[:, 0:NT]))
            prep(v.memset(tmp[:], 1.0))
            prep(v.tensor_tensor_scan(incl[:], tmp[:], hi[:], 0.0, ALU.mult, ALU.add))
            assert done[0] == N_CUM
            dve.wait_ge(s_pe0, 1)
            prep(v.tensor_copy(small[:, 0:1], psB[:, 0:1]))
            prep(v.tensor_scalar(incl[:], incl[:], small[:, 0:1], None, ALU.add))
            prep(v.tensor_tensor(lo[:], incl[:], hi[:], ALU.subtract))
            prep(v.tensor_scalar(incl[:], incl[:], -1.0, None, ALU.add))
            floor_nt(tmp[:], incl[:])
            floor_nt(lo[:], lo[:])
            prep(v.tensor_tensor(lo[:], tmp[:], lo[:], ALU.is_gt))
            prep(v.scalar_tensor_tensor(out=tmp[:], in0=tmp[:], scalar=float(FIX), in1=incl[:],
                                        op0=ALU.add, op1=ALU.subtract))
            prep(v.tensor_tensor(tmp[:], tmp[:], lo[:], ALU.mult))
            prep(v.tensor_tensor(tmp[:], tmp[:], incl[:], ALU.add))
            prep(v.tensor_copy(pidx[:], pidx_i[:]))
            prep(v.tensor_scalar(hi[:], hi[:], 0.0, None, ALU.is_equal))
            prep(v.tensor_scalar(lo[:], hi[:], -1.0, 1.0, ALU.mult, ALU.add))
            prep(v.tensor_tensor(tmp[:], tmp[:], lo[:], ALU.mult))
            prep(v.tensor_scalar(small[:, 1:2], pidx[:], float(EMPTY), None, ALU.add))
            prep(v.scalar_tensor_tensor(out=lo[:], in0=hi[:], scalar=small[:, 1:2], in1=tmp[:],
                                        op0=ALU.mult, op1=ALU.add))
            prep(v.tensor_copy(tmp[:], rep_i[:]))
            prep(v.tensor_tensor(notlast[:], dstf[:], tmp[:], ALU.is_equal))
            prep(v.tensor_copy(rep_i[:], lo[:]))
            assert done[0] == N_REP
            prep(v.tensor_scalar(last[:], notlast[:], -1.0, 1.0, ALU.mult, ALU.add))
            prep(v.memset(same[:, 0:1], 0.0))
            prep(v.tensor_copy(same[:, 1:NT], notlast[:, 0:NT - 1]))
            prep(v.tensor_scalar(first[:], dstf[:], dstf[:, 0:1], None, ALU.is_equal))
            prep(v.tensor_tensor(last_first[:, 0:NT - 1], first[:, 0:NT - 1], last[:, 0:NT - 1], ALU.mult))
            prep(v.tensor_copy(last_first[:, NT - 1:NT], first[:, NT - 1:NT]))
            prep(v.tensor_tensor(small[:, 2:3], first[:, NT - 1:NT], notlast[:, NT - 1:NT], ALU.mult))
            prep(v.tensor_scalar(ends_in[:], small[:, 2:3], -1.0, 1.0, ALU.mult, ALU.add))
            prep(v.tensor_scalar(diag[:], ident[:], dstf[:, 0:1], None, ALU.mult))
            assert done[0] == N_DIAG1
            dve.wait_ge(s_pe0, 2)
            prep(v.tensor_scalar(diag[:], ident[:], dstf[:, NT - 1:NT], None, ALU.mult))
            assert done[0] == N_DIAG2
            prep(v.scalar_tensor_tensor(out=carry_in[:], in0=psD[:, 0:P], scalar=dstf[:, NT - 1:NT],
                                        in1=below[:], op0=ALU.is_equal, op1=ALU.mult))
            dve.wait_ge(s_pe0, 3)
            prep(v.scalar_tensor_tensor(out=carry_to[:], in0=psD[:, KB:KB + P], scalar=dstf[:, 0:1],
                                        in1=above[:], op0=ALU.is_equal, op1=ALU.mult))
            prep(v.tensor_scalar(v_from[:], carry_to[:], ends_in[:], None, ALU.mult))
            prep(v.tensor_scalar(w2[:], w1[:], 2.0, None, ALU.mult))
            dve.wait_ge(s_wload, 16 * N_WLOAD)
            prep(v.tensor_tensor(wmix[:, 0, :], wraw[:, 0, :], wraw[:, 2, :], ALU.subtract))
            prep(v.tensor_tensor(wmix[:, 0, :], wmix[:, 0, :], wraw[:, 4, :], ALU.add))
            prep(v.tensor_tensor(wmix[:, 1, :], wraw[:, 1, :], wraw[:, 3, :], ALU.subtract))
            prep(v.tensor_tensor(wmix[:, 1, :], wmix[:, 1, :], wraw[:, 5, :], ALU.add))
            for k in (2, 3):
                prep(v.tensor_tensor(wmix[:, k, :], wraw[:, k, :], wraw[:, k + 2, :], ALU.subtract))
                prep(v.tensor_scalar(wmix[:, k, :], wmix[:, k, :], 2.0, None, ALU.mult))
            for k in (4, 5):
                prep(v.tensor_scalar(wmix[:, k, :], wraw[:, k, :], 2.0, None, ALU.mult))
            dve.wait_ge(s_pe0, 5)
            prep(v.tensor_copy(watt[:], psC[:, 0:P]))
            prep(v.tensor_copy(w12[:], psC[:, P:P + D]))
            prep(v.tensor_tensor(brow[:, 2, :], brow[:, 2, :], brow[:, 3, :], ALU.add))
            for j in range(3):
                prep(v.tensor_copy(bias[:, j], brow[:, j, :].unsqueeze(1).to_broadcast([1, 8, D])))
            prep(v.tensor_copy(center[:], ident[:]))
            for h in range(2):
                q = slice(h * D, (h + 1) * D)
                prep(v.tensor_scalar(center[q, q], center[q, q], -1.0 / D, None, ALU.add))
            prep(v.memset(run[:], 0.0))
            prep(v.memset(fseg[:], 0.0))
            assert done[0] == N_PREP, done[0]

            def centered(c, b, n):
                dve.wait_ge(s_xin[b], 16 * (n + 1))
                v.tensor_reduce(stat[:, b, 0, :], rows3(xbuf[:, b, :]), AX.X, ALU.add).then_inc(s_mean, 1)
                dve.wait_ge(s_mean, 2 * c + 1)
                v.tensor_scalar(stat[:, b, 1, :], stat[:, b, 0, :], -1.0 / D, None, ALU.mult).then_inc(s_mean, 1)
                dve.wait_ge(s_mean, 2 * c + 2)
                if not isinstance(c, int):
                    dve.wait_ge(s_btr, c - 1)
                    dve.wait_ge(s_rowx, 3 * (c - 1))
                v.tensor_tensor(rows3(hbuf[:, b, :]), rows3(xbuf[:, b, :]), over_d(stat[:, b, 1, :]),
                                ALU.add).then_inc(s_xc, 1)

            def inverse_deviation(seq, b):
                dve.wait_ge(s_sq, seq + 1)
                v.tensor_reduce(stat[:, b, 2, :], rows3(sq[:, b, :]), AX.X, ALU.add).then_inc(s_var, 1)
                dve.wait_ge(s_sd, seq + 1)
                v.reciprocal(stat[:, b, 0, :], stat[:, b, 3, :]).then_inc(s_rs, 1)
                dve.wait_ge(s_rs, seq + 1)

            def normed(c, b, n):
                inverse_deviation(c, b)
                v.scalar_tensor_tensor(out=rows3(hbuf[:, b, :]), in0=rows3(hbuf[:, b, :]), scalar=0.0,
                                       in1=over_d(stat[:, b, 0, :]), op0=ALU.max, op1=ALU.mult
                                       ).then_inc(s_h, 1)

            def node_step(c, b, n):
                centered(c + 1, 1 - b, n + b)
                normed(c, b, n)

            one(0, centered)
            one(0, node_step)
            steps(dve, 1, NC - 1, node_step)
            one(NC - 1, normed)

            def scan(seq, c, b, terms, keep):
                base = seq * CHAIN

                def run_step(t):
                    before = run[:, 1 - b, CW - D:CW] if t == 0 else run[:, b, (t - 1) * D:t * D]
                    return v.scalar_tensor_tensor(out=run[:, b, t * D:(t + 1) * D], in0=before, scalar=keep(t),
                                                  in1=terms[:, t * D:(t + 1) * D], op0=ALU.mult, op1=ALU.add)

                def first_step(t):
                    return v.scalar_tensor_tensor(out=fseg[:], in0=run[:, b, t * D:(t + 1) * D],
                                                  scalar=last_first[:, bass.ds(c * T + t, 1)], in1=fseg[:],
                                                  op0=ALU.mult, op1=ALU.add)

                run_step(0).then_inc(s_scan, 1)
                for t in range(1, T):
                    dve.wait_ge(s_scan, base + max(2 * (t - 1), 1))
                    run_step(t).then_inc(s_rlast if t == T - 1 else s_scan, 1)
                    if t > 1:
                        dve.wait_ge(s_scan, base + 2 * t - 1)
                    first_step(t - 1).then_inc(s_scan, 1)
                dve.wait_ge(s_rlast, seq + 1)
                dve.wait_ge(s_scan, base + CHAIN - 1)
                first_step(T - 1).then_inc(s_scan, 1)

            fs = [0]

            def fseg_step(i_):
                i_.then_inc(s_fseg, 1)
                fs[0] += 1
                dve.wait_ge(s_fseg, fs[0])

            dve.sem_inc(s_yadd, 2)
            dve.sem_inc(s_tfree, 2)
            for k in range(1, ORDER + 1):
                g0 = (k - 1) * NC
                weight = w1 if k < 3 else w2
                if k == ORDER:
                    dve.wait_ge(s_tfree, (ORDER - 1) * NC + 2)

                def product(c, b, n):
                    dve.wait_ge(s_got[b], 16 * T * ((k - 1) * NC // 2 + n + 1))
                    at = 0
                    if k == 1:
                        at = RH
                        v.tensor_copy(hi[:, cols(c)], gat[:, b, :, RREP]).then_inc(s_vins, 1)
                    v.tensor_tensor(rows3(hbuf[:, b, :]), gat[:, b, :, at:at + D], over_d(weight[:, cols(c)]),
                                    ALU.mult).then_inc(s_gread, 1)
                    dve.wait_ge(s_gread, g0 + c + 1)
                    if k < ORDER:
                        dve.wait_ge(s_tfree, g0 + c + 1)
                    scan(g0 + c, c, b, hbuf[:, b, :], lambda t: same[:, bass.ds(c * T + t, 1)])
                    if k >= 3:
                        dve.wait_ge(s_prev[b], 16 * ((k - 3) * NC // 2 + n + 1))
                        v.tensor_tensor(sout[:, b, :], run[:, b, :], xbuf[:, b, :], ALU.subtract
                                        ).then_inc(s_sub, 1)

                def y_add(c, b, n):
                    dve.wait_ge(s_ymm, g0 + c + 1)
                    part = (psB, psD)[b][:, 0:CW]
                    y = yall[:, bass.ds(c * CW, CW)]
                    if k == 1:
                        v.tensor_copy(y, part).then_inc(s_yadd, 1)
                    else:
                        v.tensor_tensor(y, part, y, ALU.add).then_inc(s_yadd, 1)

                def step(c, b, n):
                    product(c + 1, 1 - b, n + b)
                    y_add(c, b, n)

                one(0, product)
                one(0, step)
                steps(dve, 1, NC - 1, step)
                if k >= 3:
                    dve.wait_ge(s_scan, k * NC * CHAIN)
                    fseg_step(v.tensor_tensor(fseg[:], fseg[:], fixp[:, k - 2, 0:D], ALU.subtract))
                dve.wait_ge(s_scan, k * NC * CHAIN)
                dve.wait_ge(s_fixm, 3 * k - 2)
                v.tensor_tensor(fixp[:, k, 0:D], psC[:, 0:D], fseg[:], ALU.add).then_inc(s_fixv, 1)
                if k < 3:
                    v.tensor_copy(fixp[:, k, D:PAIR], psC[:, 0:D]).then_inc(s_fixv, 1)
                else:
                    v.tensor_tensor(fixp[:, k, D:PAIR], psC[:, 0:D], fixp[:, k - 2, D:PAIR], ALU.subtract
                                    ).then_inc(s_fixv, 1)
                if k == 1:
                    dve.wait_ge(s_vins, NC)
                    v.tensor_copy(reps_i[:], hi[:]).then_inc(s_repi, 1)
                one(NC - 1, y_add)
                dve.wait_ge(s_fixv, 3 * k - 1)
                fseg_step(v.memset(fseg[:], 0.0))
                dve.wait_ge(s_fixm, 3 * k)
                if k == 1:
                    v.tensor_copy(yfix[:], psC[:, 2 * P:3 * P]).then_inc(s_fixv, 1)
                else:
                    v.tensor_tensor(yfix[:], psC[:, 2 * P:3 * P], yfix[:], ALU.add).then_inc(s_fixv, 1)
                dve.wait_ge(s_fixv, 3 * k)
            if stop == "y":
                return

            v.tensor_scalar(cfill[:], yfix[:, D:PAIR], ends_in[:], None, ALU.mult).then_inc(s_ysel, 1)
            dve.wait_ge(s_vin, 1)
            v.tensor_copy(vinit[:], psC[:, 0:D]).then_inc(s_vins, 1)
            dve.wait_ge(s_vins, NC + 1)
            dve.wait_ge(s_ysel, 1)
            got6 = ORDER * NC // 2

            def x1_of(seq, b, z_rows, x_rows, y_rows):
                v.tensor_tensor(rows3(xbuf[:, b, :]), y_rows, z_rows, ALU.add).then_inc(s_u, 1)
                dve.wait_ge(s_u, seq + 1)
                v.scalar_tensor_tensor(out=rows3(xbuf[:, b, :]), in0=rows3(xbuf[:, b, :]), scalar=0.0,
                                       in1=x_rows, op0=ALU.max, op1=ALU.add).then_inc(s_x1, 1)

            def h1_of(seq, b):
                inverse_deviation(NC + seq, b)
                v.scalar_tensor_tensor(out=rows3(hbuf[:, b, :]), in0=rows3(psB[:, 0:CW]), scalar=0.0,
                                       in1=over_d(stat[:, b, 0, :]), op0=ALU.max, op1=ALU.mult
                                       ).then_inc(s_h, 1)

            def fill(c, b, n):
                at = (NC - 1) - c
                filled = sout[:, b, :]
                v.tensor_tensor(rows3(filled), rows3(yall[:, bass.ds(at * CW, CW)]), over_d(last[:, cols(at)]),
                                ALU.mult).then_inc(s_ysel, 1)
                dve.wait_ge(s_ysel, c + 2)
                base = 2 * T * c

                def fill_step(s):
                    t = T - 1 - s
                    if s > 0:
                        after = filled[:, (t + 1) * D:(t + 2) * D]
                    elif isinstance(c, int) and c == 0:
                        after = vinit[:]
                    else:
                        after = sout[:, 1 - b, 0:D]
                    v.scalar_tensor_tensor(out=filled[:, t * D:(t + 1) * D], in0=after,
                                           scalar=notlast[:, bass.ds(at * T + t, 1)],
                                           in1=filled[:, t * D:(t + 1) * D], op0=ALU.mult, op1=ALU.add
                                           ).then_inc(s_fill, 1)

                def carry_step(s):
                    t = T - 1 - s
                    v.scalar_tensor_tensor(out=xbuf[:, b, t * D:(t + 1) * D], in0=cfill[:],
                                           scalar=first[:, bass.ds(at * T + t, 1)],
                                           in1=filled[:, t * D:(t + 1) * D], op0=ALU.mult, op1=ALU.add
                                           ).then_inc(s_fill, 1)

                fill_step(0)
                for s in range(1, T):
                    dve.wait_ge(s_fill, base + max(2 * (s - 1), 1))
                    fill_step(s)
                    carry_step(s - 1)
                dve.wait_ge(s_fill, base + 2 * T - 2)
                carry_step(T - 1)
                dve.wait_ge(s_fill, base + 2 * T)
                dve.wait_ge(s_got[b], 16 * T * (got6 + n + 1))
                x1_of(c, b, gat[:, b, :, RZ:RZ + D], gat[:, b, :, RX:RX + D], rows3(xbuf[:, b, :]))

            def target_step(c, b, n):
                fill(c + 1, 1 - b, n + b)
                h1_of(c, b)

            one(0, fill)
            one(0, target_step)
            steps(dve, 1, NC - 1, target_step)
            h1_of(NC - 1, 1)

            dve.wait_ge(s_x1, NC)
            v.memset(m_all, 0.0).then_inc(s_vins, 1)
            fseg_step(v.memset(den_all, 0.0))
            fseg_step(v.tensor_scalar(restart, same[:], -1.0, BIG, ALU.add, ALU.mult))
            dve.wait_ge(s_vins, NC + 2)
            got7 = (ORDER + 1) * NC // 2
            got8 = (ORDER + 2) * NC // 2

            def source_x1(c, b, n):
                dve.wait_ge(s_nl[b], 16 * (n + 1))
                dve.wait_ge(s_got[b], 16 * T * (got7 + n + 1))
                x1_of(NC + c, b, xzb[:, b, :, D:PAIR], xzb[:, b, :, 0:D], gat[:, b, :, 0:D])

            def add_attributes(c, b, n):
                dve.wait_ge(s_lin, 2 * NC + c + 1)
                dve.wait_ge(s_ld[b], 16 * (n + 1))
                v.tensor_tensor(ub[:, b, :], psD[:, 0:CW], erb[:, b, :], ALU.add).then_inc(s_linu, 1)

            def scores(c, b, n):
                d0 = 12 * c
                s1, s2, s3 = (sc[:, b, q, :] for q in range(3))
                mx = m_all[:, bass.ds(c * T + 1, T)]
                dve.wait_ge(s_th, c + 1)
                dve.wait_ge(s_lh[b], 16 * (n + 1))
                v.tensor_tensor(ub[:, b, :], thb[:, b, :], htb[:, b, :], ALU.mult).then_inc(s_q, 1)
                dve.wait_ge(s_q, c + 1)
                v.tensor_reduce(s1, rows3(ub[:, b, :]), AX.X, ALU.add).then_inc(s_d, 1)
                dve.wait_ge(s_d, d0 + 1)
                v.tensor_scalar(s2, s1, 0.2 / 8.0, None, ALU.mult).then_inc(s_d, 1)
                dve.wait_ge(s_d, d0 + 2)
                v.scalar_tensor_tensor(out=s3, in0=s1, scalar=1.0 / 8.0, in1=s2, op0=ALU.mult, op1=ALU.max
                                       ).then_inc(s_d, 1)
                dve.wait_ge(s_d, d0 + 3)
                v.tensor_tensor_scan(mx, restart[:, cols(c)], s3, m_all[:, bass.ds(c * T, 1)],
                                     ALU.add, ALU.max).then_inc(s_d, 1)
                dve.wait_ge(s_d, d0 + 4)
                v.tensor_tensor(s1, m_all[:, cols(c)], mx, ALU.subtract).then_inc(s_d, 1)
                dve.wait_ge(s_d, d0 + 5)
                v.tensor_scalar(ab[:, b, 0, :], s1, 0.0, None, ALU.min).then_inc(s_d, 1)
                v.tensor_tensor(ab[:, b, 1, :], s3, mx, ALU.subtract).then_inc(s_d, 1)

            def sums(c, b, n):
                d0 = 12 * c + 7
                s4, s1 = sc[:, b, 3, :], sc[:, b, 0, :]
                den = den_all[:, bass.ds(c * T + 1, T)]
                dve.wait_ge(s_exp, c + 1)
                v.tensor_tensor(s4, ab[:, b, 0, :], same[:, cols(c)], ALU.mult).then_inc(s_d, 1)
                v.tensor_tensor(rows3(thb[:, b, :]), rows3(hbuf[:, b, :]), over_d(ab[:, b, 1, :]),
                                ALU.mult).then_inc(s_hw, 1)
                dve.wait_ge(s_d, d0 + 1)
                v.tensor_tensor_scan(den, s4, ab[:, b, 1, :], den_all[:, bass.ds(c * T, 1)],
                                     ALU.mult, ALU.add).then_inc(s_d, 1)
                dve.wait_ge(s_d, d0 + 2)
                v.tensor_scalar(s1, den, 1e-9, None, ALU.add).then_inc(s_d, 1)
                dve.wait_ge(s_d, d0 + 3)
                v.reciprocal(s1, s1).then_inc(s_d, 1)
                dve.wait_ge(s_hw, c + 1)
                scan(ORDER * NC + c, c, b, thb[:, b, :], lambda t: sc[:, b, 3, t:t + 1])
                dve.wait_ge(s_d, d0 + 4)
                dve.wait_ge(s_nbfree, c + 1)
                v.tensor_tensor(rows3(sout[:, b, :]), rows3(run[:, b, :]), over_d(s1), ALU.mult
                                ).then_inc(s_nb, 1)
                v.tensor_copy(sc[:, b, 2, 0:1], s1[:, 0:1]).then_inc(s_d, 1)

            def source_h(c, b, n):
                h1_of(NC + c, b)

            def source_step(c, b, n):
                if not (isinstance(c, int) and c == 0):
                    scores(c - 1, 1 - b, n + b - 1)
                source_x1(c + 1, 1 - b, n + b)
                if not (isinstance(c, int) and c == 0):
                    sums(c - 1, 1 - b, n + b - 1)
                source_h(c + 1, 1 - b, n)
                add_attributes(c, b, n)

            one(0, source_x1)
            one(0, source_h)
            one(0, source_step)
            steps(dve, 1, NC - 1, source_step)
            one(NC - 2, scores)
            one(NC - 2, sums)
            one(NC - 1, add_attributes)
            one(NC - 1, scores)
            one(NC - 1, sums)

            fin = [0]

            def fin_step(i_):
                i_.then_inc(s_fin, 1)
                fin[0] += 1
                dve.wait_ge(s_fin, fin[0])

            m_first, d_first, m_carry, neg_m, e_first, d_all = (fz[:, q:q + 1] for q in range(6))
            dve.wait_ge(s_scan, (ORDER + 1) * NC * CHAIN)
            dve.wait_ge(s_d, 12 * NC)
            fin_step(v.tensor_scalar(diag[:], ident[:], m_all[:, NT:NT + 1], None, ALU.mult))
            assert fin[0] == F_DIAG
            fin_step(v.tensor_tensor(tmp[:], m_all[:, 1:NT + 1], last_first[:], ALU.mult))
            fin_step(v.tensor_reduce(m_first, tmp[:], AX.X, ALU.add))
            fin_step(v.tensor_tensor(tmp[:], den_all[:, 1:NT + 1], last_first[:], ALU.mult))
            fin_step(v.tensor_reduce(d_first, tmp[:], AX.X, ALU.add))
            fin_step(v.tensor_copy(nd[:, 0:D], run[:, 1, CW - D:CW]))
            fin_step(v.tensor_copy(nd[:, D:D + 1], den_all[:, NT:NT + 1]))
            fin_step(v.tensor_scalar(masked, carry_to[:], -1.0, BIG, ALU.add, ALU.mult))
            dve.wait_ge(s_finm, 1)
            fin_step(v.tensor_tensor(wts, psC[:, 0:P], carry_to[:], ALU.mult))
            fin_step(v.tensor_tensor(masked, masked, wts, ALU.add))
            fin_step(v.tensor_reduce(m_carry, masked, AX.X, ALU.max))
            fin_step(v.tensor_tensor(m_carry, m_carry, m_first, ALU.max))
            fin_step(v.tensor_scalar(neg_m, m_carry, -1.0, None, ALU.mult))
            assert fin[0] == F_MAX
            dve.wait_ge(s_finm, 2)
            fin_step(v.tensor_copy(wtsT, psC[:, P:2 * P]))
            assert fin[0] == F_WTS
            dve.wait_ge(s_fina, 2)
            fin_step(v.tensor_tensor(d_first, d_first, e_first, ALU.mult))
            dve.wait_ge(s_finm, 3)
            fin_step(v.tensor_tensor(d_all, psC[:, 2 * P + D:2 * P + D + 1], d_first, ALU.add))
            fin_step(v.tensor_scalar(d_all, d_all, 1e-9, None, ALU.add))
            fin_step(v.reciprocal(d_all, d_all))
            fin_step(v.scalar_tensor_tensor(out=fseg[:], in0=fseg[:], scalar=e_first,
                                            in1=psC[:, 2 * P:2 * P + D], op0=ALU.mult, op1=ALU.add))
            fin_step(v.tensor_scalar(yfix[:, D:PAIR], fseg[:], d_all, None, ALU.mult))
            assert fin[0] == N_FIN

            def node_x1(c, b, n):
                dve.wait_ge(s_nl[b], 16 * (NC // 2 + n + 1))
                dve.wait_ge(s_got[b], 16 * T * (got8 + n + 1))
                x1_of(2 * NC + c, b, xzb[:, b, :, D:PAIR], xzb[:, b, :, 0:D], gat[:, b, :, 0:D])

            def node_h(c, b, n):
                h1_of(2 * NC + c, b)
                dve.wait_ge(s_h, 3 * NC + c + 1)
                v.tensor_tensor(spb[:, b, :, 0:D], rows3(hbuf[:, b, :]), gat[:, b, :, D:PAIR],
                                ALU.add).then_inc(s_sp, 1)
                v.tensor_tensor(spb[:, b, :, D:PAIR], rows3(hbuf[:, b, :]), gat[:, b, :, D:PAIR],
                                ALU.mult).then_inc(s_sp, 1)

            def result(c, b, n):
                dve.wait_ge(s_slope, c + 1)
                v.tensor_tensor(ob[:, b, :], psD[:, 0:CW], ob[:, b, :], ALU.max).then_inc(s_linu, 1)
                dve.wait_ge(s_linu, 3 * NC + c + 2)
                dve.wait_ge(s_ofree, c + 1)
                v.tensor_tensor(sout[:, b, :], ob[:, b, :], xbuf[:, b, :], ALU.add).then_inc(s_o, 1)

            def update_step(c, b, n):
                if not (isinstance(c, int) and c == 0):
                    result(c - 1, 1 - b, n)
                node_x1(c + 1, 1 - b, n + b)
                node_h(c, b, n)

            dve.wait_ge(s_nbfree, NC + 2)
            one(0, node_x1)
            one(0, update_step)
            steps(dve, 1, NC - 1, update_step)
            one(NC - 2, result)
            one(NC - 1, node_h)
            one(NC - 1, result)


_INS = ['x', 'src', 'dst', 'dst_next', 'edge_weight', 'edge_attr_64', 'L0_gnn_W', 'L0_gnn_bias', 'L1_gnn_W1_w',
        'L1_gnn_W1_b', 'L1_gnn_W2_w', 'L1_gnn_W2_b', 'L1_gnn_Watt_w', 'L1_gnn_Watt_b']


def kernel(**inputs):
    import numpy as _np
    import concourse.bacc as _bacc
    from concourse import mybir as _mybir
    from concourse.bass_utils import run_bass_kernel_spmd as _run

    def padded(a, value):
        a = _np.asarray(a)
        o = _np.full((ROWS,) + a.shape[1:], value, a.dtype)
        o[:len(a)] = a
        return o

    given = dict(inputs)
    for name in ('x', 'edge_attr_64', 'edge_weight'):
        given[name] = padded(inputs[name], 0)
    for name in ('src', 'dst'):
        given[name] = padded(inputs[name], N_NODES)
    after = _np.full(ROWS, N_NODES + 1, given['dst'].dtype)
    after[:-1] = given['dst'][1:]
    given['dst_next'] = after
    nc = _bacc.Bacc("TRN2", target_bir_lowering=False, num_devices=1)
    arrays, args = {}, []
    for name in _INS:
        a = _np.ascontiguousarray(given[name])
        arrays[f"in_{name}"] = a
        args.append(nc.dram_tensor(f"in_{name}", a.shape, _mybir.dt.from_np(a.dtype), kind="ExternalInput").ap())
    args.append(nc.dram_tensor("out_0", (ROWS, D), F32, kind="ExternalOutput").ap())
    build(nc, *args, stop=STOP)
    r = _run(nc, [arrays], core_ids=[0])
    return r.results[0]["out_0"][:N_NODES]
```

```python
from contextlib import ExitStack

import concourse.bass as bass
from concourse import mybir
from concourse.alu_op_type import AluOpType as ALU

ACT = mybir.ActivationFunctionType
AX = mybir.AxisListType
F32 = mybir.dt.float32
F16 = mybir.dt.float16
I32 = mybir.dt.int32

P = 128
D = 64
N_NODES = 50000
NT = 392
ROWS = P * NT
T = 14
NC = NT // T
PAIR = 2 * D
PAIRS = T // 2
CW = T * D
FIX = ROWS
EMPTY = ROWS + P
TROWS = ROWS + 2 * P
ROW = 3 * D + 1
RH, RX, RZ, RREP = 0, D, 2 * D, 3 * D
EPS = 1e-5
ROUND = 1.5 * 2.0 ** 23
BIG = 1e30
ORDER = 5
HR = 8
KB = 512
STOP = None
F_DIAG, F_MAX, F_WTS, N_FIN = 1, 14, 15, 22
N_IOTA, N_CUM, N_REP, N_DIAG1, N_DIAG2, N_PREP = 1, 8, 29, 44, 45, 69
T1 = T + 1


def steps(eng, lo, hi, step):
    with eng.Fori(0, (hi - lo) // 2) as i:
        for j in range(2):
            step(2 * i + (lo + j), (lo + j) % 2, i + (lo + j) // 2)


def one(c, step):
    step(c, c % 2, c // 2)


def build(nc, x, src, dst, dst_next, edge_w, edge_attr, W, b0, W1, b1, W2, b2, Wa, ba, out, stop=None):
    with ExitStack() as ctx:
        def sb(name, shape, dt=F32):
            return ctx.enter_context(nc.sbuf_tensor(name, shape, dt))

        def ps(name, shape, dt=F32):
            return ctx.enter_context(nc.psum_tensor(name, shape, dt))

        def sem(name):
            return ctx.enter_context(nc.semaphore(name))

        def dram(name, shape, dt=F32):
            return nc.dram_tensor(name, shape, dt, kind="Internal").ap()

        node_rows = dram("node_rows", (ROWS, ROW))
        tables = [dram(f"segsum{k}", (TROWS, D)) for k in range(1, ORDER)]
        yn_table = dram("yn_table", (TROWS, 2 * D))
        y_table = dram("y_table", (TROWS, D))
        src_xz = dram("src_xz", (ROWS, 2 * D))
        htd_table = dram("htd_table", (ROWS, D))

        def by_part(t):
            return t[0:ROWS, :].rearrange("(p t) d -> p t d", t=NT)

        x_pt, er_pt, out_pt = by_part(x), by_part(edge_attr), by_part(out)
        node_pt, xz_pt, htd_pt, yn_pt = by_part(node_rows), by_part(src_xz), by_part(htd_table), by_part(yn_table)
        y_pt = by_part(y_table)
        tab_pt = [by_part(t) for t in tables]

        src_i = sb("src_i", [P, NT], I32)
        dst_i = sb("dst_i", [P, NT], I32)
        dstf = sb("dstf", [P, NT])
        w1 = sb("w1", [P, NT])
        w2 = sb("w2", [P, NT])
        same = sb("same", [P, NC, T1])
        first = sb("first", [P, NT])
        last = sb("last", [P, NT])
        notlast = sb("notlast", [P, NT])
        last_first = sb("last_first", [P, NT])
        tmp = sb("tmp", [P, NT])
        hi = sb("hi", [P, NT])
        lo = sb("lo", [P, NT])
        incl = sb("incl", [P, NT])
        rep_i = sb("rep_i", [P, NT], I32)
        reps_i = sb("reps_i", [P, NT], I32)
        ident = sb("ident", [P, P])
        ones = sb("ones", [P, P])
        below = sb("below", [P, P])
        above = sb("above", [P, P])
        center = sb("center", [P, P])
        pidx_i = sb("pidx_i", [P, 1], I32)
        pidx = sb("pidx", [P, 1])
        first_row = sb("first_row", [P, 1], I32)
        zrow = sb("zrow", [P, PAIR])
        wmix = sb("wmix", [P, 6, PAIR])
        watt = sb("watt", [P, PAIR])
        w12 = sb("w12", [P, D])
        empty = sb("empty", [P, PAIR])
        brow = sb("brow", [1, 4, D])
        eps_c = sb("eps_c", [P, 1])
        diag = sb("diag", [P, P])
        carry_in = sb("carry_in", [P, P])
        carry_to = sb("carry_to", [P, P])
        v_from = sb("v_from", [P, P])
        ends_in = sb("ends_in", [P, 1])
        small = sb("small", [P, 8])
        idx = sb("idx", [P, 2, T], I32)
        gat = sb("gat", [P, 2, T, ROW])
        xbuf = sb("xbuf", [P, 2, CW])
        keep = sb("keep", [P, 2, D * T1])
        hbuf = keep[:, :, 0:CW]
        xT = sb("xT", [P, CW])
        hT = sb("hT", [P, CW])
        sq = sb("sq", [P, 2, CW])
        run = sb("run", [P, 2, D * T1])
        sout = sb("sout", [P, 2, CW])
        stat = sb("stat", [P, 2, 5, T])
        fseg = sb("fseg", [P, D])
        fpart = sb("fpart", [P, D])
        fixp = sb("fixp", [P, ORDER + 1, PAIR])
        fixT = sb("fixT", [P, P])
        yfix = sb("yfix", [P, PAIR])
        yall = sb("yall", [P, NT * D])

        early = [NT * D]

        def early_room(n):
            early[0] -= n
            return yall[:, early[0]:early[0] + n]

        iota_i = early_room(NT).bitcast(I32)
        iota_h = early_room(NT // 2).bitcast(F16)
        zeros_h = early_room(P // 2).bitcast(F16)
        onehot = early_room(HR * (P + NT) // 2).bitcast(F16).rearrange("p (r c) -> p r c", r=HR)
        wraw = early_room(6 * PAIR).rearrange("p (k d) -> p k d", k=6)
        wa_raw = early_room(PAIR)
        w12_raw = early_room(2 * D)[0:D, :]
        XC = early[0] // CW
        vinit = sb("vinit", [P, D])
        cfill = sb("cfill", [P, D])
        spare = [0]

        def room(n):
            spare[0] += n
            return yall[:, spare[0] - n:spare[0]]

        xzb = room(2 * T * PAIR).rearrange("p (b t d) -> p b t d", b=2, t=T)
        erb = room(2 * CW).rearrange("p (b c) -> p b c", b=2)
        htb = room(2 * CW).rearrange("p (b c) -> p b c", b=2)
        ub = room(2 * CW).rearrange("p (b c) -> p b c", b=2)
        thb = room(2 * CW).rearrange("p (b c) -> p b c", b=2)
        ob = room(2 * CW).rearrange("p (b c) -> p b c", b=2)
        spb = room(2 * T * PAIR).rearrange("p (b t d) -> p b t d", b=2, t=T)
        m_all = room(NT + 1)
        den_all = room(NT + 1)
        restart = room(NT)
        ab = room(2 * 2 * T).rearrange("p (b k t) -> p b k t", b=2, k=2)
        sc = room(2 * 4 * T).rearrange("p (b k t) -> p b k t", b=2, k=4)
        decay = room(2 * T1).rearrange("p (b t) -> p b t", b=2)
        dx = room(2 * T1 * D).rearrange("p (b c) -> p b c", b=2)
        masked = room(P)
        wts = room(P)
        wtsT = room(P)
        nd = room(D + 1)
        first_yn = room(PAIR)
        fz = room(16)

        psA = ps("psA", [P, 2 * KB])
        psB = ps("psB", [P, 2 * KB])
        psC = ps("psC", [P, 2 * KB])
        psD = ps("psD", [P, 2 * KB])

        def rows3(ap):
            return ap.rearrange("p (t d) -> p t d", d=D)

        def scanned(b, lo_=1, hi_=T1):
            return run[:, b, :].rearrange("p (d t) -> p t d", t=T1)[:, lo_:hi_, :]

        def last_scanned(b):
            return run[:, b, :].rearrange("p (d t) -> p d t", t=T1)[:, :, T]

        def expand(rows, b, out_):
            return nc.scalar.copy(out_.rearrange("p (d t) -> p d t", t=T1), rows.unsqueeze(1).to_broadcast([P, D, T1]))

        def over_d(ap):
            return ap.unsqueeze(2).to_broadcast([P, T, D])

        def stored_before(eng, sem2, c, b, n, base=0):
            eng.wait_ge(sem2[b], 16 * (base + n + 1))

        def cols(c):
            return bass.ds(c * T, T)

        s_turn = sem("sp_turns")
        s_const = sem("constants_set")
        s_load = sem("inputs_loaded")
        s_wload = sem("weights_loaded")
        s_prep = sem("prep_steps")
        s_pe0 = sem("prep_products")
        s_hot = sem("onehot_made")
        s_hot_free = sem("onehot_slot_free")
        s_count = sem("counts_made")
        s_xin = sem("x_loaded")
        s_xlate = sem("x_last_chunks_loaded")
        s_xcopy = sem("x_in_node_rows")
        s_xc = sem("x_centered")
        s_sq = sem("squares_made")
        s_mean = sem("means_made")
        s_var = sem("variances_made")
        s_rs = sem("inverse_deviations_made")
        s_sd = sem("deviations_made")
        s_h = sem("h_made")
        s_rowx = sem("row_rep_set")
        s_row = [sem(f"z_rep_chunk_stored{b}") for b in range(2)]
        s_hst = [sem(f"h_chunk_stored{b}") for b in range(2)]
        s_node = sem("node_rows_ready")
        s_btr = sem("h_transposed")
        s_bcp = sem("h_transpose_copied")
        s_lin = sem("linear_made")
        s_linu = sem("linear_used")
        s_started = sem("gathers_started")
        s_got = [sem(f"gathered{b}") for b in range(2)]
        s_gread = sem("gather_read")
        s_scan = sem("scan_steps")
        s_keep = sem("keep_expanded")
        s_relay = sem("sums_by_row_made")
        s_fsum = sem("first_segment_sums")
        s_sub = sem("older_product_subtracted")
        s_prev = [sem(f"older_product_loaded{b}") for b in range(2)]
        s_str = sem("product_transposed")
        s_scp = sem("product_transpose_copied")
        s_ymm = sem("y_part_made")
        s_yadd = sem("y_part_added")
        s_tst = [sem(f"table_chunk_stored{b}") for b in range(2)]
        s_xz = [sem(f"xz_chunk_stored{b}") for b in range(2)]
        s_fixm = sem("fix_products")
        s_fixv = sem("fix_steps")
        s_fixa = sem("fix_transpose_copied")
        s_fixst = sem("fix_rows_stored")
        s_pass = sem("table_ready")
        s_zero = sem("zero_rows_stored")
        s_yst = sem("y_chunk_stored")
        s_out = [sem(f"out_stored{b}") for b in range(2)]
        s_repi = sem("source_reps_ready")
        s_idx = sem("indices_staged")
        s_fseg = sem("first_sum_steps")
        s_vin = sem("fill_start_made")
        s_vins = sem("fill_start_steps")
        s_ysel = sem("segment_ends_selected")
        s_fill = sem("fill_steps")
        s_u = sem("l0_sum_made")
        s_x1 = sem("x1_made")
        s_ftr = sem("x1_transposed")
        s_fcp = sem("x1_transpose_copied")
        s_cen = sem("x1_centered")
        s_ht = [sem(f"target_rows_stored{b}") for b in range(2)]
        s_ld = [sem(f"edge_rows_loaded{b}") for b in range(2)]
        s_lh = [sem(f"target_rows_loaded{b}") for b in range(2)]
        s_th = sem("tanh_made")
        s_q = sem("score_terms_made")
        s_d = sem("score_steps")
        s_exp = sem("exponentials_made")
        s_hw = sem("weighted_h_made")
        s_nb = sem("neighbour_sum_made")
        s_nbst = [sem(f"neighbour_sum_stored{b}") for b in range(2)]
        s_fin = sem("attention_fix_steps")
        s_finm = sem("attention_fix_products")
        s_fina = sem("attention_fix_exponentials")
        s_fgot = sem("first_sums_gathered")
        s_yn = sem("update_table_ready")
        s_nl = [sem(f"node_xz_loaded{b}") for b in range(2)]
        s_sp = sem("sum_and_product_made")
        s_utr = sem("update_transposed")
        s_ucp = sem("update_transpose_copied")
        s_slope = sem("leaky_slope_made")
        s_o = sem("output_made")

        N_CONST, N_LOAD = 12, 4
        N_WLOAD = 2 * 6 + 2 + 2 + 4
        inv = 1.0 / NT
        block = ctx.enter_context(nc.Block())

        @block.sync
        def _(sp):
            sp.dma_start(src_i[:], src.rearrange("(p t) -> p t", t=NT)).then_inc(s_load, 16)
            sp.dma_start(dst_i[:], dst.rearrange("(p t) -> p t", t=NT)).then_inc(s_load, 16)
            sp.dma_start(rep_i[:], dst_next.rearrange("(p t) -> p t", t=NT)).then_inc(s_load, 16)
            sp.dma_start(w1[:], edge_w.rearrange("(p t) -> p t", t=NT)).then_inc(s_load, 16)
            sp.wait_ge(s_const, N_CONST)
            for k in range(6):
                for h in range(2):
                    sp.dma_start(wraw[h * D:(h + 1) * D, k, h * D:(h + 1) * D], W[k]).then_inc(s_wload, 16)
            for h in range(2):
                sp.dma_start(wa_raw[h * D:(h + 1) * D, h * D:(h + 1) * D], Wa).then_inc(s_wload, 16)
            sp.dma_start(w12_raw[:, 0:D], W1).then_inc(s_wload, 16)
            sp.dma_start(w12_raw[:, D:2 * D], W2).then_inc(s_wload, 16)
            for j, b in enumerate((b0, ba, b1, b2)):
                sp.dma_start(brow[:, j, :], b.rearrange("(a d) -> a d", a=1)).then_inc(s_wload, 16)
            sp.dma_start(rows3(yall[:, 0:XC * CW]), x_pt[:, 0:XC * T, :]).then_inc(s_xin, 16)
            sp.dma_start(node_rows[:, RX:RX + D], x).then_inc(s_xcopy, 16)
            for sem2 in (s_row, s_hst, s_tst, s_xz, s_ht, s_nbst, s_out):
                for b in range(2):
                    sp.sem_inc(sem2[b], 16)
            for t in tables:
                sp.dma_start(t[EMPTY:EMPTY + P, :], zrow[:, 0:D]).then_inc(s_zero, 16)
            sp.wait_ge(s_prep, N_PREP)
            sp.dma_start(rows3(yall[:, XC * CW:]), x_pt[:, XC * T:, :]).then_inc(s_xlate, 16)
            sp.dma_start(y_table[EMPTY:EMPTY + P, :], empty[:, 0:D]).then_inc(s_zero, 16)
            sp.dma_start(yn_table[EMPTY:EMPTY + P, :], empty[:]).then_inc(s_zero, 16)

            def store_h(c, b, n):
                sp.wait_ge(s_h, c + 1)
                sp.sem_inc(s_turn)
                sp.dma_start(node_pt[:, cols(c), RH:RH + D], rows3(hbuf[:, b, :])).then_inc(s_hst[b], 16)

            def store_z_rep(c, b, n):
                sp.wait_ge(s_rowx, c + 1)
                sp.sem_inc(s_turn)
                sp.wait_ge(s_linu, c + 2)
                sp.dma_start(node_pt[:, cols(c), RZ:ROW], gat[:, b, :, RZ:ROW]).then_inc(s_row[b], 16)

            def row_step(c, b, n):
                store_h(c, b, n)
                store_z_rep(c - 2, b, n - 1)

            one(0, store_h)
            one(1, store_h)
            steps(sp, 2, NC, row_step)
            one(NC - 2, store_z_rep)
            one(NC - 1, store_z_rep)
            sp.wait_ge(s_xcopy, 16)
            for b in range(2):
                sp.wait_ge(s_hst[b], 16 * (NC // 2 + 1))
                sp.wait_ge(s_row[b], 16 * (NC // 2 + 1))
            sp.sem_inc(s_node)

            for k in range(1, ORDER + 1):
                g0 = (k - 1) * NC

                def load(c, b, n):
                    if k >= 3:
                        if not isinstance(c, int):
                            sp.wait_ge(s_sub, (k - 3) * NC + c - 1)
                            sp.sem_inc(s_turn)
                        elif k > 3:
                            sp.wait_ge(s_sub, (k - 3) * NC - 1 + c)
                            sp.sem_inc(s_turn)
                        sp.dma_start(rows3(xbuf[:, b, :]), tab_pt[k - 3][:, cols(c), :]).then_inc(s_prev[b], 16)

                def store(c, b, n):
                    if k < 3:
                        sp.wait_ge(s_relay, g0 + c + 1)
                        sp.sem_inc(s_turn)
                    elif k < ORDER:
                        sp.wait_ge(s_sub, (k - 3) * NC + c + 1)
                        sp.sem_inc(s_turn)
                    if k < ORDER:
                        sp.dma_start(tab_pt[k - 1][:, cols(c), :], rows3(sout[:, b, :])).then_inc(s_tst[b], 16)
                    if k == 1:
                        sp.dma_start(xz_pt[:, cols(c), :], gat[:, b, :, RX:RX + 2 * D]).then_inc(s_xz[b], 16)
                    if k == ORDER:
                        sp.wait_ge(s_yadd, g0 + c + 3)
                        sp.dma_start(yn_pt[:, cols(c), 0:D], rows3(yall[:, bass.ds(c * CW, CW)])).then_inc(s_yst, 16)
                        sp.dma_start(y_pt[:, cols(c), :], rows3(yall[:, bass.ds(c * CW, CW)])).then_inc(s_yst, 16)

                def step(c, b, n):
                    load(c + 2, b, n + 1)
                    store(c, b, n)

                one(0, load)
                one(1, load)
                steps(sp, 0, NC - 2, step)
                one(NC - 2, store)
                one(NC - 1, store)
                if k < ORDER:
                    sp.wait_ge(s_fixv, 3 * k - 1)
                    sp.dma_start(tables[k - 1][FIX:FIX + P, :], fixp[:, k, 0:D]).then_inc(s_fixst, 16)
                    sp.wait_ge(s_fixst, k * 16)
                    for b in range(2):
                        sp.wait_ge(s_tst[b], 16 * (k * (NC // 2) + 1))
                    sp.wait_ge(s_zero, 16 * (ORDER + 1))
                    sp.sem_inc(s_pass)
            sp.wait_ge(s_fixv, 3 * ORDER)
            sp.dma_start(yn_table[FIX:FIX + P, 0:D], yfix[:, 0:D]).then_inc(s_fixst, 16)
            sp.dma_start(y_table[FIX:FIX + P, :], yfix[:, 0:D]).then_inc(s_fixst, 16)
            sp.wait_ge(s_fixst, (ORDER + 1) * 16)
            sp.wait_ge(s_yst, NC * 32)
            sp.wait_ge(s_zero, 16 * (ORDER + 1))
            sp.sem_inc(s_pass)
            if stop == "y":
                for p in range(1):
                    sp.dma_start(out.rearrange("(p t) d -> p (t d)", t=NT), yall[:]).then_inc(s_out[0], 16)
                    sp.wait_ge(s_out[0], 16)
                return


            def store_target(c, b, n):
                sp.wait_ge(s_linu, NC + c + 2)
                sp.sem_inc(s_turn)
                sp.dma_start(htd_pt[:, cols((NC - 1) - c), :], rows3(run[:, b, 0:CW])).then_inc(s_ht[b], 16)

            steps(sp, 0, NC, store_target)
            for b in range(2):
                sp.wait_ge(s_ht[b], 16 * (NC // 2 + 1))

            def later(c):
                return not isinstance(c, int) or c >= 2

            def load_xz(c, b, n):
                if later(c):
                    sp.wait_ge(s_x1, NC + c - 1)
                    sp.sem_inc(s_turn)
                sp.dma_start(xzb[:, b], xz_pt[:, cols(c), :]).then_inc(s_nl[b], 16)

            def load_attributes(c, b, n):
                if later(c):
                    sp.wait_ge(s_linu, 2 * NC + c)
                    sp.sem_inc(s_turn)
                sp.dma_start(rows3(erb[:, b, :]), er_pt[:, cols(c), :]).then_inc(s_ld[b], 16)

            def load_targets(c, b, n):
                if later(c):
                    sp.wait_ge(s_q, c - 1)
                    sp.sem_inc(s_turn)
                sp.dma_start(rows3(htb[:, b, :]), htd_pt[:, cols(c), :]).then_inc(s_lh[b], 16)

            def store_neighbours(c, b, n):
                sp.wait_ge(s_nb, c + 1)
                sp.sem_inc(s_turn)
                sp.dma_start(yn_pt[:, cols(c), D:PAIR], rows3(sout[:, b, :])).then_inc(s_nbst[b], 16)

            def source_step(c, b, n):
                if not isinstance(c, int) or c + 3 < NC:
                    load_xz(c + 3, 1 - b, n + 1 + b)
                if later(c):
                    store_neighbours(c - 2, b, n - 1)
                if not isinstance(c, int) or c + 1 < NC:
                    load_targets(c + 1, 1 - b, n + b)
                if not isinstance(c, int) or c + 2 < NC:
                    load_attributes(c + 2, b, n + 1)

            sp.wait_ge(s_vins, NC + 2)
            for load in (load_xz, load_attributes):
                one(0, load)
                one(1, load)
            one(0, load_targets)
            one(2, load_xz)
            for c in range(3):
                one(c, source_step)
            steps(sp, 3, NC - 3, source_step)
            for c in range(NC - 3, NC + 2):
                one(c, source_step)
            sp.wait_ge(s_fin, N_FIN)
            sp.dma_start(yn_table[FIX:FIX + P, D:PAIR], yfix[:, D:PAIR]).then_inc(s_fixst, 16)

            def load_nodes(c, b, n):
                if not isinstance(c, int):
                    sp.wait_ge(s_x1, 2 * NC + c - 1)
                    sp.sem_inc(s_turn)
                sp.dma_start(xzb[:, b], node_pt[:, cols(c), RX:RX + 2 * D]).then_inc(s_nl[b], 16)

            def store_out(c, b, n):
                sp.wait_ge(s_o, c + 1)
                sp.sem_inc(s_turn)
                sp.dma_start(out_pt[:, cols(c), :], rows3(sout[:, b, :])).then_inc(s_out[b], 16)

            def update_io(c, b, n):
                load_nodes(c + 2, b, n + 1)
                store_out(c, b, n)

            one(0, load_nodes)
            one(1, load_nodes)
            sp.wait_ge(s_fixst, (ORDER + 2) * 16)
            sp.sem_inc(s_yn)
            steps(sp, 0, NC - 2, update_io)
            one(NC - 2, store_out)
            one(NC - 1, store_out)
            for b in range(2):
                sp.wait_ge(s_out[b], 16 * (NC // 2 + 1))

        @block.gpsimd
        def _(pool):
            g = nc.gpsimd
            g.memset(ident[:], 0.0).then_inc(s_const, 1)
            g.memset(ones[:], 1.0).then_inc(s_const, 1)
            g.memset(wraw, 0.0).then_inc(s_const, 1)
            g.memset(wa_raw, 0.0).then_inc(s_const, 1)
            g.memset(zrow[:], 0.0).then_inc(s_const, 1)
            g.memset(zeros_h, 0.0).then_inc(s_const, 1)
            g.memset(eps_c[:], EPS).then_inc(s_const, 1)
            g.iota(iota_i, [[1, NT]], base=0, channel_multiplier=0).then_inc(s_const, 1)
            g.iota(pidx_i[:], [[0, 1]], base=0, channel_multiplier=1).then_inc(s_const, 1)
            pool.wait_ge(s_const, 9)
            g.affine_select(out=ident[:], in_=ident[:], compare_op=ALU.not_equal, fill=1.0, base=0,
                            pattern=[[-1, P]], channel_multiplier=1).then_inc(s_const, 1)
            g.affine_select(out=below[:], in_=ones[:], compare_op=ALU.is_gt, fill=0.0, base=0,
                            pattern=[[1, P]], channel_multiplier=-1).then_inc(s_const, 1)
            g.affine_select(out=above[:], in_=ones[:], compare_op=ALU.is_gt, fill=0.0, base=0,
                            pattern=[[-1, P]], channel_multiplier=1).then_inc(s_const, 1)

            pool.wait_ge(s_prep, N_REP)

            def row_rep(c, b, n):
                stored_before(pool, s_row, c, b, n)
                pool.sem_inc(s_started)
                g.tensor_copy(gat[:, b, :, RREP], lo[:, cols(c)]).then_inc(s_rowx, 1)

            steps(pool, 0, NC, row_rep)
            pool.wait_ge(s_node, 1)

            def gathers(g0, width, table, indices, freed, at=lambda c: c):
                def chunk(c, b, n):
                    freed(c, b, n)
                    pool.sem_inc(s_started)
                    g.tensor_copy(idx[:, b, :], indices[:, cols(at(c))]).then_inc(s_idx, 1)
                    pool.wait_ge(s_idx, g0 + c + 1)
                    pool.sem_inc(s_started)
                    for t in range(T):
                        g.indirect_dma_start(gat[:, b, t, 0:width], None, table,
                                             bass.IndirectOffsetOnAxis(ap=idx[:, b, t:t + 1], axis=0)
                                             ).then_inc(s_got[b], 16)
                one(0, chunk)
                one(1, chunk)
                steps(pool, 2, NC, chunk)

            def freed1(c, b, n):
                if not isinstance(c, int):
                    pool.wait_ge(s_gread, c - 1)
                    stored_before(pool, s_xz, c, b, n)

            gathers(0, ROW, node_rows, src_i, freed1)
            for b in range(2):
                pool.wait_ge(s_xz[b], 16 * (NC // 2 + 1))
            for k in range(2, ORDER + 1):
                pool.wait_ge(s_pass, k - 1)
                if k == 2:
                    pool.wait_ge(s_repi, 1)

                def freed(c, b, n):
                    pool.wait_ge(s_gread, (k - 1) * NC + c - 1)

                gathers((k - 1) * NC, D, tables[k - 2], reps_i, freed)
            if stop == "y":
                return

            def freed_targets(c, b, n):
                if isinstance(c, int):
                    pool.wait_ge(s_gread, ORDER * NC + c - 1)
                else:
                    pool.wait_ge(s_x1, c - 1)

            gathers(ORDER * NC, ROW, node_rows, dst_i, freed_targets, at=lambda c: (NC - 1) - c)

            def freed_sources(c, b, n):
                pool.wait_ge(s_x1, NC + c - 1)

            pool.wait_ge(s_pass, ORDER)
            gathers((ORDER + 1) * NC, D, y_table, reps_i, freed_sources)

            for b in range(2):
                pool.wait_ge(s_nbst[b], 16 * (NC // 2 + 1))
            g.indirect_dma_start(first_yn, None, yn_table[0:ROWS, :],
                                 bass.IndirectOffsetOnAxis(ap=first_row[:], axis=0)).then_inc(s_fgot, 16)

            def freed_nodes(c, b, n):
                if isinstance(c, int):
                    pool.wait_ge(s_x1, 2 * NC + c - 1)
                else:
                    pool.wait_ge(s_sp, 2 * (c - 1))

            pool.wait_ge(s_yn, 1)
            gathers((ORDER + 2) * NC, PAIR, yn_table, rep_i, freed_nodes)

        @block.scalar
        def _(act):
            a = nc.scalar

            def square(c, b, n):
                act.wait_ge(s_xc, c + 1)
                a.activation(sq[:, b, :], yall[:, bass.ds(c * CW, CW)], ACT.Square).then_inc(s_sq, 1)

            def node_deviation(c, b, n):
                act.wait_ge(s_var, c + 1)
                a.activation(stat[:, b, 3, :], stat[:, b, 2, :], ACT.Sqrt, bias=eps_c[:], scale=1.0 / D
                             ).then_inc(s_sd, 1)

            def z_out(c, b, n):
                act.wait_ge(s_lin, c + 1)
                stored_before(act, s_row, c, b, n)
                a.copy(gat[:, b, :, RZ:RZ + D], rows3((psD, psB)[b][:, 0:CW])).then_inc(s_linu, 1)

            def copy_node_h(c, b, n):
                act.wait_ge(s_btr, c + 1)
                a.copy((hT, xT)[b][:], (psC, psA)[b][:, 0:CW]).then_inc(s_bcp, 1)

            def node_step(c, b, n):
                square(c + 1, 1 - b, n + b)
                node_deviation(c, b, n)
                if not (isinstance(c, int) and c < 2):
                    z_out(c - 2, b, n - 1)
                copy_node_h(c, b, n)

            act.wait_ge(s_const, N_CONST)
            act.sem_inc(s_linu)
            one(0, square)
            for c in range(3):
                one(c, node_step)
            steps(act, 3, NC - 1, node_step)
            one(NC - 1, node_deviation)
            one(NC - 3, z_out)
            one(NC - 1, copy_node_h)
            one(NC - 2, z_out)
            one(NC - 1, z_out)

            for k in range(1, ORDER + 1):
                g0 = (k - 1) * NC

                def keep_of(c, b, n):
                    if not (k == 1 and isinstance(c, int)):
                        act.wait_ge(s_scan, 2 * (g0 + c - 1))
                    expand(same[:, bass.ds(c, 1), :].rearrange("p a t -> p (a t)"), b, keep[:, b, :]
                           ).then_inc(s_keep, 1)

                def copy(c, b, n):
                    if k < 3:
                        act.wait_ge(s_scan, 2 * (g0 + c + 1))
                        stored_before(act, s_tst, c, b, n, (k - 1) * (NC // 2))
                        a.copy(rows3(sout[:, b, :]), scanned(b)).then_inc(s_relay, 1)
                    act.wait_ge(s_str, g0 + c + 1)
                    a.copy(xT[:], psA[:, 0:CW]).then_inc(s_scp, 1)

                def step(c, b, n):
                    copy(c, b, n)
                    keep_of(c + 2, b, n + 1)

                if k == 1:
                    act.wait_ge(s_node, 1)
                one(0, keep_of)
                one(1, keep_of)
                steps(act, 0, NC - 2, step)
                one(NC - 2, copy)
                one(NC - 1, copy)
                act.wait_ge(s_fixm, 3 * k - 1)
                a.copy(fixT[:], psC[:, P:2 * P]).then_inc(s_fixa, 1)
            if stop == "y":
                return

            def copy_x1(seq, b):
                act.wait_ge(s_ftr, seq + 1)
                a.copy(xT[:], psA[:, 0:CW]).then_inc(s_fcp, 1)

            def squares(seq, b):
                act.wait_ge(s_cen, seq + 1)
                a.activation(sq[:, b, :], psB[:, 0:CW], ACT.Square).then_inc(s_sq, 1)

            def deviations(seq, b):
                act.wait_ge(s_var, NC + seq + 1)
                a.activation(stat[:, b, 3, :], stat[:, b, 2, :], ACT.Sqrt, bias=eps_c[:], scale=1.0 / D
                             ).then_inc(s_sd, 1)

            def copy_h(seq, b):
                act.wait_ge(s_btr, NC + seq + 1)
                a.copy(hT[:], psC[:, 0:CW]).then_inc(s_bcp, 1)

            def target_tail(c, b, n):
                deviations(c, b)

            def target_out(c, b, n):
                copy_h(c, b)
                act.wait_ge(s_lin, NC + c + 1)
                stored_before(act, s_ht, c, b, n)
                a.copy(run[:, b, 0:CW], psD[:, 0:CW]).then_inc(s_linu, 1)

            def target_step(c, b, n):
                copy_x1(c + 1, 1 - b)
                deviations(c, b)
                squares(c + 1, 1 - b)
                target_out(c, b, n)

            copy_x1(0, 0)
            squares(0, 0)
            one(0, target_step)
            steps(act, 1, NC - 1, target_step)
            deviations(NC - 1, 1)
            one(NC - 1, target_out)

            def source_norm(c, b):
                squares(NC + c, b)
                deviations(NC + c, b)
                copy_h(NC + c, b)

            def tanh(c, b):
                act.wait_ge(s_linu, 2 * NC + c + 2)
                a.activation(thb[:, b, :], ub[:, b, :], ACT.Tanh).then_inc(s_th, 1)

            def exponentials(c, b):
                act.wait_ge(s_d, 11 * c + 7)
                a.activation(ab[:, b], ab[:, b], ACT.Exp).then_inc(s_exp, 1)
                act.wait_ge(s_d, 11 * c + 8)
                expand(decay[:, b, :], b, dx[:, b, :]).then_inc(s_keep, 1)

            def neighbours(c, b, n):
                act.wait_ge(s_d, 11 * c + 11)
                act.wait_ge(s_scan, 2 * (ORDER * NC + c + 1))
                stored_before(act, s_nbst, c, b, n)
                for t in range(T):
                    i_ = a.mul(sout[:, b, t * D:(t + 1) * D], scanned(b)[:, t, :], sc[:, b, 2, t:t + 1])
                i_.then_inc(s_nb, 1)

            def source_step(c, b, n):
                copy_x1(NC + c + 1, 1 - b)
                if not (isinstance(c, int) and c == 0):
                    exponentials(c - 1, 1 - b)
                source_norm(c + 1, 1 - b)
                tanh(c, b)
                if not (isinstance(c, int) and c == 0):
                    neighbours(c - 1, 1 - b, n + b - 1)

            copy_x1(NC, 0)
            source_norm(0, 0)
            one(0, source_step)
            steps(act, 1, NC - 1, source_step)
            exponentials(NC - 2, 0)
            tanh(NC - 1, 1)
            one(NC - 2, neighbours)
            exponentials(NC - 1, 1)
            one(NC - 1, neighbours)
            act.wait_ge(s_fin, F_MAX)
            a.activation(wts, masked, ACT.Exp, bias=fz[:, 3:4]).then_inc(s_fina, 1)
            a.activation(fz[:, 4:5], fz[:, 0:1], ACT.Exp, bias=fz[:, 3:4]).then_inc(s_fina, 1)

            def update_norm(c, b, n):
                act.wait_ge(s_xc, NC + c + 1)
                a.activation(sq[:, b, :], hbuf[:, b, :], ACT.Square).then_inc(s_sq, 1)
                deviations(2 * NC + c, b)

            def update_copies(c, b, n):
                for q in range(2):
                    act.wait_ge(s_utr, 2 * c + q + 1)
                    a.copy((hT, xT)[q][:], (psC, psA)[q][:, 0:CW]).then_inc(s_ucp, 1)

            def slope(c, b, n):
                act.wait_ge(s_lin, 3 * NC + c + 1)
                a.mul(ob[:, b, :], psD[:, 0:CW], 0.2).then_inc(s_slope, 1)

            def update_step(c, b, n):
                update_copies(c, b, n)
                update_norm(c + 1, 1 - b, n + b)
                slope(c, b, n)

            one(0, update_norm)
            one(0, update_step)
            steps(act, 1, NC - 1, update_step)
            one(NC - 1, update_copies)
            one(NC - 1, slope)

        @block.tensor
        def _(pe):
            m = nc.tensor
            pe.wait_ge(s_const, N_CONST)
            pe.wait_ge(s_prep, N_IOTA)
            m.matmul(psA[:, 0:NT], zeros_h, iota_h, start=True, stop=False)
            with pe.Fori(0, NT // HR) as i:
                for j in range(HR):
                    pe.wait_ge(s_hot, 2 * HR * i + 2 * (j + 1))
                    m.matmul(psA[:, 0:NT], onehot[:, j, 0:P], onehot[:, j, P:], start=False, stop=False
                             ).then_inc(s_hot_free, 1)
            m.matmul(psA[:, 0:NT], zeros_h, iota_h, start=False, stop=True).then_inc(s_count, 1)
            pe.wait_ge(s_prep, N_CUM)
            m.matmul(psB[:, 0:1], below[:], incl[:, NT - 1:NT], start=True, stop=True).then_inc(s_pe0, 1)
            pe.wait_ge(s_prep, N_DIAG1)
            m.matmul(psD[:, 0:P], ones[:], diag[:], start=True, stop=True).then_inc(s_pe0, 1)
            pe.wait_ge(s_prep, N_DIAG2)
            m.matmul(psD[:, KB:KB + P], ones[:], diag[:], start=True, stop=True).then_inc(s_pe0, 1)
            pe.wait_ge(s_wload, 16 * N_WLOAD)
            m.transpose(psC[:, 0:P], wa_raw, ident[:]).then_inc(s_pe0, 1)
            m.transpose(psC[:, P:P + D], w12_raw, ident[0:D, 0:D]).then_inc(s_pe0, 1)
            m.matmul(psC[:, 2 * P:2 * P + D], ones[0:1, :], brow[:, 0, :], start=True, stop=True).then_inc(s_pe0, 1)
            pe.wait_ge(s_prep, N_PREP)

            def bias_rows(ps_, j, stop=False):
                for q in range(2):
                    n = min(KB, CW - q * KB)
                    m.matmul(ps_[:, q * KB:q * KB + n], ones[0:1, :],
                             brow[:, j, :].unsqueeze(1).to_broadcast([1, n // D, D]), start=True, stop=False)

            def transpose_h(c, b, n):
                pe.wait_ge(s_h, c + 1)
                for j in range(PAIRS):
                    i_ = m.transpose((psC, psA)[b][:, j * P:(j + 1) * P], hbuf[:, b, j * P:(j + 1) * P], ident[:])
                i_.then_inc(s_btr, 1)

            def linear_h(c, b, n):
                pe.wait_ge(s_bcp, c + 1)
                if not (isinstance(c, int) and c < 2):
                    pe.wait_ge(s_linu, c)
                for j in range(PAIRS):
                    i_ = m.matmul((psD, psB)[b][:, j * P:(j + 1) * P], (hT, xT)[b][:, j * P:(j + 1) * P],
                                  wmix[:, 0, :], start=True, stop=True)
                i_.then_inc(s_lin, 1)

            def node_step(c, b, n):
                transpose_h(c + 1, 1 - b, n + b)
                linear_h(c, b, n)

            one(0, transpose_h)
            one(0, node_step)
            steps(pe, 1, NC - 1, node_step)
            one(NC - 1, linear_h)

            for k in range(1, ORDER + 1):
                g0 = (k - 1) * NC

                def y_part(c, b, n):
                    if k < 3:
                        pe.wait_ge(s_relay, g0 + c + 1)
                    else:
                        pe.wait_ge(s_sub, (k - 3) * NC + c + 1)
                    for j in range(PAIRS):
                        i_ = m.transpose(psA[:, j * P:(j + 1) * P], sout[:, b, j * P:(j + 1) * P], ident[:])
                    i_.then_inc(s_str, 1)
                    pe.wait_ge(s_yadd, g0 + c + 1)
                    pe.wait_ge(s_scp, g0 + c + 1)
                    part = (psB, psD)[b]
                    for j in range(PAIRS):
                        i_ = m.matmul(part[:, j * P:(j + 1) * P], xT[:, j * P:(j + 1) * P], wmix[:, k, :],
                                      start=True, stop=True)
                    i_.then_inc(s_ymm, 1)

                steps(pe, 0, NC, y_part)
                pe.wait_ge(s_scan, 2 * k * NC)
                m.matmul(psC[:, 0:D], carry_in[:], last_scanned(1), start=True, stop=True
                         ).then_inc(s_fixm, 1)
                pe.wait_ge(s_fixv, 3 * k - 1)
                m.transpose(psC[:, P:2 * P], fixp[:, k, :], ident[:]).then_inc(s_fixm, 1)
                pe.wait_ge(s_fixa, k)
                m.matmul(psC[:, 2 * P:3 * P], fixT[:], wmix[:, k, :], start=True, stop=True
                         ).then_inc(s_fixm, 1)
            if stop == "y":
                return
            pe.wait_ge(s_fixv, 3 * ORDER)
            m.matmul(psC[:, 0:D], v_from[:], yfix[:, 0:D], start=True, stop=True).then_inc(s_vin, 1)

            def front_transpose(seq, b):
                pe.wait_ge(s_x1, seq + 1)
                for j in range(PAIRS):
                    i_ = m.transpose(psA[:, j * P:(j + 1) * P], xbuf[:, b, j * P:(j + 1) * P], ident[:])
                i_.then_inc(s_ftr, 1)

            def front_center(seq, b):
                pe.wait_ge(s_fcp, seq + 1)
                pe.wait_ge(s_h, NC + seq)
                for j in range(PAIRS):
                    i_ = m.matmul(psB[:, j * P:(j + 1) * P], xT[:, j * P:(j + 1) * P], center[:],
                                  start=True, stop=True)
                i_.then_inc(s_cen, 1)

            def attention_map(seq, b):
                pe.wait_ge(s_h, NC + seq + 1)
                for j in range(PAIRS):
                    i_ = m.transpose(psC[:, j * P:(j + 1) * P], hbuf[:, b, j * P:(j + 1) * P], ident[:])
                i_.then_inc(s_btr, 1)
                pe.wait_ge(s_linu, NC + seq + 1)
                bias_rows(psD, 1)
                pe.wait_ge(s_bcp, NC + seq + 1)
                for j in range(PAIRS):
                    i_ = m.matmul(psD[:, j * P:(j + 1) * P], hT[:, j * P:(j + 1) * P], watt[:],
                                  start=False, stop=(j % 4 == 3 or j == PAIRS - 1))
                i_.then_inc(s_lin, 1)

            def target_step(c, b, n):
                front_transpose(c + 1, 1 - b)
                front_center(c + 1, 1 - b)
                attention_map(c, b)

            pe.wait_ge(s_vins, NC + 1)
            front_transpose(0, 0)
            front_center(0, 0)
            one(0, target_step)
            steps(pe, 1, NC - 1, target_step)
            attention_map(NC - 1, 1)

            def source_step(c, b, n):
                front_transpose(NC + c, b)
                front_center(NC + c, b)
                attention_map(NC + c, b)

            steps(pe, 0, NC, source_step)
            pe.wait_ge(s_fin, F_DIAG)
            m.matmul(psC[:, 0:P], ones[:], diag[:], start=True, stop=True).then_inc(s_finm, 1)
            pe.wait_ge(s_fina, 2)
            m.transpose(psC[:, P:2 * P], wts, ident[:]).then_inc(s_finm, 1)
            pe.wait_ge(s_fin, F_WTS)
            m.matmul(psC[:, 2 * P:2 * P + D + 1], wtsT, nd, start=True, stop=True).then_inc(s_finm, 1)
            pe.wait_ge(s_fin, N_FIN)

            def update_map(c, b, n):
                pe.wait_ge(s_linu, 3 * NC + c + 1)
                bias_rows(psD, 2)
                pe.wait_ge(s_sp, 2 * (c + 1))
                for q in range(2):
                    for j in range(PAIRS):
                        i_ = m.transpose((psC, psA)[q][:, j * P:(j + 1) * P], spb[:, b, q * PAIRS + j, :], ident[:])
                    i_.then_inc(s_utr, 1)
                for q in range(2):
                    pe.wait_ge(s_ucp, 2 * c + q + 1)
                    for j in range(PAIRS):
                        t = q * PAIRS + j
                        i_ = m.matmul(psD[:, t * D:(t + 1) * D], (hT, xT)[q][:, j * P:(j + 1) * P], w12[:],
                                      start=False, stop=(t % 8 == 7 or t == T - 1))
                i_.then_inc(s_lin, 1)

            steps(pe, 0, NC, update_map)

        @block.vector
        def _(dve):
            v = nc.vector
            done = [0]
            marks = {}

            def prep(i_, wait=True):
                i_.then_inc(s_prep, 1)
                done[0] += 1
                if wait:
                    dve.wait_ge(s_prep, done[0])

            def floor_nt(out_, in_):
                prep(v.tensor_scalar(out_, in_, inv, -0.5 + 0.5 * inv, ALU.mult, ALU.add))
                prep(v.tensor_scalar(out_, out_, ROUND, -ROUND, ALU.add, ALU.add))

            dve.wait_ge(s_const, N_CONST)
            prep(v.tensor_copy(iota_h, iota_i))
            assert done[0] == N_IOTA
            dve.wait_ge(s_load, 16 * N_LOAD)
            prep(v.tensor_copy(dstf[:], dst_i[:]))
            floor_nt(hi[:], dstf[:])
            prep(v.scalar_tensor_tensor(out=lo[:], in0=hi[:], scalar=-float(NT), in1=dstf[:],
                                        op0=ALU.mult, op1=ALU.add))
            dve.sem_inc(s_hot_free, HR)
            with dve.Fori(0, NT // HR) as i:
                for j in range(HR):
                    dve.wait_ge(s_hot_free, HR * i + j + 1)
                    v.tensor_scalar(onehot[:, j, 0:P], iota_h[:, 0:P], hi[:, bass.ds(HR * i + j, 1)], None,
                                    ALU.is_equal).then_inc(s_hot, 1)
                    v.tensor_scalar(onehot[:, j, P:], iota_h, lo[:, bass.ds(HR * i + j, 1)], None,
                                    ALU.is_equal).then_inc(s_hot, 1)
            dve.wait_ge(s_count, 1)
            prep(v.tensor_copy(hi[:], psA[:, 0:NT]))
            prep(v.memset(tmp[:], 1.0))
            prep(v.tensor_tensor_scan(incl[:], tmp[:], hi[:], 0.0, ALU.mult, ALU.add))
            assert done[0] == N_CUM
            dve.wait_ge(s_pe0, 1)
            prep(v.tensor_copy(small[:, 0:1], psB[:, 0:1]))
            prep(v.tensor_scalar(incl[:], incl[:], small[:, 0:1], None, ALU.add))
            prep(v.tensor_tensor(lo[:], incl[:], hi[:], ALU.subtract))
            prep(v.tensor_scalar(incl[:], incl[:], -1.0, None, ALU.add))
            floor_nt(tmp[:], incl[:])
            floor_nt(lo[:], lo[:])
            prep(v.tensor_tensor(lo[:], tmp[:], lo[:], ALU.is_gt))
            prep(v.scalar_tensor_tensor(out=tmp[:], in0=tmp[:], scalar=float(FIX), in1=incl[:],
                                        op0=ALU.add, op1=ALU.subtract))
            prep(v.tensor_tensor(tmp[:], tmp[:], lo[:], ALU.mult))
            prep(v.tensor_tensor(tmp[:], tmp[:], incl[:], ALU.add))
            prep(v.tensor_copy(pidx[:], pidx_i[:]))
            prep(v.tensor_scalar(hi[:], hi[:], 0.0, None, ALU.is_equal))
            prep(v.tensor_scalar(lo[:], hi[:], -1.0, 1.0, ALU.mult, ALU.add))
            prep(v.tensor_tensor(tmp[:], tmp[:], lo[:], ALU.mult))
            prep(v.tensor_scalar(small[:, 1:2], pidx[:], float(EMPTY), None, ALU.add))
            prep(v.scalar_tensor_tensor(out=lo[:], in0=hi[:], scalar=small[:, 1:2], in1=tmp[:],
                                        op0=ALU.mult, op1=ALU.add))
            prep(v.tensor_copy(tmp[:], rep_i[:]))
            prep(v.tensor_tensor(notlast[:], dstf[:], tmp[:], ALU.is_equal))
            prep(v.tensor_copy(rep_i[:], lo[:]))
            assert done[0] == N_REP
            prep(v.tensor_scalar(last[:], notlast[:], -1.0, 1.0, ALU.mult, ALU.add))
            prep(v.memset(tmp[:, 0:1], 0.0))
            prep(v.tensor_copy(tmp[:, 1:NT], notlast[:, 0:NT - 1]))
            prep(v.memset(same[:], 0.0))
            prep(v.tensor_copy(same[:, :, 1:T1], tmp[:].rearrange("p (c t) -> p c t", t=T)))
            prep(v.tensor_scalar(first[:], dstf[:], dstf[:, 0:1], None, ALU.is_equal))
            prep(v.tensor_tensor(last_first[:, 0:NT - 1], first[:, 0:NT - 1], last[:, 0:NT - 1], ALU.mult))
            prep(v.tensor_copy(last_first[:, NT - 1:NT], first[:, NT - 1:NT]))
            prep(v.tensor_tensor(tmp[:], iota_h, last_first[:], ALU.mult))
            prep(v.tensor_reduce(small[:, 3:4], tmp[:], AX.X, ALU.add))
            prep(v.scalar_tensor_tensor(out=small[:, 4:5], in0=pidx[:], scalar=float(NT), in1=small[:, 3:4],
                                        op0=ALU.mult, op1=ALU.add))
            prep(v.tensor_copy(first_row[:], small[:, 4:5]))
            prep(v.tensor_tensor(small[:, 2:3], first[:, NT - 1:NT], notlast[:, NT - 1:NT], ALU.mult))
            prep(v.tensor_scalar(ends_in[:], small[:, 2:3], -1.0, 1.0, ALU.mult, ALU.add))
            prep(v.tensor_scalar(diag[:], ident[:], dstf[:, 0:1], None, ALU.mult))
            assert done[0] == N_DIAG1
            dve.wait_ge(s_pe0, 2)
            prep(v.tensor_scalar(diag[:], ident[:], dstf[:, NT - 1:NT], None, ALU.mult))
            assert done[0] == N_DIAG2
            prep(v.scalar_tensor_tensor(out=carry_in[:], in0=psD[:, 0:P], scalar=dstf[:, NT - 1:NT],
                                        in1=below[:], op0=ALU.is_equal, op1=ALU.mult))
            dve.wait_ge(s_pe0, 3)
            prep(v.scalar_tensor_tensor(out=carry_to[:], in0=psD[:, KB:KB + P], scalar=dstf[:, 0:1],
                                        in1=above[:], op0=ALU.is_equal, op1=ALU.mult))
            prep(v.tensor_scalar(v_from[:], carry_to[:], ends_in[:], None, ALU.mult))
            prep(v.tensor_scalar(w2[:], w1[:], 2.0, None, ALU.mult))
            dve.wait_ge(s_wload, 16 * N_WLOAD)
            prep(v.tensor_tensor(wmix[:, 0, :], wraw[:, 0, :], wraw[:, 2, :], ALU.subtract))
            prep(v.tensor_tensor(wmix[:, 0, :], wmix[:, 0, :], wraw[:, 4, :], ALU.add))
            prep(v.tensor_tensor(wmix[:, 1, :], wraw[:, 1, :], wraw[:, 3, :], ALU.subtract))
            prep(v.tensor_tensor(wmix[:, 1, :], wmix[:, 1, :], wraw[:, 5, :], ALU.add))
            for k in (2, 3):
                prep(v.tensor_tensor(wmix[:, k, :], wraw[:, k, :], wraw[:, k + 2, :], ALU.subtract))
                prep(v.tensor_scalar(wmix[:, k, :], wmix[:, k, :], 2.0, None, ALU.mult))
            for k in (4, 5):
                prep(v.tensor_scalar(wmix[:, k, :], wraw[:, k, :], 2.0, None, ALU.mult))
            dve.wait_ge(s_pe0, 6)
            prep(v.tensor_copy(watt[:], psC[:, 0:P]))
            prep(v.tensor_copy(w12[:], psC[:, P:P + D]))
            prep(v.memset(empty[:], 0.0))
            prep(v.tensor_copy(empty[:, 0:D], psC[:, 2 * P:2 * P + D]))
            prep(v.tensor_tensor(brow[:, 2, :], brow[:, 2, :], brow[:, 3, :], ALU.add))
            prep(v.tensor_copy(center[:], ident[:]))
            for h in range(2):
                q = slice(h * D, (h + 1) * D)
                prep(v.tensor_scalar(center[q, q], center[q, q], -1.0 / D, None, ALU.add))
            prep(v.memset(run[:], 0.0))
            prep(v.memset(fseg[:], 0.0))
            assert done[0] == N_PREP, done[0]

            def center_of(seq, b, out_, in_):
                v.tensor_reduce(stat[:, b, 4, :], rows3(in_), AX.X, ALU.add).then_inc(s_mean, 1)
                dve.wait_ge(s_mean, 2 * seq + 1)
                v.tensor_scalar(stat[:, b, 1, :], stat[:, b, 4, :], -1.0 / D, None, ALU.mult).then_inc(s_mean, 1)
                dve.wait_ge(s_mean, 2 * seq + 2)
                v.tensor_tensor(rows3(out_), rows3(in_), over_d(stat[:, b, 1, :]), ALU.add).then_inc(s_xc, 1)

            def scale_h(b, in_):
                v.scalar_tensor_tensor(out=rows3(hbuf[:, b, :]), in0=rows3(in_), scalar=0.0,
                                       in1=over_d(stat[:, b, 0, :]), op0=ALU.max, op1=ALU.mult
                                       ).then_inc(s_h, 1)

            def inverse_deviation(seq, b):
                dve.wait_ge(s_sq, seq + 1)
                v.tensor_reduce(stat[:, b, 2, :], rows3(sq[:, b, :]), AX.X, ALU.add).then_inc(s_var, 1)
                dve.wait_ge(s_sd, seq + 1)
                v.reciprocal(stat[:, b, 0, :], stat[:, b, 3, :]).then_inc(s_rs, 1)
                dve.wait_ge(s_rs, seq + 1)

            def centered(c, b, n):
                x_c = yall[:, bass.ds(c * CW, CW)]
                center_of(c, b, x_c, x_c)

            def normed(c, b, n):
                inverse_deviation(c, b)
                if not (isinstance(c, int) and c < 2):
                    dve.wait_ge(s_btr, c - 1)
                stored_before(dve, s_hst, c, b, n)
                scale_h(b, yall[:, bass.ds(c * CW, CW)])

            def node_step(c, b, n):
                centered(c + 1, 1 - b, n + b)
                normed(c, b, n)

            dve.wait_ge(s_xin, 16)
            one(0, centered)
            one(0, node_step)
            one(1, node_step)
            last_in = XC - 3 + (XC - 3) % 2
            steps(dve, 2, last_in, node_step)
            dve.wait_ge(s_xlate, 16)
            steps(dve, last_in, NC - 2, node_step)
            one(NC - 2, node_step)
            one(NC - 1, normed)
            dve.wait_ge(s_node, 1)

            def scan_start(seq, b):
                v.tensor_copy(run[:, b, :].rearrange("p (d t) -> p d t", t=T1)[:, :, 0], last_scanned(1 - b)
                              ).then_inc(s_scan, 1)

            def scan(seq, b, keep_):
                dve.wait_ge(s_scan, 2 * seq + 1)
                v.tensor_tensor_scan(run[:, b, :], keep_, run[:, b, :], 0.0, ALU.mult, ALU.add).then_inc(s_scan, 1)
                dve.wait_ge(s_scan, 2 * seq + 2)

            fs = [0]

            def fseg_step(i_):
                i_.then_inc(s_fseg, 1)
                fs[0] += 1
                dve.wait_ge(s_fseg, fs[0])

            dve.sem_inc(s_yadd, 2)
            for k in range(1, ORDER + 1):
                g0 = (k - 1) * NC
                weight = w1 if k < 3 else w2
                if k == ORDER:
                    for b in range(2):
                        dve.wait_ge(s_tst[b], 16 * ((ORDER - 1) * (NC // 2) + 1))

                def product(c, b, n):
                    dve.wait_ge(s_got[b], 16 * T * ((k - 1) * NC // 2 + n + 1))
                    at = 0
                    if k == 1:
                        at = RH
                        v.tensor_copy(hi[:, cols(c)], gat[:, b, :, RREP]).then_inc(s_vins, 1)
                    if k < 3 and not (k == 1 and isinstance(c, int)):
                        dve.wait_ge(s_relay, g0 + c - 1)
                    v.tensor_tensor(scanned(b), gat[:, b, :, at:at + D], over_d(weight[:, cols(c)]),
                                    ALU.mult).then_inc(s_gread, 1)
                    scan_start(g0 + c, b)
                    dve.wait_ge(s_gread, g0 + c + 1)
                    dve.wait_ge(s_keep, g0 + c + 1)
                    scan(g0 + c, b, keep[:, b, :])
                    if k >= 3:
                        dve.wait_ge(s_prev[b], 16 * ((k - 3) * NC // 2 + n + 1))
                        if k < ORDER:
                            stored_before(dve, s_tst, c, b, n, (k - 1) * (NC // 2))
                        v.tensor_tensor(rows3(sout[:, b, :]), scanned(b), rows3(xbuf[:, b, :]), ALU.subtract
                                        ).then_inc(s_sub, 1)
                    v.tensor_tensor(rows3(sq[:, b, :]), scanned(b), over_d(last_first[:, cols(c)]),
                                    ALU.mult).then_inc(s_fsum, 1)
                    dve.wait_ge(s_fsum, 3 * (g0 + c) + 1)
                    v.tensor_reduce(fpart[:], sq[:, b, :].rearrange("p (t d) -> p d t", d=D), AX.X, ALU.add).then_inc(s_fsum, 1)
                    dve.wait_ge(s_fsum, 3 * (g0 + c) + 2)
                    v.tensor_tensor(fseg[:], fseg[:], fpart[:], ALU.add).then_inc(s_fsum, 1)
                    dve.wait_ge(s_fsum, 3 * (g0 + c) + 3)

                def y_add(c, b, n):
                    dve.wait_ge(s_ymm, g0 + c + 1)
                    part = (psB, psD)[b][:, 0:CW]
                    y = yall[:, bass.ds(c * CW, CW)]
                    if k == 1:
                        v.tensor_tensor(rows3(y), rows3(part), empty[:, 0:D].unsqueeze(1).to_broadcast([P, T, D]),
                                        ALU.add).then_inc(s_yadd, 1)
                    else:
                        v.tensor_tensor(y, part, y, ALU.add).then_inc(s_yadd, 1)

                def step(c, b, n):
                    product(c + 1, 1 - b, n + b)
                    y_add(c, b, n)

                one(0, product)
                one(0, step)
                steps(dve, 1, NC - 1, step)
                if k >= 3:
                    fseg_step(v.tensor_tensor(fseg[:], fseg[:], fixp[:, k - 2, 0:D], ALU.subtract))
                dve.wait_ge(s_fixm, 3 * k - 2)
                v.tensor_tensor(fixp[:, k, 0:D], psC[:, 0:D], fseg[:], ALU.add).then_inc(s_fixv, 1)
                if k < 3:
                    v.tensor_copy(fixp[:, k, D:PAIR], psC[:, 0:D]).then_inc(s_fixv, 1)
                else:
                    v.tensor_tensor(fixp[:, k, D:PAIR], psC[:, 0:D], fixp[:, k - 2, D:PAIR], ALU.subtract
                                    ).then_inc(s_fixv, 1)
                if k == 1:
                    dve.wait_ge(s_vins, NC)
                    v.tensor_copy(reps_i[:], hi[:]).then_inc(s_repi, 1)
                one(NC - 1, y_add)
                dve.wait_ge(s_fixv, 3 * k - 1)
                fseg_step(v.memset(fseg[:], 0.0))
                dve.wait_ge(s_fixm, 3 * k)
                if k == 1:
                    v.tensor_tensor(yfix[:], psC[:, 2 * P:3 * P], empty[:], ALU.add).then_inc(s_fixv, 1)
                else:
                    v.tensor_tensor(yfix[:], psC[:, 2 * P:3 * P], yfix[:], ALU.add).then_inc(s_fixv, 1)
                dve.wait_ge(s_fixv, 3 * k)
            if stop == "y":
                return

            v.tensor_scalar(cfill[:], yfix[:, D:PAIR], ends_in[:], None, ALU.mult).then_inc(s_ysel, 1)
            dve.wait_ge(s_vin, 1)
            v.tensor_copy(vinit[:], psC[:, 0:D]).then_inc(s_vins, 1)
            dve.wait_ge(s_vins, NC + 1)
            dve.wait_ge(s_ysel, 1)
            got6 = ORDER * NC // 2

            def x1_of(seq, b, z_rows, x_rows, y_rows):
                v.tensor_tensor(rows3(xbuf[:, b, :]), y_rows, z_rows, ALU.add).then_inc(s_u, 1)
                dve.wait_ge(s_u, seq + 1)
                v.scalar_tensor_tensor(out=rows3(xbuf[:, b, :]), in0=rows3(xbuf[:, b, :]), scalar=0.0,
                                       in1=x_rows, op0=ALU.max, op1=ALU.add).then_inc(s_x1, 1)

            def h1_of(seq, b):
                inverse_deviation(NC + seq, b)
                v.scalar_tensor_tensor(out=rows3(hbuf[:, b, :]), in0=rows3(psB[:, 0:CW]), scalar=0.0,
                                       in1=over_d(stat[:, b, 0, :]), op0=ALU.max, op1=ALU.mult
                                       ).then_inc(s_h, 1)

            def fill(c, b, n):
                at = (NC - 1) - c
                filled = sout[:, b, :]
                v.tensor_tensor(rows3(filled), rows3(yall[:, bass.ds(at * CW, CW)]), over_d(last[:, cols(at)]),
                                ALU.mult).then_inc(s_ysel, 1)
                dve.wait_ge(s_ysel, c + 2)
                base = 2 * T * c

                def fill_step(s):
                    t = T - 1 - s
                    if s > 0:
                        after = filled[:, (t + 1) * D:(t + 2) * D]
                    elif isinstance(c, int) and c == 0:
                        after = vinit[:]
                    else:
                        after = sout[:, 1 - b, 0:D]
                    v.scalar_tensor_tensor(out=filled[:, t * D:(t + 1) * D], in0=after,
                                           scalar=notlast[:, bass.ds(at * T + t, 1)],
                                           in1=filled[:, t * D:(t + 1) * D], op0=ALU.mult, op1=ALU.add
                                           ).then_inc(s_fill, 1)

                def carry_step(s):
                    t = T - 1 - s
                    v.scalar_tensor_tensor(out=xbuf[:, b, t * D:(t + 1) * D], in0=cfill[:],
                                           scalar=first[:, bass.ds(at * T + t, 1)],
                                           in1=filled[:, t * D:(t + 1) * D], op0=ALU.mult, op1=ALU.add
                                           ).then_inc(s_fill, 1)

                fill_step(0)
                for s in range(1, T):
                    dve.wait_ge(s_fill, base + max(2 * (s - 1), 1))
                    fill_step(s)
                    carry_step(s - 1)
                dve.wait_ge(s_fill, base + 2 * T - 2)
                carry_step(T - 1)
                dve.wait_ge(s_fill, base + 2 * T)
                dve.wait_ge(s_got[b], 16 * T * (got6 + n + 1))
                x1_of(c, b, gat[:, b, :, RZ:RZ + D], gat[:, b, :, RX:RX + D], rows3(xbuf[:, b, :]))

            def target_step(c, b, n):
                fill(c + 1, 1 - b, n + b)
                h1_of(c, b)

            one(0, fill)
            one(0, target_step)
            steps(dve, 1, NC - 1, target_step)
            h1_of(NC - 1, 1)

            dve.wait_ge(s_x1, NC)
            v.memset(m_all, 0.0).then_inc(s_vins, 1)
            fseg_step(v.memset(den_all, 0.0))
            fseg_step(v.tensor_scalar(restart.rearrange("p (c t) -> p c t", t=T), same[:, :, 1:T1], -1.0, BIG,
                                      ALU.add, ALU.mult))
            fseg_step(v.memset(decay, 0.0))
            dve.wait_ge(s_vins, NC + 2)
            got7 = (ORDER + 1) * NC // 2
            got8 = (ORDER + 2) * NC // 2

            def source_x1(c, b, n):
                dve.wait_ge(s_nl[b], 16 * (n + 1))
                dve.wait_ge(s_got[b], 16 * T * (got7 + n + 1))
                x1_of(NC + c, b, xzb[:, b, :, D:PAIR], xzb[:, b, :, 0:D], gat[:, b, :, 0:D])

            def add_attributes(c, b, n):
                dve.wait_ge(s_lin, 2 * NC + c + 1)
                dve.wait_ge(s_ld[b], 16 * (n + 1))
                v.tensor_tensor(ub[:, b, :], psD[:, 0:CW], erb[:, b, :], ALU.add).then_inc(s_linu, 1)

            def scores(c, b, n):
                d0 = 11 * c
                s1, s2, s3 = (sc[:, b, q, :] for q in range(3))
                mx = m_all[:, bass.ds(c * T + 1, T)]
                dve.wait_ge(s_th, c + 1)
                dve.wait_ge(s_lh[b], 16 * (n + 1))
                v.tensor_tensor(ub[:, b, :], thb[:, b, :], htb[:, b, :], ALU.mult).then_inc(s_q, 1)
                dve.wait_ge(s_q, c + 1)
                v.tensor_reduce(s1, rows3(ub[:, b, :]), AX.X, ALU.add).then_inc(s_d, 1)
                dve.wait_ge(s_d, d0 + 1)
                v.tensor_scalar(s2, s1, 0.2 / 8.0, None, ALU.mult).then_inc(s_d, 1)
                dve.wait_ge(s_d, d0 + 2)
                v.scalar_tensor_tensor(out=s3, in0=s1, scalar=1.0 / 8.0, in1=s2, op0=ALU.mult, op1=ALU.max
                                       ).then_inc(s_d, 1)
                dve.wait_ge(s_d, d0 + 3)
                v.tensor_tensor_scan(mx, restart[:, cols(c)], s3, m_all[:, bass.ds(c * T, 1)],
                                     ALU.add, ALU.max).then_inc(s_d, 1)
                dve.wait_ge(s_d, d0 + 4)
                v.tensor_tensor(s1, m_all[:, cols(c)], mx, ALU.subtract).then_inc(s_d, 1)
                dve.wait_ge(s_d, d0 + 5)
                v.tensor_scalar(ab[:, b, 0, :], s1, 0.0, None, ALU.min).then_inc(s_d, 1)
                v.tensor_tensor(ab[:, b, 1, :], s3, mx, ALU.subtract).then_inc(s_d, 1)

            def sums(c, b, n):
                d0 = 11 * c + 7
                s4, s1 = decay[:, b, 1:T1], sc[:, b, 0, :]
                den = den_all[:, bass.ds(c * T + 1, T)]
                if not isinstance(c, int):
                    dve.wait_ge(s_nb, c - 1)
                scan_start(ORDER * NC + c, b)
                dve.wait_ge(s_exp, c + 1)
                v.tensor_tensor(s4, ab[:, b, 0, :], same[:, bass.ds(c, 1), 1:T1].rearrange("p a t -> p (a t)"),
                                ALU.mult).then_inc(s_d, 1)
                v.tensor_tensor(scanned(b), rows3(hbuf[:, b, :]), over_d(ab[:, b, 1, :]),
                                ALU.mult).then_inc(s_hw, 1)
                dve.wait_ge(s_d, d0 + 1)
                v.tensor_tensor_scan(den, s4, ab[:, b, 1, :], den_all[:, bass.ds(c * T, 1)],
                                     ALU.mult, ALU.add).then_inc(s_d, 1)
                dve.wait_ge(s_d, d0 + 2)
                v.tensor_scalar(s1, den, 1e-9, None, ALU.add).then_inc(s_d, 1)
                dve.wait_ge(s_d, d0 + 3)
                v.reciprocal(sc[:, b, 2, :], s1).then_inc(s_d, 1)
                dve.wait_ge(s_hw, c + 1)
                dve.wait_ge(s_keep, ORDER * NC + c + 1)
                scan(ORDER * NC + c, b, dx[:, b, :])

            def source_h(c, b, n):
                h1_of(NC + c, b)

            def source_step(c, b, n):
                source_x1(c + 1, 1 - b, n + b)
                if not (isinstance(c, int) and c == 0):
                    scores(c - 1, 1 - b, n + b - 1)
                    sums(c - 1, 1 - b, n + b - 1)
                source_h(c + 1, 1 - b, n)
                add_attributes(c, b, n)

            one(0, source_x1)
            one(0, source_h)
            for c in range(3):
                one(c, source_step)
            steps(dve, 3, NC - 1, source_step)
            one(NC - 2, scores)
            one(NC - 2, sums)
            one(NC - 1, add_attributes)
            one(NC - 1, scores)
            one(NC - 1, sums)

            fin = [0]

            def fin_step(i_):
                i_.then_inc(s_fin, 1)
                fin[0] += 1
                dve.wait_ge(s_fin, fin[0])

            m_first, d_first, m_carry, neg_m, e_first, d_all, d_own = (fz[:, q:q + 1] for q in range(7))
            dve.wait_ge(s_d, 11 * NC)
            fin_step(v.tensor_scalar(diag[:], ident[:], m_all[:, NT:NT + 1], None, ALU.mult))
            assert fin[0] == F_DIAG
            fin_step(v.tensor_tensor(tmp[:], m_all[:, 1:NT + 1], last_first[:], ALU.mult))
            fin_step(v.tensor_reduce(m_first, tmp[:], AX.X, ALU.add))
            fin_step(v.tensor_tensor(tmp[:], den_all[:, 1:NT + 1], last_first[:], ALU.mult))
            fin_step(v.tensor_reduce(d_first, tmp[:], AX.X, ALU.add))
            fin_step(v.tensor_scalar(d_own, d_first, 1e-9, None, ALU.add))
            fin_step(v.tensor_copy(nd[:, 0:D], last_scanned(1)))
            fin_step(v.tensor_copy(nd[:, D:D + 1], den_all[:, NT:NT + 1]))
            fin_step(v.tensor_scalar(masked, carry_to[:], -1.0, BIG, ALU.add, ALU.mult))
            dve.wait_ge(s_finm, 1)
            fin_step(v.tensor_tensor(wts, psC[:, 0:P], carry_to[:], ALU.mult))
            fin_step(v.tensor_tensor(masked, masked, wts, ALU.add))
            fin_step(v.tensor_reduce(m_carry, masked, AX.X, ALU.max))
            fin_step(v.tensor_tensor(m_carry, m_carry, m_first, ALU.max))
            fin_step(v.tensor_scalar(neg_m, m_carry, -1.0, None, ALU.mult))
            assert fin[0] == F_MAX
            dve.wait_ge(s_finm, 2)
            fin_step(v.tensor_copy(wtsT, psC[:, P:2 * P]))
            assert fin[0] == F_WTS
            dve.wait_ge(s_fina, 2)
            fin_step(v.tensor_tensor(d_first, d_first, e_first, ALU.mult))
            dve.wait_ge(s_finm, 3)
            fin_step(v.tensor_tensor(d_all, psC[:, 2 * P + D:2 * P + D + 1], d_first, ALU.add))
            fin_step(v.tensor_scalar(d_all, d_all, 1e-9, None, ALU.add))
            fin_step(v.reciprocal(d_all, d_all))
            dve.wait_ge(s_fgot, 16)
            fin_step(v.tensor_scalar(fseg[:], first_yn[:, D:PAIR], d_own, None, ALU.mult))
            fin_step(v.scalar_tensor_tensor(out=fseg[:], in0=fseg[:], scalar=e_first,
                                            in1=psC[:, 2 * P:2 * P + D], op0=ALU.mult, op1=ALU.add))
            fin_step(v.tensor_scalar(yfix[:, D:PAIR], fseg[:], d_all, None, ALU.mult))
            assert fin[0] == N_FIN

            def node_x1(c, b, n):
                dve.wait_ge(s_nl[b], 16 * (NC // 2 + n + 1))
                dve.wait_ge(s_got[b], 16 * T * (got8 + n + 1))
                if not isinstance(c, int):
                    dve.wait_ge(s_o, c - 1)
                x1_of(2 * NC + c, b, xzb[:, b, :, D:PAIR], xzb[:, b, :, 0:D], gat[:, b, :, 0:D])
                dve.wait_ge(s_x1, 2 * NC + c + 1)
                if not isinstance(c, int):
                    dve.wait_ge(s_sp, 2 * (c - 1))
                center_of(NC + c, b, hbuf[:, b, :], xbuf[:, b, :])

            def node_h(c, b, n):
                inverse_deviation(3 * NC + c, b)
                scale_h(b, hbuf[:, b, :])
                dve.wait_ge(s_h, 3 * NC + c + 1)

            def node_sums(c, b, n):
                v.tensor_tensor(spb[:, b, :, 0:D], rows3(hbuf[:, b, :]), gat[:, b, :, D:PAIR],
                                ALU.add).then_inc(s_sp, 1)
                v.tensor_tensor(spb[:, b, :, D:PAIR], rows3(hbuf[:, b, :]), gat[:, b, :, D:PAIR],
                                ALU.mult).then_inc(s_sp, 1)

            def result(c, b, n):
                dve.wait_ge(s_slope, c + 1)
                v.tensor_tensor(ob[:, b, :], psD[:, 0:CW], ob[:, b, :], ALU.max).then_inc(s_linu, 1)
                dve.wait_ge(s_linu, 3 * NC + c + 2)
                stored_before(dve, s_out, c, b, n)
                v.tensor_tensor(sout[:, b, :], ob[:, b, :], xbuf[:, b, :], ALU.add).then_inc(s_o, 1)

            def update_step(c, b, n):
                node_x1(c, b, n)
                node_h(c, b, n)
                result(c - 1, 1 - b, n + b - 1)
                node_sums(c, b, n)

            for b in range(2):
                dve.wait_ge(s_nbst[b], 16 * (NC // 2 + 1))
            one(0, node_x1)
            one(0, node_h)
            one(0, node_sums)
            one(1, update_step)
            steps(dve, 2, NC, update_step)
            one(NC - 1, result)


_INS = ['x', 'src', 'dst', 'dst_next', 'edge_weight', 'edge_attr_64', 'L0_gnn_W', 'L0_gnn_bias', 'L1_gnn_W1_w',
        'L1_gnn_W1_b', 'L1_gnn_W2_w', 'L1_gnn_W2_b', 'L1_gnn_Watt_w', 'L1_gnn_Watt_b']


def kernel(**inputs):
    import numpy as _np
    import concourse.bacc as _bacc
    from concourse import mybir as _mybir
    from concourse.bass_utils import run_bass_kernel_spmd as _run

    def padded(a, value):
        a = _np.asarray(a)
        o = _np.full((ROWS,) + a.shape[1:], value, a.dtype)
        o[:len(a)] = a
        return o

    given = dict(inputs)
    for name in ('x', 'edge_attr_64', 'edge_weight'):
        given[name] = padded(inputs[name], 0)
    for name in ('src', 'dst'):
        given[name] = padded(inputs[name], N_NODES)
    after = _np.full(ROWS, N_NODES + 1, given['dst'].dtype)
    after[:-1] = given['dst'][1:]
    given['dst_next'] = after
    nc = _bacc.Bacc("TRN2", target_bir_lowering=False, num_devices=1)
    arrays, args = {}, []
    for name in _INS:
        a = _np.ascontiguousarray(given[name])
        arrays[f"in_{name}"] = a
        args.append(nc.dram_tensor(f"in_{name}", a.shape, _mybir.dt.from_np(a.dtype), kind="ExternalInput").ap())
    args.append(nc.dram_tensor("out_0", (ROWS, D), F32, kind="ExternalOutput").ap())
    build(nc, *args, stop=STOP)
    r = _run(nc, [arrays], core_ids=[0])
    return r.results[0]["out_0"][:N_NODES]
```

```python
from contextlib import ExitStack

import concourse.bass as bass
from concourse import mybir
from concourse.alu_op_type import AluOpType as ALU

ACT = mybir.ActivationFunctionType
AX = mybir.AxisListType
F32 = mybir.dt.float32
F16 = mybir.dt.float16
I32 = mybir.dt.int32

P = 128
D = 64
N_NODES = 50000
NT = 392
ROWS = P * NT
T = 14
NC = NT // T
PAIR = 2 * D
PAIRS = T // 2
CW = T * D
FIX = ROWS
EMPTY = ROWS + P
TROWS = ROWS + 2 * P
ROW = 3 * D + 1
RREP, RH, RZ, RX = 0, 1, 1 + D, 1 + 2 * D
EPS = 1e-5
ROUND = 1.5 * 2.0 ** 23
BIG = 1e30
ORDER = 5
HR = 8
KB = 512
X_PIECES = (0, 2, 6, 14, NC)
X_DVE = NC - 4
F_DIAG, F_MAX, F_WTS, N_FIN = 1, 14, 15, 22
N_IOTA, N_MEAN, N_CUM, N_REP, N_DIAG1, N_DIAG2, N_PREP = 1, 7, 10, 31, 46, 47, 69
T1 = T + 1


def steps(eng, lo, hi, step):
    with eng.Fori(0, (hi - lo) // 2) as i:
        for j in range(2):
            step(2 * i + (lo + j), (lo + j) % 2, i + (lo + j) // 2)


def one(c, step):
    step(c, c % 2, c // 2)


def build(nc, x, src, dst, dst_next, edge_w, edge_attr, W, b0, W1, b1, W2, b2, Wa, ba, out):
    with ExitStack() as ctx:
        def sb(name, shape, dt=F32):
            return ctx.enter_context(nc.sbuf_tensor(name, shape, dt))

        def ps(name, shape, dt=F32):
            return ctx.enter_context(nc.psum_tensor(name, shape, dt))

        def sem(name):
            return ctx.enter_context(nc.semaphore(name))

        def dram(name, shape, dt=F32):
            return nc.dram_tensor(name, shape, dt, kind="Internal").ap()

        node_rows = dram("node_rows", (ROWS, ROW))
        tables = [dram(f"segsum{k}", (TROWS, D)) for k in range(1, ORDER)]
        yn_table = dram("yn_table", (TROWS, 2 * D))
        y_table = dram("y_table", (TROWS, D))
        src_xz = dram("src_xz", (ROWS, 2 * D))
        htd_table = dram("htd_table", (ROWS, D))

        def by_part(t):
            return t[0:ROWS, :].rearrange("(p t) d -> p t d", t=NT)

        x_pt, er_pt, out_pt = by_part(x), by_part(edge_attr), by_part(out)
        node_pt, xz_pt, htd_pt, yn_pt = by_part(node_rows), by_part(src_xz), by_part(htd_table), by_part(yn_table)
        y_pt = by_part(y_table)
        tab_pt = [by_part(t) for t in tables]

        src_i = sb("src_i", [P, NT], I32)
        dst_i = sb("dst_i", [P, NT], I32)
        dstf = sb("dstf", [P, NT])
        w1 = sb("w1", [P, NT])
        w2 = sb("w2", [P, NT])
        same = sb("same", [P, NC, T1])
        first = sb("first", [P, NT])
        last = sb("last", [P, NT])
        notlast = sb("notlast", [P, NT])
        last_first = sb("last_first", [P, NT])
        tmp = sb("tmp", [P, NT])
        hi = sb("hi", [P, NT])
        lo = sb("lo", [P, NT])
        incl = sb("incl", [P, NT])
        rep_i = sb("rep_i", [P, NT], I32)
        reps_i = sb("reps_i", [P, NT], I32)
        ident = sb("ident", [P, P])
        ones = sb("ones", [P, P])
        below = sb("below", [P, P])
        above = sb("above", [P, P])
        center = sb("center", [P, P])
        pidx_i = sb("pidx_i", [P, 1], I32)
        pidx = sb("pidx", [P, 1])
        first_row = sb("first_row", [P, 1], I32)
        zrow = sb("zrow", [P, PAIR])
        wmix = sb("wmix", [P, 6, PAIR])
        watt = sb("watt", [P, PAIR])
        w12 = sb("w12", [P, D])
        empty = sb("empty", [P, PAIR])
        brow = sb("brow", [1, 4, D])
        eps_c = sb("eps_c", [P, 1])
        diag = sb("diag", [P, P])
        carry_in = sb("carry_in", [P, P])
        carry_to = sb("carry_to", [P, P])
        v_from = sb("v_from", [P, P])
        ends_in = sb("ends_in", [P, 1])
        small = sb("small", [P, 8])
        idx = sb("idx", [P, 2, 2 * T], I32)
        gat = sb("gat", [P, 2, T, ROW])
        xbuf = sb("xbuf", [P, 2, CW])
        keep = sb("keep", [P, 2, D * T1])
        hbuf = keep[:, :, 0:CW]
        xT = sb("xT", [P, CW])
        hT = sb("hT", [P, CW])
        sq = sb("sq", [P, 2, CW])
        run = sb("run", [P, 2, D * T1])
        sout = sb("sout", [P, 2, CW])
        stat = sb("stat", [P, 2, 5, T])
        fseg = sb("fseg", [P, D])
        fpart = sb("fpart", [P, D])
        fixp = sb("fixp", [P, ORDER + 1, PAIR])
        fixT = sb("fixT", [P, P])
        yfix = sb("yfix", [P, PAIR])
        yall = sb("yall", [P, NT * D])

        gat_room = gat[:].rearrange("p b t r -> p (b t r)")
        early = [0]

        def early_room(n):
            early[0] += n
            return gat_room[:, early[0] - n:early[0]]

        x_sum, x_neg_mean, x_dev, x_rs = (sout[:].rearrange("p b c -> p (b c)")[:, q * NT:(q + 1) * NT]
                                          for q in range(4))
        iota_i = early_room(NT).bitcast(I32)
        iota_h = early_room(NT // 2).bitcast(F16)
        zeros_h = early_room(P // 2).bitcast(F16)
        onehot = early_room(HR * (P + NT) // 2).bitcast(F16).rearrange("p (r c) -> p r c", r=HR)
        wraw = early_room(6 * PAIR).rearrange("p (k d) -> p k d", k=6)
        wa_raw = early_room(PAIR)
        w12_raw = early_room(2 * D)[0:D, :]
        vinit = sb("vinit", [P, D])
        cfill = sb("cfill", [P, D])
        spare = [0]

        def room(n):
            spare[0] += n
            return yall[:, spare[0] - n:spare[0]]

        xzb = room(2 * T * PAIR).rearrange("p (b t d) -> p b t d", b=2, t=T)
        erb = room(2 * CW).rearrange("p (b c) -> p b c", b=2)
        htb = room(2 * CW).rearrange("p (b c) -> p b c", b=2)
        ub = room(2 * CW).rearrange("p (b c) -> p b c", b=2)
        thb = room(2 * CW).rearrange("p (b c) -> p b c", b=2)
        ob = room(2 * CW).rearrange("p (b c) -> p b c", b=2)
        spb = room(2 * T * PAIR).rearrange("p (b t d) -> p b t d", b=2, t=T)
        m_all = room(NT + 1)
        den_all = room(NT + 1)
        restart = room(NT)
        ab = room(2 * 2 * T).rearrange("p (b k t) -> p b k t", b=2, k=2)
        sc = room(2 * 4 * T).rearrange("p (b k t) -> p b k t", b=2, k=4)
        decay = room(2 * T1).rearrange("p (b t) -> p b t", b=2)
        dx = room(2 * T1 * D).rearrange("p (b c) -> p b c", b=2)
        masked = room(P)
        wts = room(P)
        wtsT = room(P)
        nd = room(D + 1)
        first_yn = room(PAIR)
        fz = room(16)

        psA = ps("psA", [P, 2 * KB])
        psB = ps("psB", [P, 2 * KB])
        psC = ps("psC", [P, 2 * KB])
        psD = ps("psD", [P, 2 * KB])

        def rows3(ap):
            return ap.rearrange("p (t d) -> p t d", d=D)

        def scanned(b, lo_=1, hi_=T1):
            return run[:, b, :].rearrange("p (d t) -> p t d", t=T1)[:, lo_:hi_, :]

        def last_scanned(b):
            return run[:, b, :].rearrange("p (d t) -> p d t", t=T1)[:, :, T]

        def expand(rows, b, out_):
            return nc.scalar.copy(out_.rearrange("p (d t) -> p d t", t=T1), rows.unsqueeze(1).to_broadcast([P, D, T1]))

        def over_d(ap):
            return ap.unsqueeze(2).to_broadcast([P, T, D])

        def stored_before(eng, sem2, c, b, n, base=0):
            eng.wait_ge(sem2[b], 16 * (base + n + 1))

        def cols(c):
            return bass.ds(c * T, T)

        s_turn = sem("sp_turns")
        s_const = sem("constants_set")
        s_load = sem("inputs_loaded")
        s_wload = sem("weights_loaded")
        s_prep = sem("prep_steps")
        s_pe0 = sem("prep_products")
        s_hot = sem("onehot_made")
        s_hot_free = sem("onehot_slot_free")
        s_count = sem("counts_made")
        s_xin = [sem(f"x_piece_loaded{q}") for q in range(len(X_PIECES) - 1)]
        s_xcopy = sem("x_in_node_rows")
        s_xc = sem("x_centered")
        s_sq = sem("squares_made")
        s_mean = sem("means_made")
        s_var = sem("variances_made")
        s_rs = sem("inverse_deviations_made")
        s_sd = sem("deviations_made")
        s_h = sem("h_made")
        s_rowx = sem("row_rep_set")
        s_row = [sem(f"row_chunk_stored{b}") for b in range(2)]
        s_hcp = sem("h_in_row")
        s_stat = sem("x_statistics")
        s_schunk = sem("x_statistics_chunks")
        s_nsub = sem("x_less_mean_made")
        s_node = sem("node_rows_ready")
        s_btr = sem("h_transposed")
        s_bcp = sem("h_transpose_copied")
        s_lin = sem("linear_made")
        s_linu = sem("linear_used")
        s_started = sem("gathers_started")
        s_got = [sem(f"gathered{b}") for b in range(2)]
        s_gread = sem("gather_read")
        s_scan = sem("scan_steps")
        s_keep = sem("keep_expanded")
        s_relay = sem("sums_by_row_made")
        s_fsum = sem("first_segment_sums")
        s_sub = sem("older_product_subtracted")
        s_prev = [sem(f"older_product_loaded{b}") for b in range(2)]
        s_str = sem("product_transposed")
        s_scp = sem("product_transpose_copied")
        s_ymm = sem("y_part_made")
        s_yadd = sem("y_part_added")
        s_tst = [sem(f"table_chunk_stored{b}") for b in range(2)]
        s_xz = [sem(f"xz_chunk_stored{b}") for b in range(2)]
        s_fixm = sem("fix_products")
        s_fixv = sem("fix_steps")
        s_fixa = sem("fix_transpose_copied")
        s_fixst = sem("fix_rows_stored")
        s_pass = sem("table_ready")
        s_zero = sem("zero_rows_stored")
        s_yst = sem("y_chunk_stored")
        s_out = [sem(f"out_stored{b}") for b in range(2)]
        s_repi = sem("source_reps_ready")
        s_idx = sem("indices_staged")
        s_fseg = sem("first_sum_steps")
        s_vin = sem("fill_start_made")
        s_vins = sem("fill_start_steps")
        s_ysel = sem("segment_ends_selected")
        s_fill = sem("fill_steps")
        s_u = sem("l0_sum_made")
        s_x1 = sem("x1_made")
        s_ftr = sem("x1_transposed")
        s_fcp = sem("x1_transpose_copied")
        s_cen = sem("x1_centered")
        s_ht = [sem(f"target_rows_stored{b}") for b in range(2)]
        s_ld = [sem(f"edge_rows_loaded{b}") for b in range(2)]
        s_lh = [sem(f"target_rows_loaded{b}") for b in range(2)]
        s_th = sem("tanh_made")
        s_q = sem("score_terms_made")
        s_d = sem("score_steps")
        s_exp = sem("exponentials_made")
        s_hw = sem("weighted_h_made")
        s_nb = sem("neighbour_sum_made")
        s_nbst = [sem(f"neighbour_sum_stored{b}") for b in range(2)]
        s_fin = sem("attention_fix_steps")
        s_finm = sem("attention_fix_products")
        s_fina = sem("attention_fix_exponentials")
        s_fgot = sem("first_sums_gathered")
        s_yn = sem("update_table_ready")
        s_nl = [sem(f"node_xz_loaded{b}") for b in range(2)]
        s_sp = sem("sum_and_product_made")
        s_utr = sem("update_transposed")
        s_ucp = sem("update_transpose_copied")
        s_slope = sem("leaky_slope_made")
        s_o = sem("output_made")

        N_CONST, N_LOAD = 14, 4
        N_WLOAD = 2 * 6 + 2 + 2 + 4
        inv = 1.0 / NT
        block = ctx.enter_context(nc.Block())

        @block.sync
        def _(sp):
            sp.dma_start(src_i[:], src.rearrange("(p t) -> p t", t=NT)).then_inc(s_load, 16)
            sp.dma_start(dst_i[:], dst.rearrange("(p t) -> p t", t=NT)).then_inc(s_load, 16)
            sp.dma_start(rep_i[:], dst_next.rearrange("(p t) -> p t", t=NT)).then_inc(s_load, 16)
            sp.dma_start(w1[:], edge_w.rearrange("(p t) -> p t", t=NT)).then_inc(s_load, 16)
            for q in range(len(X_PIECES) - 1):
                t0, t1 = (X_PIECES[q + j] * T for j in range(2))
                sp.dma_start(rows3(yall[:, t0 * D:t1 * D]), x_pt[:, t0:t1, :]).then_inc(s_xin[q], 16)
            sp.wait_ge(s_const, N_CONST)
            for k in range(6):
                for h in range(2):
                    sp.dma_start(wraw[h * D:(h + 1) * D, k, h * D:(h + 1) * D], W[k]).then_inc(s_wload, 16)
            for h in range(2):
                sp.dma_start(wa_raw[h * D:(h + 1) * D, h * D:(h + 1) * D], Wa).then_inc(s_wload, 16)
            sp.dma_start(w12_raw[:, 0:D], W1).then_inc(s_wload, 16)
            sp.dma_start(w12_raw[:, D:2 * D], W2).then_inc(s_wload, 16)
            for j, b in enumerate((b0, ba, b1, b2)):
                sp.dma_start(brow[:, j, :], b.rearrange("(a d) -> a d", a=1)).then_inc(s_wload, 16)
            sp.dma_start(node_rows[:, RX:RX + D], x).then_inc(s_xcopy, 16)
            for sem2 in (s_row, s_tst, s_xz, s_ht, s_nbst, s_out):
                for b in range(2):
                    sp.sem_inc(sem2[b], 16)
            for t in tables:
                sp.dma_start(t[EMPTY:EMPTY + P, :], zrow[:, 0:D]).then_inc(s_zero, 16)
            sp.wait_ge(s_prep, N_PREP)
            sp.dma_start(y_table[EMPTY:EMPTY + P, :], empty[:, 0:D]).then_inc(s_zero, 16)
            sp.dma_start(yn_table[EMPTY:EMPTY + P, :], empty[:]).then_inc(s_zero, 16)

            def store_row(c, b, n):
                sp.wait_ge(s_rowx, c + 1)
                sp.sem_inc(s_turn)
                sp.wait_ge(s_linu, c + 2)
                sp.dma_start(node_pt[:, cols(c), 0:RX], gat[:, b, :, 0:RX]).then_inc(s_row[b], 16)

            steps(sp, 0, NC, store_row)
            sp.wait_ge(s_xcopy, 16)
            for b in range(2):
                sp.wait_ge(s_row[b], 16 * (NC // 2 + 1))
            sp.sem_inc(s_node)

            for k in range(1, ORDER + 1):
                g0 = (k - 1) * NC

                def load(c, b, n):
                    if k >= 3:
                        if not isinstance(c, int):
                            sp.wait_ge(s_sub, (k - 3) * NC + c - 1)
                            sp.sem_inc(s_turn)
                        elif k > 3:
                            sp.wait_ge(s_sub, (k - 3) * NC - 1 + c)
                            sp.sem_inc(s_turn)
                        sp.dma_start(rows3(xbuf[:, b, :]), tab_pt[k - 3][:, cols(c), :]).then_inc(s_prev[b], 16)

                def store(c, b, n):
                    if k < 3:
                        sp.wait_ge(s_relay, g0 + c + 1)
                        sp.sem_inc(s_turn)
                    elif k < ORDER:
                        sp.wait_ge(s_sub, (k - 3) * NC + c + 1)
                        sp.sem_inc(s_turn)
                    if k < ORDER:
                        sp.dma_start(tab_pt[k - 1][:, cols(c), :], rows3(sout[:, b, :])).then_inc(s_tst[b], 16)
                    if k == 1:
                        sp.dma_start(xz_pt[:, cols(c), :], gat[:, b, :, RZ:ROW]).then_inc(s_xz[b], 16)
                    if k == ORDER:
                        sp.wait_ge(s_yadd, g0 + c + 3)
                        sp.dma_start(yn_pt[:, cols(c), 0:D], rows3(yall[:, bass.ds(c * CW, CW)])).then_inc(s_yst, 16)
                        sp.dma_start(y_pt[:, cols(c), :], rows3(yall[:, bass.ds(c * CW, CW)])).then_inc(s_yst, 16)

                def step(c, b, n):
                    load(c + 2, b, n + 1)
                    store(c, b, n)

                one(0, load)
                one(1, load)
                steps(sp, 0, NC - 2, step)
                one(NC - 2, store)
                one(NC - 1, store)
                if k < ORDER:
                    sp.wait_ge(s_fixv, 3 * k - 1)
                    sp.dma_start(tables[k - 1][FIX:FIX + P, :], fixp[:, k, 0:D]).then_inc(s_fixst, 16)
                    sp.wait_ge(s_fixst, k * 16)
                    for b in range(2):
                        sp.wait_ge(s_tst[b], 16 * (k * (NC // 2) + 1))
                    sp.wait_ge(s_zero, 16 * (ORDER + 1))
                    sp.sem_inc(s_pass)
            sp.wait_ge(s_fixv, 3 * ORDER)
            sp.dma_start(yn_table[FIX:FIX + P, 0:D], yfix[:, 0:D]).then_inc(s_fixst, 16)
            sp.dma_start(y_table[FIX:FIX + P, :], yfix[:, 0:D]).then_inc(s_fixst, 16)
            sp.wait_ge(s_fixst, (ORDER + 1) * 16)
            sp.wait_ge(s_yst, NC * 32)
            sp.wait_ge(s_zero, 16 * (ORDER + 1))
            sp.sem_inc(s_pass)


            def store_target(c, b, n):
                sp.wait_ge(s_linu, NC + c + 2)
                sp.sem_inc(s_turn)
                sp.dma_start(htd_pt[:, cols((NC - 1) - c), :], rows3(run[:, b, 0:CW])).then_inc(s_ht[b], 16)

            steps(sp, 0, NC, store_target)

            def later(c):
                return not isinstance(c, int) or c >= 2

            def load_xz(c, b, n):
                if later(c):
                    sp.wait_ge(s_x1, NC + c - 1)
                    sp.sem_inc(s_turn)
                sp.dma_start(xzb[:, b], xz_pt[:, cols(c), :]).then_inc(s_nl[b], 16)

            def load_attributes(c, b, n):
                if later(c):
                    sp.wait_ge(s_linu, 2 * NC + c)
                    sp.sem_inc(s_turn)
                sp.dma_start(rows3(erb[:, b, :]), er_pt[:, cols(c), :]).then_inc(s_ld[b], 16)

            def load_targets(c, b, n):
                if later(c):
                    sp.wait_ge(s_q, c - 1)
                    sp.sem_inc(s_turn)
                sp.dma_start(rows3(htb[:, b, :]), htd_pt[:, cols(c), :]).then_inc(s_lh[b], 16)

            def store_neighbours(c, b, n):
                sp.wait_ge(s_nb, c + 1)
                sp.sem_inc(s_turn)
                sp.dma_start(yn_pt[:, cols(c), D:PAIR], rows3(sout[:, b, :])).then_inc(s_nbst[b], 16)

            def source_step(c, b, n):
                if not isinstance(c, int) or c + 3 < NC:
                    load_xz(c + 3, 1 - b, n + 1 + b)
                if later(c):
                    store_neighbours(c - 2, b, n - 1)
                if not isinstance(c, int) or c + 1 < NC:
                    load_targets(c + 1, 1 - b, n + b)
                if not isinstance(c, int) or c + 2 < NC:
                    load_attributes(c + 2, b, n + 1)

            sp.wait_ge(s_vins, NC + 2)
            for load in (load_xz, load_attributes):
                one(0, load)
                one(1, load)
            for b in range(2):
                sp.wait_ge(s_ht[b], 16 * (NC // 2 + 1))
            one(0, load_targets)
            one(2, load_xz)
            for c in range(3):
                one(c, source_step)
            steps(sp, 3, NC - 3, source_step)
            for c in range(NC - 3, NC + 2):
                one(c, source_step)
            sp.wait_ge(s_fin, N_FIN)
            sp.dma_start(yn_table[FIX:FIX + P, D:PAIR], yfix[:, D:PAIR]).then_inc(s_fixst, 16)

            def load_nodes(c, b, n):
                if not isinstance(c, int):
                    sp.wait_ge(s_x1, 2 * NC + c - 1)
                    sp.sem_inc(s_turn)
                sp.dma_start(xzb[:, b], node_pt[:, cols(c), RZ:ROW]).then_inc(s_nl[b], 16)

            def store_out(c, b, n):
                sp.wait_ge(s_o, c + 1)
                sp.sem_inc(s_turn)
                sp.dma_start(out_pt[:, cols(c), :], rows3(sout[:, b, :])).then_inc(s_out[b], 16)

            def update_io(c, b, n):
                load_nodes(c + 2, b, n + 1)
                store_out(c, b, n)

            one(0, load_nodes)
            one(1, load_nodes)
            sp.wait_ge(s_fixst, (ORDER + 2) * 16)
            sp.sem_inc(s_yn)
            steps(sp, 0, NC - 2, update_io)
            one(NC - 2, store_out)
            one(NC - 1, store_out)
            for b in range(2):
                sp.wait_ge(s_out[b], 16 * (NC // 2 + 1))

        @block.gpsimd
        def _(pool):
            g = nc.gpsimd
            g.memset(ident[:], 0.0).then_inc(s_const, 1)
            g.memset(ones[:], 1.0).then_inc(s_const, 1)
            g.memset(wraw, 0.0).then_inc(s_const, 1)
            g.memset(wa_raw, 0.0).then_inc(s_const, 1)
            g.memset(zrow[:], 0.0).then_inc(s_const, 1)
            g.memset(zeros_h, 0.0).then_inc(s_const, 1)
            g.memset(eps_c[:], EPS).then_inc(s_const, 1)
            g.iota(iota_i, [[1, NT]], base=0, channel_multiplier=0).then_inc(s_const, 1)
            g.iota(pidx_i[:], [[0, 1]], base=0, channel_multiplier=1).then_inc(s_const, 1)
            pool.wait_ge(s_const, 9)
            g.affine_select(out=ident[:], in_=ident[:], compare_op=ALU.not_equal, fill=1.0, base=0,
                            pattern=[[-1, P]], channel_multiplier=1).then_inc(s_const, 1)
            g.affine_select(out=below[:], in_=ones[:], compare_op=ALU.is_gt, fill=0.0, base=0,
                            pattern=[[1, P]], channel_multiplier=-1).then_inc(s_const, 1)
            g.affine_select(out=above[:], in_=ones[:], compare_op=ALU.is_gt, fill=0.0, base=0,
                            pattern=[[-1, P]], channel_multiplier=1).then_inc(s_const, 1)
            g.memset(run[:], 0.0).then_inc(s_const, 1)
            g.memset(fseg[:], 0.0).then_inc(s_const, 1)

            pool.wait_ge(s_prep, N_PREP)

            def row_rep(c, b, n):
                stored_before(pool, s_row, c, b, n)
                pool.sem_inc(s_started)
                g.tensor_copy(gat[:, b, :, RREP], lo[:, cols(c)]).then_inc(s_rowx, 1)

            steps(pool, 0, NC, row_rep)
            pool.wait_ge(s_node, 1)

            def gathers(g0, width, table, indices, freed, backwards=False):
                def stage(c, pair):
                    low = (NC - 2) - c if backwards else c
                    g.tensor_copy(idx[:, pair, :], indices[:, bass.ds(low * T, 2 * T)]).then_inc(s_idx, 1)

                def chunk(c, b, n, pair):
                    freed(c, b, n)
                    if b == 0:
                        pool.wait_ge(s_idx, g0 // 2 + n + 1)
                    pool.sem_inc(s_started)
                    at = (1 - b if backwards else b) * T
                    for t in range(T):
                        g.indirect_dma_start(gat[:, b, t, 0:width], None, table,
                                             bass.IndirectOffsetOnAxis(ap=idx[:, pair, at + t:at + t + 1], axis=0)
                                             ).then_inc(s_got[b], 16)

                def pairs(c, n):
                    for pair in range(2):
                        stage(c + 2 * pair, pair)
                        for b in range(2):
                            chunk(c + 2 * pair + b, b, n + pair, pair)

                pairs(0, 0)
                with pool.Fori(0, NC // 4 - 1) as i:
                    pairs(4 * i + 4, 2 * i + 2)

            def freed1(c, b, n):
                if not isinstance(c, int) or c >= 2:
                    pool.wait_ge(s_gread, c - 1)
                    stored_before(pool, s_xz, c, b, n)

            gathers(0, ROW, node_rows, src_i, freed1)
            for b in range(2):
                pool.wait_ge(s_xz[b], 16 * (NC // 2 + 1))
            for k in range(2, ORDER + 1):
                pool.wait_ge(s_pass, k - 1)
                if k == 2:
                    pool.wait_ge(s_repi, 1)

                def freed(c, b, n):
                    pool.wait_ge(s_gread, (k - 1) * NC + c - 1)

                gathers((k - 1) * NC, D, tables[k - 2], reps_i, freed)

            def freed_targets(c, b, n):
                if isinstance(c, int) and c < 2:
                    pool.wait_ge(s_gread, ORDER * NC + c - 1)
                else:
                    pool.wait_ge(s_x1, c - 1)

            gathers(ORDER * NC, ROW, node_rows, dst_i, freed_targets, backwards=True)

            def freed_sources(c, b, n):
                pool.wait_ge(s_x1, NC + c - 1)

            pool.wait_ge(s_pass, ORDER)
            gathers((ORDER + 1) * NC, D, y_table, reps_i, freed_sources)

            for b in range(2):
                pool.wait_ge(s_nbst[b], 16 * (NC // 2 + 1))
            g.indirect_dma_start(first_yn, None, yn_table[0:ROWS, :],
                                 bass.IndirectOffsetOnAxis(ap=first_row[:], axis=0)).then_inc(s_fgot, 16)

            def freed_nodes(c, b, n):
                if isinstance(c, int) and c < 2:
                    pool.wait_ge(s_x1, 2 * NC + c - 1)
                else:
                    pool.wait_ge(s_sp, 2 * (c - 1))

            pool.wait_ge(s_yn, 1)
            gathers((ORDER + 2) * NC, PAIR, yn_table, rep_i, freed_nodes)

        @block.scalar
        def _(act):
            a = nc.scalar

            def row_sums(c, b, n):
                stat_chunk_before(c)
                for t in range(T):
                    i_ = a.activation(sq[:, b, t * D:(t + 1) * D], yall[:, bass.ds(c * CW + t * D, D)], ACT.Copy,
                                      accum_out=x_sum[:, bass.ds(c * T + t, 1)])
                i_.then_inc(s_schunk, 1)

            def row_squares(c, b, n):
                stat_chunk_before(X_DVE + c)
                for t in range(T):
                    i_ = a.activation(sq[:, b, t * D:(t + 1) * D], yall[:, bass.ds(c * CW + t * D, D)], ACT.Square,
                                      bias=x_neg_mean[:, bass.ds(c * T + t, 1)],
                                      accum_out=x_dev[:, bass.ds(c * T + t, 1)])
                i_.then_inc(s_schunk, 1)

            def stat_chunk_before(seq):
                if not isinstance(seq, int):
                    act.wait_ge(s_schunk, seq - 1)

            act.wait_ge(s_const, N_CONST)
            act.sem_inc(s_linu)
            for q in range(len(X_PIECES) - 1):
                act.wait_ge(s_xin[q], 16)
                if q == 0:
                    for c in range(X_PIECES[1]):
                        one(c, row_sums)
                else:
                    steps(act, X_PIECES[q], min(X_PIECES[q + 1], X_DVE), row_sums)
            act.wait_ge(s_schunk, X_DVE)
            a.mul(x_neg_mean[:, 0:X_DVE * T], x_sum[:, 0:X_DVE * T], -1.0 / D).then_inc(s_stat, 1)
            act.wait_ge(s_stat, 1)
            steps(act, 0, X_DVE, row_squares)
            act.wait_ge(s_prep, N_MEAN)
            steps(act, X_DVE, NC, row_squares)
            act.wait_ge(s_schunk, X_DVE + NC)
            a.activation(x_dev, x_dev, ACT.Sqrt, bias=eps_c[:], scale=1.0 / D).then_inc(s_stat, 1)

            def z_out(c, b, n):
                act.wait_ge(s_lin, c + 1)
                stored_before(act, s_row, c, b, n)
                a.copy(gat[:, b, :, RZ:RZ + D], rows3((psD, psB)[b][:, 0:CW])).then_inc(s_linu, 1)

            def copy_node_h(c, b, n):
                act.wait_ge(s_btr, c + 1)
                a.copy((hT, xT)[b][:], (psC, psA)[b][:, 0:CW]).then_inc(s_bcp, 1)

            def h_out(c, b, n):
                act.wait_ge(s_h, c + 1)
                stored_before(act, s_row, c, b, n)
                a.copy(gat[:, b, :, RH:RH + D], rows3(hbuf[:, b, :])).then_inc(s_hcp, 1)

            def node_step(c, b, n):
                if not (isinstance(c, int) and c == 0):
                    h_out(c - 1, 1 - b, n + b - 1)
                copy_node_h(c, b, n)
                if not (isinstance(c, int) and c == 0):
                    z_out(c - 1, 1 - b, n + b - 1)

            one(0, node_step)
            steps(act, 1, NC - 1, node_step)
            one(NC - 1, node_step)
            one(NC - 1, h_out)
            one(NC - 1, z_out)

            for k in range(1, ORDER + 1):
                g0 = (k - 1) * NC

                def keep_of(c, b, n):
                    if not (k == 1 and isinstance(c, int)):
                        act.wait_ge(s_scan, 2 * (g0 + c - 1))
                    expand(same[:, bass.ds(c, 1), :].rearrange("p a t -> p (a t)"), b, keep[:, b, :]
                           ).then_inc(s_keep, 1)

                def copy(c, b, n):
                    if k < 3:
                        act.wait_ge(s_scan, 2 * (g0 + c + 1))
                        stored_before(act, s_tst, c, b, n, (k - 1) * (NC // 2))
                        a.copy(rows3(sout[:, b, :]), scanned(b)).then_inc(s_relay, 1)
                    act.wait_ge(s_str, g0 + c + 1)
                    a.copy(xT[:], psA[:, 0:CW]).then_inc(s_scp, 1)

                def step(c, b, n):
                    copy(c, b, n)
                    keep_of(c + 2, b, n + 1)

                if k == 1:
                    act.wait_ge(s_node, 1)
                one(0, keep_of)
                one(1, keep_of)
                steps(act, 0, NC - 2, step)
                one(NC - 2, copy)
                one(NC - 1, copy)
                act.wait_ge(s_fixm, 3 * k - 1)
                a.copy(fixT[:], psC[:, P:2 * P]).then_inc(s_fixa, 1)

            def copy_x1(seq, b):
                act.wait_ge(s_ftr, seq + 1)
                a.copy(xT[:], psA[:, 0:CW]).then_inc(s_fcp, 1)

            def squares(seq, b):
                act.wait_ge(s_cen, seq + 1)
                a.activation(sq[:, b, :], psB[:, 0:CW], ACT.Square).then_inc(s_sq, 1)

            def deviations(seq, b):
                act.wait_ge(s_var, seq + 1)
                a.activation(stat[:, b, 3, :], stat[:, b, 2, :], ACT.Sqrt, bias=eps_c[:], scale=1.0 / D
                             ).then_inc(s_sd, 1)

            def copy_h(seq, b):
                act.wait_ge(s_btr, NC + seq + 1)
                a.copy(hT[:], psC[:, 0:CW]).then_inc(s_bcp, 1)

            def target_tail(c, b, n):
                deviations(c, b)

            def target_out(c, b, n):
                copy_h(c, b)
                act.wait_ge(s_lin, NC + c + 1)
                stored_before(act, s_ht, c, b, n)
                a.copy(run[:, b, 0:CW], psD[:, 0:CW]).then_inc(s_linu, 1)

            def target_step(c, b, n):
                copy_x1(c + 1, 1 - b)
                deviations(c, b)
                squares(c + 1, 1 - b)
                target_out(c, b, n)

            copy_x1(0, 0)
            squares(0, 0)
            one(0, target_step)
            steps(act, 1, NC - 1, target_step)
            deviations(NC - 1, 1)
            one(NC - 1, target_out)

            def source_norm(c, b):
                squares(NC + c, b)
                deviations(NC + c, b)

            def tanh(c, b):
                act.wait_ge(s_linu, 2 * NC + c + 2)
                a.activation(thb[:, b, :], ub[:, b, :], ACT.Tanh).then_inc(s_th, 1)

            def exponentials(c, b):
                act.wait_ge(s_d, 11 * c + 7)
                a.activation(ab[:, b], ab[:, b], ACT.Exp).then_inc(s_exp, 1)
                act.wait_ge(s_d, 11 * c + 8)
                expand(decay[:, b, :], b, dx[:, b, :]).then_inc(s_keep, 1)

            def neighbours(c, b, n):
                act.wait_ge(s_d, 11 * c + 11)
                act.wait_ge(s_scan, 2 * (ORDER * NC + c + 1))
                stored_before(act, s_nbst, c, b, n)
                for t in range(T):
                    i_ = a.mul(sout[:, b, t * D:(t + 1) * D], scanned(b)[:, t, :], sc[:, b, 2, t:t + 1])
                i_.then_inc(s_nb, 1)

            def source_step(c, b, n):
                copy_x1(NC + c + 1, 1 - b)
                if not (isinstance(c, int) and c == 0):
                    exponentials(c - 1, 1 - b)
                source_norm(c + 1, 1 - b)
                tanh(c, b)
                copy_h(NC + c + 1, 1 - b)
                if not (isinstance(c, int) and c == 0):
                    neighbours(c - 1, 1 - b, n + b - 1)

            copy_x1(NC, 0)
            source_norm(0, 0)
            copy_h(NC, 0)
            one(0, source_step)
            steps(act, 1, NC - 1, source_step)
            exponentials(NC - 2, 0)
            tanh(NC - 1, 1)
            one(NC - 2, neighbours)
            exponentials(NC - 1, 1)
            act.wait_ge(s_fin, F_MAX)
            a.activation(wts, masked, ACT.Exp, bias=fz[:, 3:4]).then_inc(s_fina, 1)
            a.activation(fz[:, 4:5], fz[:, 0:1], ACT.Exp, bias=fz[:, 3:4]).then_inc(s_fina, 1)

            def update_norm(c, b, n):
                act.wait_ge(s_xc, c + 1)
                a.activation(sq[:, b, :], hbuf[:, b, :], ACT.Square).then_inc(s_sq, 1)
                deviations(2 * NC + c, b)

            def update_copies(c, b, n):
                for q in range(2):
                    act.wait_ge(s_utr, 2 * c + q + 1)
                    a.copy((hT, xT)[q][:], (psC, psA)[q][:, 0:CW]).then_inc(s_ucp, 1)

            def slope(c, b, n):
                act.wait_ge(s_lin, 3 * NC + c + 1)
                a.mul(ob[:, b, :], psD[:, 0:CW], 0.2).then_inc(s_slope, 1)

            def update_step(c, b, n):
                update_copies(c, b, n)
                update_norm(c + 1, 1 - b, n + b)
                slope(c, b, n)

            one(0, update_norm)
            one(0, update_step)
            steps(act, 1, NC - 1, update_step)
            one(NC - 1, update_copies)
            one(NC - 1, slope)

        @block.tensor
        def _(pe):
            m = nc.tensor
            pe.wait_ge(s_const, N_CONST)
            pe.wait_ge(s_prep, N_IOTA)
            m.matmul(psA[:, 0:NT], zeros_h, iota_h, start=True, stop=False)
            with pe.Fori(0, NT // HR) as i:
                for j in range(HR):
                    pe.wait_ge(s_hot, 2 * HR * i + 2 * (j + 1))
                    m.matmul(psA[:, 0:NT], onehot[:, j, 0:P], onehot[:, j, P:], start=False, stop=False
                             ).then_inc(s_hot_free, 1)
            m.matmul(psA[:, 0:NT], zeros_h, iota_h, start=False, stop=True).then_inc(s_count, 1)
            pe.wait_ge(s_prep, N_CUM)
            m.matmul(psB[:, 0:1], below[:], incl[:, NT - 1:NT], start=True, stop=True).then_inc(s_pe0, 1)
            pe.wait_ge(s_prep, N_DIAG1)
            m.matmul(psD[:, 0:P], ones[:], diag[:], start=True, stop=True).then_inc(s_pe0, 1)
            pe.wait_ge(s_prep, N_DIAG2)
            m.matmul(psD[:, KB:KB + P], ones[:], diag[:], start=True, stop=True).then_inc(s_pe0, 1)
            pe.wait_ge(s_wload, 16 * N_WLOAD)
            m.transpose(psC[:, 0:P], wa_raw, ident[:]).then_inc(s_pe0, 1)
            m.transpose(psC[:, P:P + D], w12_raw, ident[0:D, 0:D]).then_inc(s_pe0, 1)
            m.matmul(psC[:, 2 * P:2 * P + D], ones[0:1, :], brow[:, 0, :], start=True, stop=True).then_inc(s_pe0, 1)
            pe.wait_ge(s_prep, N_PREP)

            def bias_rows(ps_, j, stop=False):
                for q in range(2):
                    n = min(KB, CW - q * KB)
                    m.matmul(ps_[:, q * KB:q * KB + n], ones[0:1, :],
                             brow[:, j, :].unsqueeze(1).to_broadcast([1, n // D, D]), start=True, stop=False)

            def transpose_h(c, b, n):
                pe.wait_ge(s_h, c + 1)
                for j in range(PAIRS):
                    i_ = m.transpose((psC, psA)[b][:, j * P:(j + 1) * P], hbuf[:, b, j * P:(j + 1) * P], ident[:])
                i_.then_inc(s_btr, 1)

            def linear_h(c, b, n):
                pe.wait_ge(s_bcp, c + 1)
                if not (isinstance(c, int) and c < 2):
                    pe.wait_ge(s_linu, c)
                for j in range(PAIRS):
                    i_ = m.matmul((psD, psB)[b][:, j * P:(j + 1) * P], (hT, xT)[b][:, j * P:(j + 1) * P],
                                  wmix[:, 0, :], start=True, stop=True)
                i_.then_inc(s_lin, 1)

            def node_step(c, b, n):
                transpose_h(c + 1, 1 - b, n + b)
                linear_h(c, b, n)

            one(0, transpose_h)
            one(0, node_step)
            steps(pe, 1, NC - 1, node_step)
            one(NC - 1, linear_h)

            for k in range(1, ORDER + 1):
                g0 = (k - 1) * NC

                def y_part(c, b, n):
                    if k < 3:
                        pe.wait_ge(s_relay, g0 + c + 1)
                    else:
                        pe.wait_ge(s_sub, (k - 3) * NC + c + 1)
                    for j in range(PAIRS):
                        i_ = m.transpose(psA[:, j * P:(j + 1) * P], sout[:, b, j * P:(j + 1) * P], ident[:])
                    i_.then_inc(s_str, 1)
                    pe.wait_ge(s_yadd, g0 + c + 1)
                    pe.wait_ge(s_scp, g0 + c + 1)
                    part = (psB, psD)[b]
                    for j in range(PAIRS):
                        i_ = m.matmul(part[:, j * P:(j + 1) * P], xT[:, j * P:(j + 1) * P], wmix[:, k, :],
                                      start=True, stop=True)
                    i_.then_inc(s_ymm, 1)

                steps(pe, 0, NC - 2, y_part)
                one(NC - 2, y_part)
                pe.wait_ge(s_scan, 2 * k * NC)
                m.matmul(psC[:, 0:D], carry_in[:], last_scanned(1), start=True, stop=True
                         ).then_inc(s_fixm, 1)
                one(NC - 1, y_part)
                pe.wait_ge(s_fixv, 3 * k - 1)
                m.transpose(psC[:, P:2 * P], fixp[:, k, :], ident[:]).then_inc(s_fixm, 1)
                pe.wait_ge(s_fixa, k)
                m.matmul(psC[:, 2 * P:3 * P], fixT[:], wmix[:, k, :], start=True, stop=True
                         ).then_inc(s_fixm, 1)
            pe.wait_ge(s_fixv, 3 * ORDER)
            m.matmul(psC[:, 0:D], v_from[:], yfix[:, 0:D], start=True, stop=True).then_inc(s_vin, 1)

            def front_transpose(seq, b):
                pe.wait_ge(s_x1, seq + 1)
                for j in range(PAIRS):
                    i_ = m.transpose(psA[:, j * P:(j + 1) * P], xbuf[:, b, j * P:(j + 1) * P], ident[:])
                i_.then_inc(s_ftr, 1)

            def front_center(seq, b):
                pe.wait_ge(s_fcp, seq + 1)
                pe.wait_ge(s_h, NC + seq)
                for j in range(PAIRS):
                    i_ = m.matmul(psB[:, j * P:(j + 1) * P], xT[:, j * P:(j + 1) * P], center[:],
                                  start=True, stop=True)
                i_.then_inc(s_cen, 1)

            def attention_transpose(seq, b):
                pe.wait_ge(s_h, NC + seq + 1)
                for j in range(PAIRS):
                    i_ = m.transpose(psC[:, j * P:(j + 1) * P], hbuf[:, b, j * P:(j + 1) * P], ident[:])
                i_.then_inc(s_btr, 1)
                pe.wait_ge(s_linu, NC + seq + 1)
                bias_rows(psD, 1)

            def attention_product(seq, b):
                pe.wait_ge(s_bcp, NC + seq + 1)
                for j in range(PAIRS):
                    i_ = m.matmul(psD[:, j * P:(j + 1) * P], hT[:, j * P:(j + 1) * P], watt[:],
                                  start=False, stop=(j % 4 == 3 or j == PAIRS - 1))
                i_.then_inc(s_lin, 1)

            def attention_map(seq, b):
                attention_transpose(seq, b)
                attention_product(seq, b)

            def target_step(c, b, n):
                front_transpose(c + 1, 1 - b)
                front_center(c + 1, 1 - b)
                attention_map(c, b)

            pe.wait_ge(s_vins, NC + 1)
            front_transpose(0, 0)
            front_center(0, 0)
            one(0, target_step)
            steps(pe, 1, NC - 1, target_step)
            attention_map(NC - 1, 1)

            def source_step(c, b, n):
                attention_transpose(NC + c, b)
                front_transpose(NC + c + 1, 1 - b)
                front_center(NC + c + 1, 1 - b)
                attention_product(NC + c, b)

            front_transpose(NC, 0)
            front_center(NC, 0)
            one(0, source_step)
            steps(pe, 1, NC - 1, source_step)
            attention_map(2 * NC - 1, 1)
            pe.wait_ge(s_fin, F_DIAG)
            m.matmul(psC[:, 0:P], ones[:], diag[:], start=True, stop=True).then_inc(s_finm, 1)
            pe.wait_ge(s_fina, 2)
            m.transpose(psC[:, P:2 * P], wts, ident[:]).then_inc(s_finm, 1)
            pe.wait_ge(s_fin, F_WTS)
            m.matmul(psC[:, 2 * P:2 * P + D + 1], wtsT, nd, start=True, stop=True).then_inc(s_finm, 1)
            pe.wait_ge(s_fin, N_FIN)

            def update_map(c, b, n):
                pe.wait_ge(s_sp, 2 * (c + 1))
                for q in range(2):
                    for j in range(PAIRS):
                        i_ = m.transpose((psC, psA)[q][:, j * P:(j + 1) * P], spb[:, b, q * PAIRS + j, :], ident[:])
                    i_.then_inc(s_utr, 1)
                pe.wait_ge(s_linu, 3 * NC + c + 1)
                bias_rows(psD, 2)
                for q in range(2):
                    pe.wait_ge(s_ucp, 2 * c + q + 1)
                    for j in range(PAIRS):
                        t = q * PAIRS + j
                        i_ = m.matmul(psD[:, t * D:(t + 1) * D], (hT, xT)[q][:, j * P:(j + 1) * P], w12[:],
                                      start=False, stop=(t % 8 == 7 or t == T - 1))
                i_.then_inc(s_lin, 1)

            steps(pe, 0, NC, update_map)

        @block.vector
        def _(dve):
            v = nc.vector
            done = [0]
            marks = {}

            def prep(i_, wait=True):
                i_.then_inc(s_prep, 1)
                done[0] += 1
                if wait:
                    dve.wait_ge(s_prep, done[0])

            def floor_nt(out_, in_):
                prep(v.tensor_scalar(out_, in_, inv, -0.5 + 0.5 * inv, ALU.mult, ALU.add))
                prep(v.tensor_scalar(out_, out_, ROUND, -ROUND, ALU.add, ALU.add))

            dve.wait_ge(s_const, N_CONST)
            prep(v.tensor_copy(iota_h, iota_i))
            assert done[0] == N_IOTA
            dve.wait_ge(s_load, 16 * N_LOAD)
            prep(v.tensor_copy(dstf[:], dst_i[:]))
            floor_nt(hi[:], dstf[:])
            prep(v.scalar_tensor_tensor(out=lo[:], in0=hi[:], scalar=-float(NT), in1=dstf[:],
                                        op0=ALU.mult, op1=ALU.add))
            dve.sem_inc(s_hot_free, HR)
            with dve.Fori(0, NT // HR) as i:
                for j in range(HR):
                    dve.wait_ge(s_hot_free, HR * i + j + 1)
                    v.tensor_scalar(onehot[:, j, 0:P], iota_h[:, 0:P], hi[:, bass.ds(HR * i + j, 1)], None,
                                    ALU.is_equal).then_inc(s_hot, 1)
                    v.tensor_scalar(onehot[:, j, P:], iota_h, lo[:, bass.ds(HR * i + j, 1)], None,
                                    ALU.is_equal).then_inc(s_hot, 1)
            dve.wait_ge(s_xin[-1], 16)
            prep(v.tensor_reduce(x_sum[:, X_DVE * T:], rows3(yall[:, X_DVE * CW:]), AX.X, ALU.add))
            prep(v.tensor_scalar(x_neg_mean[:, X_DVE * T:], x_sum[:, X_DVE * T:], -1.0 / D, None, ALU.mult))
            assert done[0] == N_MEAN
            dve.wait_ge(s_count, 1)
            prep(v.tensor_copy(hi[:], psA[:, 0:NT]))
            prep(v.memset(tmp[:], 1.0))
            prep(v.tensor_tensor_scan(incl[:], tmp[:], hi[:], 0.0, ALU.mult, ALU.add))
            assert done[0] == N_CUM
            dve.wait_ge(s_pe0, 1)
            prep(v.tensor_copy(small[:, 0:1], psB[:, 0:1]))
            prep(v.tensor_scalar(incl[:], incl[:], small[:, 0:1], None, ALU.add))
            prep(v.tensor_tensor(lo[:], incl[:], hi[:], ALU.subtract))
            prep(v.tensor_scalar(incl[:], incl[:], -1.0, None, ALU.add))
            floor_nt(tmp[:], incl[:])
            floor_nt(lo[:], lo[:])
            prep(v.tensor_tensor(lo[:], tmp[:], lo[:], ALU.is_gt))
            prep(v.scalar_tensor_tensor(out=tmp[:], in0=tmp[:], scalar=float(FIX), in1=incl[:],
                                        op0=ALU.add, op1=ALU.subtract))
            prep(v.tensor_tensor(tmp[:], tmp[:], lo[:], ALU.mult))
            prep(v.tensor_tensor(tmp[:], tmp[:], incl[:], ALU.add))
            prep(v.tensor_copy(pidx[:], pidx_i[:]))
            prep(v.tensor_scalar(hi[:], hi[:], 0.0, None, ALU.is_equal))
            prep(v.tensor_scalar(lo[:], hi[:], -1.0, 1.0, ALU.mult, ALU.add))
            prep(v.tensor_tensor(tmp[:], tmp[:], lo[:], ALU.mult))
            prep(v.tensor_scalar(small[:, 1:2], pidx[:], float(EMPTY), None, ALU.add))
            prep(v.scalar_tensor_tensor(out=lo[:], in0=hi[:], scalar=small[:, 1:2], in1=tmp[:],
                                        op0=ALU.mult, op1=ALU.add))
            prep(v.tensor_copy(tmp[:], rep_i[:]))
            prep(v.tensor_tensor(notlast[:], dstf[:], tmp[:], ALU.is_equal))
            prep(v.tensor_copy(rep_i[:], lo[:]))
            assert done[0] == N_REP
            prep(v.tensor_scalar(last[:], notlast[:], -1.0, 1.0, ALU.mult, ALU.add))
            prep(v.memset(tmp[:, 0:1], 0.0))
            prep(v.tensor_copy(tmp[:, 1:NT], notlast[:, 0:NT - 1]))
            prep(v.memset(same[:], 0.0))
            prep(v.tensor_copy(same[:, :, 1:T1], tmp[:].rearrange("p (c t) -> p c t", t=T)))
            prep(v.tensor_scalar(first[:], dstf[:], dstf[:, 0:1], None, ALU.is_equal))
            prep(v.tensor_tensor(last_first[:, 0:NT - 1], first[:, 0:NT - 1], last[:, 0:NT - 1], ALU.mult))
            prep(v.tensor_copy(last_first[:, NT - 1:NT], first[:, NT - 1:NT]))
            prep(v.tensor_tensor(tmp[:], iota_h, last_first[:], ALU.mult))
            prep(v.tensor_reduce(small[:, 3:4], tmp[:], AX.X, ALU.add))
            prep(v.scalar_tensor_tensor(out=small[:, 4:5], in0=pidx[:], scalar=float(NT), in1=small[:, 3:4],
                                        op0=ALU.mult, op1=ALU.add))
            prep(v.tensor_copy(first_row[:], small[:, 4:5]))
            prep(v.tensor_tensor(small[:, 2:3], first[:, NT - 1:NT], notlast[:, NT - 1:NT], ALU.mult))
            prep(v.tensor_scalar(ends_in[:], small[:, 2:3], -1.0, 1.0, ALU.mult, ALU.add))
            prep(v.tensor_scalar(diag[:], ident[:], dstf[:, 0:1], None, ALU.mult))
            assert done[0] == N_DIAG1
            dve.wait_ge(s_pe0, 2)
            prep(v.tensor_scalar(diag[:], ident[:], dstf[:, NT - 1:NT], None, ALU.mult))
            assert done[0] == N_DIAG2
            prep(v.scalar_tensor_tensor(out=carry_in[:], in0=psD[:, 0:P], scalar=dstf[:, NT - 1:NT],
                                        in1=below[:], op0=ALU.is_equal, op1=ALU.mult))
            dve.wait_ge(s_pe0, 3)
            prep(v.scalar_tensor_tensor(out=carry_to[:], in0=psD[:, KB:KB + P], scalar=dstf[:, 0:1],
                                        in1=above[:], op0=ALU.is_equal, op1=ALU.mult))
            prep(v.tensor_scalar(v_from[:], carry_to[:], ends_in[:], None, ALU.mult))
            prep(v.tensor_scalar(w2[:], w1[:], 2.0, None, ALU.mult))
            dve.wait_ge(s_wload, 16 * N_WLOAD)
            prep(v.tensor_tensor(wmix[:, 0, :], wraw[:, 0, :], wraw[:, 2, :], ALU.subtract))
            prep(v.tensor_tensor(wmix[:, 0, :], wmix[:, 0, :], wraw[:, 4, :], ALU.add))
            prep(v.tensor_tensor(wmix[:, 1, :], wraw[:, 1, :], wraw[:, 3, :], ALU.subtract))
            prep(v.tensor_tensor(wmix[:, 1, :], wmix[:, 1, :], wraw[:, 5, :], ALU.add))
            for k in (2, 3):
                prep(v.tensor_tensor(wmix[:, k, :], wraw[:, k, :], wraw[:, k + 2, :], ALU.subtract))
                prep(v.tensor_scalar(wmix[:, k, :], wmix[:, k, :], 2.0, None, ALU.mult))
            for k in (4, 5):
                prep(v.tensor_scalar(wmix[:, k, :], wraw[:, k, :], 2.0, None, ALU.mult))
            dve.wait_ge(s_pe0, 6)
            prep(v.tensor_copy(watt[:], psC[:, 0:P]))
            prep(v.tensor_copy(w12[:], psC[:, P:P + D]))
            prep(v.memset(empty[:], 0.0))
            prep(v.tensor_copy(empty[:, 0:D], psC[:, 2 * P:2 * P + D]))
            prep(v.tensor_tensor(brow[:, 2, :], brow[:, 2, :], brow[:, 3, :], ALU.add))
            prep(v.tensor_copy(center[:], ident[:]))
            for h in range(2):
                q = slice(h * D, (h + 1) * D)
                prep(v.tensor_scalar(center[q, q], center[q, q], -1.0 / D, None, ALU.add))
            assert done[0] == N_PREP, done[0]

            def center_of(seq, b, out_, in_):
                v.tensor_reduce(stat[:, b, 4, :], rows3(in_), AX.X, ALU.add).then_inc(s_mean, 1)
                dve.wait_ge(s_mean, 2 * seq + 1)
                v.tensor_scalar(stat[:, b, 1, :], stat[:, b, 4, :], -1.0 / D, None, ALU.mult).then_inc(s_mean, 1)
                dve.wait_ge(s_mean, 2 * seq + 2)
                v.tensor_tensor(rows3(out_), rows3(in_), over_d(stat[:, b, 1, :]), ALU.add).then_inc(s_xc, 1)

            def scale_h(b, in_, rs):
                v.scalar_tensor_tensor(out=rows3(hbuf[:, b, :]), in0=rows3(in_), scalar=0.0,
                                       in1=over_d(rs), op0=ALU.max, op1=ALU.mult
                                       ).then_inc(s_h, 1)

            def inverse_deviation(seq, b):
                dve.wait_ge(s_sq, seq + 1)
                v.tensor_reduce(stat[:, b, 2, :], rows3(sq[:, b, :]), AX.X, ALU.add).then_inc(s_var, 1)
                dve.wait_ge(s_sd, seq + 1)
                v.reciprocal(stat[:, b, 0, :], stat[:, b, 3, :]).then_inc(s_rs, 1)
                dve.wait_ge(s_rs, seq + 1)

            def less_mean(c, b, n):
                if not (isinstance(c, int) and c < 2):
                    dve.wait_ge(s_h, c - 1)
                v.tensor_tensor(rows3(xbuf[:, b, :]), rows3(yall[:, bass.ds(c * CW, CW)]),
                                over_d(x_neg_mean[:, cols(c)]), ALU.add).then_inc(s_nsub, 1)

            def node_h0(c, b, n):
                dve.wait_ge(s_nsub, c + 1)
                if not (isinstance(c, int) and c < 2):
                    dve.wait_ge(s_btr, c - 1)
                    dve.wait_ge(s_hcp, c - 1)
                scale_h(b, xbuf[:, b, :], x_rs[:, cols(c)])

            def node_step(c, b, n):
                less_mean(c + 1, 1 - b, n + b)
                node_h0(c, b, n)

            dve.wait_ge(s_stat, 2)
            v.reciprocal(x_rs, x_dev).then_inc(s_stat, 1)
            dve.wait_ge(s_stat, 3)
            one(0, less_mean)
            one(0, node_step)
            one(1, node_step)
            steps(dve, 2, NC - 2, node_step)
            one(NC - 2, node_step)
            one(NC - 1, node_h0)
            dve.wait_ge(s_node, 1)

            def scan_start(seq, b):
                v.tensor_copy(run[:, b, :].rearrange("p (d t) -> p d t", t=T1)[:, :, 0], last_scanned(1 - b)
                              ).then_inc(s_scan, 1)

            def scan(seq, b, keep_):
                dve.wait_ge(s_scan, 2 * seq + 1)
                v.tensor_tensor_scan(run[:, b, :], keep_, run[:, b, :], 0.0, ALU.mult, ALU.add).then_inc(s_scan, 1)
                dve.wait_ge(s_scan, 2 * seq + 2)

            fs = [0]

            def fseg_step(i_):
                i_.then_inc(s_fseg, 1)
                fs[0] += 1
                dve.wait_ge(s_fseg, fs[0])

            dve.sem_inc(s_yadd, 2)
            for k in range(1, ORDER + 1):
                g0 = (k - 1) * NC
                weight = w1 if k < 3 else w2
                if k == ORDER:
                    for b in range(2):
                        dve.wait_ge(s_tst[b], 16 * ((ORDER - 1) * (NC // 2) + 1))

                def product(c, b, n):
                    dve.wait_ge(s_got[b], 16 * T * ((k - 1) * NC // 2 + n + 1))
                    at = 0
                    if k == 1:
                        at = RH
                        v.tensor_copy(hi[:, cols(c)], gat[:, b, :, RREP]).then_inc(s_vins, 1)
                    if k < 3 and not (k == 1 and isinstance(c, int)):
                        dve.wait_ge(s_relay, g0 + c - 1)
                    v.tensor_tensor(scanned(b), gat[:, b, :, at:at + D], over_d(weight[:, cols(c)]),
                                    ALU.mult).then_inc(s_gread, 1)
                    scan_start(g0 + c, b)
                    dve.wait_ge(s_gread, g0 + c + 1)
                    dve.wait_ge(s_keep, g0 + c + 1)
                    scan(g0 + c, b, keep[:, b, :])
                    if k >= 3:
                        dve.wait_ge(s_prev[b], 16 * ((k - 3) * NC // 2 + n + 1))
                        if k < ORDER:
                            stored_before(dve, s_tst, c, b, n, (k - 1) * (NC // 2))
                        v.tensor_tensor(rows3(sout[:, b, :]), scanned(b), rows3(xbuf[:, b, :]), ALU.subtract
                                        ).then_inc(s_sub, 1)
                    v.tensor_tensor(rows3(sq[:, b, :]), scanned(b), over_d(last_first[:, cols(c)]),
                                    ALU.mult).then_inc(s_fsum, 1)
                    dve.wait_ge(s_fsum, 3 * (g0 + c) + 1)
                    v.tensor_reduce(fpart[:], sq[:, b, :].rearrange("p (t d) -> p d t", d=D), AX.X, ALU.add).then_inc(s_fsum, 1)
                    dve.wait_ge(s_fsum, 3 * (g0 + c) + 2)
                    v.tensor_tensor(fseg[:], fseg[:], fpart[:], ALU.add).then_inc(s_fsum, 1)
                    dve.wait_ge(s_fsum, 3 * (g0 + c) + 3)

                def y_add(c, b, n):
                    dve.wait_ge(s_ymm, g0 + c + 1)
                    part = (psB, psD)[b][:, 0:CW]
                    y = yall[:, bass.ds(c * CW, CW)]
                    if k == 1:
                        v.tensor_tensor(rows3(y), rows3(part), empty[:, 0:D].unsqueeze(1).to_broadcast([P, T, D]),
                                        ALU.add).then_inc(s_yadd, 1)
                    else:
                        v.tensor_tensor(y, part, y, ALU.add).then_inc(s_yadd, 1)

                def step(c, b, n):
                    product(c + 1, 1 - b, n + b)
                    y_add(c, b, n)

                one(0, product)
                one(0, step)
                steps(dve, 1, NC - 3, step)
                for c in (NC - 3, NC - 2):
                    one(c + 1, product)
                    if c < NC - 2:
                        one(c, y_add)
                if k >= 3:
                    fseg_step(v.tensor_tensor(fseg[:], fseg[:], fixp[:, k - 2, 0:D], ALU.subtract))
                dve.wait_ge(s_fixm, 3 * k - 2)
                v.tensor_tensor(fixp[:, k, 0:D], psC[:, 0:D], fseg[:], ALU.add).then_inc(s_fixv, 1)
                if k < 3:
                    v.tensor_copy(fixp[:, k, D:PAIR], psC[:, 0:D]).then_inc(s_fixv, 1)
                else:
                    v.tensor_tensor(fixp[:, k, D:PAIR], psC[:, 0:D], fixp[:, k - 2, D:PAIR], ALU.subtract
                                    ).then_inc(s_fixv, 1)
                if k == 1:
                    dve.wait_ge(s_vins, NC)
                    v.tensor_copy(reps_i[:], hi[:]).then_inc(s_repi, 1)
                one(NC - 2, y_add)
                one(NC - 1, y_add)
                dve.wait_ge(s_fixv, 3 * k - 1)
                fseg_step(v.memset(fseg[:], 0.0))
                dve.wait_ge(s_fixm, 3 * k)
                if k == 1:
                    v.tensor_tensor(yfix[:], psC[:, 2 * P:3 * P], empty[:], ALU.add).then_inc(s_fixv, 1)
                else:
                    v.tensor_tensor(yfix[:], psC[:, 2 * P:3 * P], yfix[:], ALU.add).then_inc(s_fixv, 1)
                dve.wait_ge(s_fixv, 3 * k)

            v.tensor_scalar(cfill[:], yfix[:, D:PAIR], ends_in[:], None, ALU.mult).then_inc(s_ysel, 1)
            dve.wait_ge(s_vin, 1)
            v.tensor_copy(vinit[:], psC[:, 0:D]).then_inc(s_vins, 1)
            dve.wait_ge(s_vins, NC + 1)
            dve.wait_ge(s_ysel, 1)
            got6 = ORDER * NC // 2

            def x1_of(seq, b, z_rows, x_rows, y_rows):
                v.tensor_tensor(rows3(xbuf[:, b, :]), y_rows, z_rows, ALU.add).then_inc(s_u, 1)
                dve.wait_ge(s_u, seq + 1)
                v.scalar_tensor_tensor(out=rows3(xbuf[:, b, :]), in0=rows3(xbuf[:, b, :]), scalar=0.0,
                                       in1=x_rows, op0=ALU.max, op1=ALU.add).then_inc(s_x1, 1)

            def h1_of(seq, b):
                inverse_deviation(seq, b)
                v.scalar_tensor_tensor(out=rows3(hbuf[:, b, :]), in0=rows3(psB[:, 0:CW]), scalar=0.0,
                                       in1=over_d(stat[:, b, 0, :]), op0=ALU.max, op1=ALU.mult
                                       ).then_inc(s_h, 1)

            def fill(c, b, n):
                at = (NC - 1) - c
                filled = sout[:, b, :]
                v.tensor_tensor(rows3(filled), rows3(yall[:, bass.ds(at * CW, CW)]), over_d(last[:, cols(at)]),
                                ALU.mult).then_inc(s_ysel, 1)
                dve.wait_ge(s_ysel, c + 2)
                base = 2 * T * c

                def fill_step(s):
                    t = T - 1 - s
                    if s > 0:
                        after = filled[:, (t + 1) * D:(t + 2) * D]
                    elif isinstance(c, int) and c == 0:
                        after = vinit[:]
                    else:
                        after = sout[:, 1 - b, 0:D]
                    v.scalar_tensor_tensor(out=filled[:, t * D:(t + 1) * D], in0=after,
                                           scalar=notlast[:, bass.ds(at * T + t, 1)],
                                           in1=filled[:, t * D:(t + 1) * D], op0=ALU.mult, op1=ALU.add
                                           ).then_inc(s_fill, 1)

                def carry_step(s):
                    t = T - 1 - s
                    v.scalar_tensor_tensor(out=xbuf[:, b, t * D:(t + 1) * D], in0=cfill[:],
                                           scalar=first[:, bass.ds(at * T + t, 1)],
                                           in1=filled[:, t * D:(t + 1) * D], op0=ALU.mult, op1=ALU.add
                                           ).then_inc(s_fill, 1)

                fill_step(0)
                for s in range(1, T):
                    dve.wait_ge(s_fill, base + max(2 * (s - 1), 1))
                    fill_step(s)
                    carry_step(s - 1)
                dve.wait_ge(s_fill, base + 2 * T - 2)
                carry_step(T - 1)
                dve.wait_ge(s_fill, base + 2 * T)
                dve.wait_ge(s_got[b], 16 * T * (got6 + n + 1))
                x1_of(c, b, gat[:, b, :, RZ:RZ + D], gat[:, b, :, RX:RX + D], rows3(xbuf[:, b, :]))

            def target_step(c, b, n):
                fill(c + 1, 1 - b, n + b)
                h1_of(c, b)

            one(0, fill)
            one(0, target_step)
            steps(dve, 1, NC - 1, target_step)
            dve.wait_ge(s_x1, NC)
            v.memset(m_all, 0.0).then_inc(s_vins, 1)
            fseg_step(v.memset(den_all, 0.0))
            fseg_step(v.tensor_scalar(restart.rearrange("p (c t) -> p c t", t=T), same[:, :, 1:T1], -1.0, BIG,
                                      ALU.add, ALU.mult))
            fseg_step(v.memset(decay, 0.0))
            h1_of(NC - 1, 1)

            dve.wait_ge(s_vins, NC + 2)
            got7 = (ORDER + 1) * NC // 2
            got8 = (ORDER + 2) * NC // 2

            def source_x1(c, b, n):
                dve.wait_ge(s_nl[b], 16 * (n + 1))
                dve.wait_ge(s_got[b], 16 * T * (got7 + n + 1))
                x1_of(NC + c, b, xzb[:, b, :, 0:D], xzb[:, b, :, D:PAIR], gat[:, b, :, 0:D])

            def add_attributes(c, b, n):
                dve.wait_ge(s_lin, 2 * NC + c + 1)
                dve.wait_ge(s_ld[b], 16 * (n + 1))
                v.tensor_tensor(ub[:, b, :], psD[:, 0:CW], erb[:, b, :], ALU.add).then_inc(s_linu, 1)

            def scores(c, b, n):
                d0 = 11 * c
                s1, s2, s3 = (sc[:, b, q, :] for q in range(3))
                mx = m_all[:, bass.ds(c * T + 1, T)]
                dve.wait_ge(s_th, c + 1)
                dve.wait_ge(s_lh[b], 16 * (n + 1))
                v.tensor_tensor(ub[:, b, :], thb[:, b, :], htb[:, b, :], ALU.mult).then_inc(s_q, 1)
                dve.wait_ge(s_q, c + 1)
                v.tensor_reduce(s1, rows3(ub[:, b, :]), AX.X, ALU.add).then_inc(s_d, 1)
                dve.wait_ge(s_d, d0 + 1)
                v.tensor_scalar(s2, s1, 0.2 / 8.0, None, ALU.mult).then_inc(s_d, 1)
                dve.wait_ge(s_d, d0 + 2)
                v.scalar_tensor_tensor(out=s3, in0=s1, scalar=1.0 / 8.0, in1=s2, op0=ALU.mult, op1=ALU.max
                                       ).then_inc(s_d, 1)
                dve.wait_ge(s_d, d0 + 3)
                v.tensor_tensor_scan(mx, restart[:, cols(c)], s3, m_all[:, bass.ds(c * T, 1)],
                                     ALU.add, ALU.max).then_inc(s_d, 1)
                dve.wait_ge(s_d, d0 + 4)
                v.tensor_tensor(s1, m_all[:, cols(c)], mx, ALU.subtract).then_inc(s_d, 1)
                dve.wait_ge(s_d, d0 + 5)
                v.tensor_scalar(ab[:, b, 0, :], s1, 0.0, None, ALU.min).then_inc(s_d, 1)
                v.tensor_tensor(ab[:, b, 1, :], s3, mx, ALU.subtract).then_inc(s_d, 1)

            def sums(c, b, n):
                d0 = 11 * c + 7
                s4, s1 = decay[:, b, 1:T1], sc[:, b, 0, :]
                den = den_all[:, bass.ds(c * T + 1, T)]
                if not isinstance(c, int):
                    dve.wait_ge(s_nb, c - 1)
                scan_start(ORDER * NC + c, b)
                dve.wait_ge(s_exp, c + 1)
                v.tensor_tensor(s4, ab[:, b, 0, :], same[:, bass.ds(c, 1), 1:T1].rearrange("p a t -> p (a t)"),
                                ALU.mult).then_inc(s_d, 1)
                v.tensor_tensor(scanned(b), rows3(hbuf[:, b, :]), over_d(ab[:, b, 1, :]),
                                ALU.mult).then_inc(s_hw, 1)
                dve.wait_ge(s_d, d0 + 1)
                v.tensor_tensor_scan(den, s4, ab[:, b, 1, :], den_all[:, bass.ds(c * T, 1)],
                                     ALU.mult, ALU.add).then_inc(s_d, 1)
                dve.wait_ge(s_d, d0 + 2)
                v.tensor_scalar(s1, den, 1e-9, None, ALU.add).then_inc(s_d, 1)
                dve.wait_ge(s_d, d0 + 3)
                v.reciprocal(sc[:, b, 2, :], s1).then_inc(s_d, 1)
                dve.wait_ge(s_hw, c + 1)
                dve.wait_ge(s_keep, ORDER * NC + c + 1)
                scan(ORDER * NC + c, b, dx[:, b, :])

            def source_h(c, b, n):
                h1_of(NC + c, b)

            def source_step(c, b, n):
                source_x1(c + 1, 1 - b, n + b)
                if not (isinstance(c, int) and c == 0):
                    scores(c - 1, 1 - b, n + b - 1)
                    sums(c - 1, 1 - b, n + b - 1)
                source_h(c + 1, 1 - b, n)
                add_attributes(c, b, n)

            one(0, source_x1)
            one(0, source_h)
            for c in range(3):
                one(c, source_step)
            steps(dve, 3, NC - 1, source_step)
            one(NC - 2, scores)
            one(NC - 1, add_attributes)
            one(NC - 2, sums)
            one(NC - 1, scores)
            one(NC - 1, sums)
            stored_before(dve, s_nbst, NC - 1, 1, (NC - 1) // 2)
            v.tensor_tensor(rows3(sout[:, 1, :]), scanned(1), over_d(sc[:, 1, 2, :]), ALU.mult).then_inc(s_nb, 1)

            fin = [0]

            def fin_step(i_):
                i_.then_inc(s_fin, 1)
                fin[0] += 1
                dve.wait_ge(s_fin, fin[0])

            m_first, d_first, m_carry, neg_m, e_first, d_all, d_own = (fz[:, q:q + 1] for q in range(7))
            dve.wait_ge(s_d, 11 * NC)
            fin_step(v.tensor_scalar(diag[:], ident[:], m_all[:, NT:NT + 1], None, ALU.mult))
            assert fin[0] == F_DIAG
            fin_step(v.tensor_tensor(tmp[:], m_all[:, 1:NT + 1], last_first[:], ALU.mult))
            fin_step(v.tensor_reduce(m_first, tmp[:], AX.X, ALU.add))
            fin_step(v.tensor_tensor(tmp[:], den_all[:, 1:NT + 1], last_first[:], ALU.mult))
            fin_step(v.tensor_reduce(d_first, tmp[:], AX.X, ALU.add))
            fin_step(v.tensor_scalar(d_own, d_first, 1e-9, None, ALU.add))
            fin_step(v.tensor_copy(nd[:, 0:D], last_scanned(1)))
            fin_step(v.tensor_copy(nd[:, D:D + 1], den_all[:, NT:NT + 1]))
            fin_step(v.tensor_scalar(masked, carry_to[:], -1.0, BIG, ALU.add, ALU.mult))
            dve.wait_ge(s_finm, 1)
            fin_step(v.tensor_tensor(wts, psC[:, 0:P], carry_to[:], ALU.mult))
            fin_step(v.tensor_tensor(masked, masked, wts, ALU.add))
            fin_step(v.tensor_reduce(m_carry, masked, AX.X, ALU.max))
            fin_step(v.tensor_tensor(m_carry, m_carry, m_first, ALU.max))
            fin_step(v.tensor_scalar(neg_m, m_carry, -1.0, None, ALU.mult))
            assert fin[0] == F_MAX
            dve.wait_ge(s_finm, 2)
            fin_step(v.tensor_copy(wtsT, psC[:, P:2 * P]))
            assert fin[0] == F_WTS
            dve.wait_ge(s_fina, 2)
            fin_step(v.tensor_tensor(d_first, d_first, e_first, ALU.mult))
            dve.wait_ge(s_finm, 3)
            fin_step(v.tensor_tensor(d_all, psC[:, 2 * P + D:2 * P + D + 1], d_first, ALU.add))
            fin_step(v.tensor_scalar(d_all, d_all, 1e-9, None, ALU.add))
            fin_step(v.reciprocal(d_all, d_all))
            dve.wait_ge(s_fgot, 16)
            fin_step(v.tensor_scalar(fseg[:], first_yn[:, D:PAIR], d_own, None, ALU.mult))
            fin_step(v.scalar_tensor_tensor(out=fseg[:], in0=fseg[:], scalar=e_first,
                                            in1=psC[:, 2 * P:2 * P + D], op0=ALU.mult, op1=ALU.add))
            fin_step(v.tensor_scalar(yfix[:, D:PAIR], fseg[:], d_all, None, ALU.mult))
            assert fin[0] == N_FIN

            def node_x1(c, b, n):
                dve.wait_ge(s_nl[b], 16 * (NC // 2 + n + 1))
                dve.wait_ge(s_got[b], 16 * T * (got8 + n + 1))
                if not isinstance(c, int):
                    dve.wait_ge(s_o, c - 1)
                x1_of(2 * NC + c, b, xzb[:, b, :, 0:D], xzb[:, b, :, D:PAIR], gat[:, b, :, 0:D])
                dve.wait_ge(s_x1, 2 * NC + c + 1)
                if not isinstance(c, int):
                    dve.wait_ge(s_sp, 2 * (c - 1))
                center_of(c, b, hbuf[:, b, :], xbuf[:, b, :])

            def node_h(c, b, n):
                inverse_deviation(2 * NC + c, b)
                scale_h(b, hbuf[:, b, :], stat[:, b, 0, :])
                dve.wait_ge(s_h, 3 * NC + c + 1)

            def node_sums(c, b, n):
                v.tensor_tensor(spb[:, b, :, 0:D], rows3(hbuf[:, b, :]), gat[:, b, :, D:PAIR],
                                ALU.add).then_inc(s_sp, 1)
                v.tensor_tensor(spb[:, b, :, D:PAIR], rows3(hbuf[:, b, :]), gat[:, b, :, D:PAIR],
                                ALU.mult).then_inc(s_sp, 1)

            def result(c, b, n):
                dve.wait_ge(s_slope, c + 1)
                v.tensor_tensor(ob[:, b, :], psD[:, 0:CW], ob[:, b, :], ALU.max).then_inc(s_linu, 1)
                dve.wait_ge(s_linu, 3 * NC + c + 2)
                stored_before(dve, s_out, c, b, n)
                v.tensor_tensor(sout[:, b, :], ob[:, b, :], xbuf[:, b, :], ALU.add).then_inc(s_o, 1)

            def update_step(c, b, n):
                node_x1(c, b, n)
                node_h(c, b, n)
                node_sums(c, b, n)
                result(c - 1, 1 - b, n + b - 1)

            for b in range(2):
                dve.wait_ge(s_nbst[b], 16 * (NC // 2 + 1))
            one(0, node_x1)
            one(0, node_h)
            one(0, node_sums)
            one(1, update_step)
            steps(dve, 2, NC, update_step)
            one(NC - 1, result)


_INS = ['x', 'src', 'dst', 'dst_next', 'edge_weight', 'edge_attr_64', 'L0_gnn_W', 'L0_gnn_bias', 'L1_gnn_W1_w',
        'L1_gnn_W1_b', 'L1_gnn_W2_w', 'L1_gnn_W2_b', 'L1_gnn_Watt_w', 'L1_gnn_Watt_b']


def kernel(**inputs):
    import numpy as _np
    import concourse.bacc as _bacc
    from concourse import mybir as _mybir
    from concourse.bass_utils import run_bass_kernel_spmd as _run

    def padded(a, value):
        a = _np.asarray(a)
        o = _np.full((ROWS,) + a.shape[1:], value, a.dtype)
        o[:len(a)] = a
        return o

    given = dict(inputs)
    for name in ('x', 'edge_attr_64', 'edge_weight'):
        given[name] = padded(inputs[name], 0)
    for name in ('src', 'dst'):
        given[name] = padded(inputs[name], N_NODES)
    after = _np.full(ROWS, N_NODES + 1, given['dst'].dtype)
    after[:-1] = given['dst'][1:]
    given['dst_next'] = after
    nc = _bacc.Bacc("TRN2", target_bir_lowering=False, num_devices=1)
    arrays, args = {}, []
    for name in _INS:
        a = _np.ascontiguousarray(given[name])
        arrays[f"in_{name}"] = a
        args.append(nc.dram_tensor(f"in_{name}", a.shape, _mybir.dt.from_np(a.dtype), kind="ExternalInput").ap())
    args.append(nc.dram_tensor("out_0", (ROWS, D), F32, kind="ExternalOutput").ap())
    build(nc, *args)
    r = _run(nc, [arrays], core_ids=[0])
    return r.results[0]["out_0"][:N_NODES]
```
